# Optimizing a Trainium2 kernel written in Bass

```python
import numpy as np
import jax
import jax.numpy as jnp

def _softmax(x, axis=-1):
    return jax.nn.softmax(x, axis=axis)

def _gelu(x):
    return jax.nn.gelu(x, approximate=True)

def _silu(x):
    return jax.nn.silu(x)

def _sigmoid(x):
    return jax.nn.sigmoid(x)

def _layernorm(x, axis=-1, eps=1e-05):
    m = jnp.mean(x, axis=axis, keepdims=True)
    v = jnp.var(x, axis=axis, keepdims=True)
    return (x - m) / jnp.sqrt(v + eps)

def _scatter_add(tgt, idx, src, axis=0):
    return tgt.at[idx].add(src)

def _segment_sum(src, seg, n):
    return jax.ops.segment_sum(src, seg, n)
kernel_name = 'mk_xattn_ffn_d2_seqx_r8_725ac4'

def setup_inputs(seed: int=0):
    np.random.seed(seed)
    _w = jnp.asarray

    def _rec_inputs():
        import jax
        import jax.numpy as jnp
        _rk = jax.random.key(seed)
        x = 7.22e-05 + 1 * jax.random.normal(jax.random.fold_in(_rk, 1), (4, 512, 128), jnp.float32)
        _lenS = 512 - jax.random.randint(jax.random.fold_in(_rk, 7), (4,), 0, max(1, 512 // 4) + 1, jnp.int32)
        _lenS2 = 32 - jax.random.randint(jax.random.fold_in(_rk, 8), (4,), 0, max(1, 32 // 4) + 1, jnp.int32)
        _ctx_1024P = jax.random.normal(jax.random.fold_in(_rk, 11), (4, 16, 128), jnp.float32)
        _ctx_1024c = jax.random.dirichlet(jax.random.fold_in(_rk, 511), 0.3 * jnp.ones((16,), jnp.float32), (4, 32))
        _ctx_1024t = jnp.einsum('bsk,bkd->bsd', _ctx_1024c, _ctx_1024P)
        _ctx_1024t = _ctx_1024t * jax.lax.rsqrt(jnp.mean(jnp.square(_ctx_1024t)) + 1e-12) * 0.953939
        ctx_1024 = 4.13588e-05 + 0.999923 * (_ctx_1024t + 0.3 * jax.random.normal(jax.random.fold_in(_rk, 611), (4, 32, 128), jnp.float32))
        _validS = jnp.arange(512)[None, :] < _lenS[:, None]
        _validS2 = jnp.arange(32)[None, :] < _lenS2[:, None]
        _causal = jnp.tril(jnp.ones((512, 512), dtype=bool))
        mask_BxS2_bf0 = jnp.logical_not(jnp.ones((4, 32), dtype=bool))
        return (x, ctx_1024, mask_BxS2_bf0)
    x, ctx_1024, mask_BxS2_bf0 = _rec_inputs()

    def _L0_xattn_setup():
        import jax, jax.numpy as jnp
        import numpy as np
        C = 128
        B, SQ, SKV = (4, 256, 256)
        key = jax.random.key(seed)
        ks = jax.random.split(key, 10)
        s = 1.0 / np.sqrt(C)
        return {'x': jax.random.normal(ks[0], (B, SQ, C), jnp.float32), 'content_embeddings': jax.random.normal(ks[1], (B, SKV, C), jnp.float32), 'Wq': jax.random.normal(ks[2], (C, C), jnp.float32) * s, 'bq': jnp.zeros((C,), jnp.float32), 'Wk': jax.random.normal(ks[3], (C, C), jnp.float32) * s, 'bk': jnp.zeros((C,), jnp.float32), 'Wv': jax.random.normal(ks[4], (C, C), jnp.float32) * s, 'bv': jnp.zeros((C,), jnp.float32), 'Wo': jax.random.normal(ks[5], (C, C), jnp.float32) * s, 'bo': jnp.zeros((C,), jnp.float32)}
    _L0_xattn_all = _L0_xattn_setup()
    _L0_xattn_in = {k: v for k, v in _L0_xattn_all.items() if k in ('Wq', 'bq', 'Wk', 'bk', 'Wv', 'bv', 'Wo', 'bo')}
    del _L0_xattn_all

    def _L0_ffn_setup():
        import jax, jax.numpy as jnp
        import numpy as np
        B, T, E, C, H, G = (2, 256, 8, 128, 256, 16)
        key = jax.random.key(seed)
        ks = jax.random.split(key, 7)
        return {'hidden_states': jax.random.normal(ks[0], (B, T, C), jnp.float32), 'w_red': jax.random.normal(ks[1], (C, G), jnp.float32) * 0.02, 'wg': jax.random.normal(ks[2], (E, G), jnp.float32), 'W1': jax.random.normal(ks[3], (E, C, H), jnp.float32) * 0.02, 'b1': jax.random.normal(ks[4], (E, H), jnp.float32) * 0.02, 'W2': jax.random.normal(ks[5], (E, H, C), jnp.float32) * 0.02, 'b2': jax.random.normal(ks[6], (E, C), jnp.float32) * 0.02}
    _L0_ffn_all = _L0_ffn_setup()
    _L0_ffn_in = {k: v for k, v in _L0_ffn_all.items() if k in ('w_red', 'wg', 'W1', 'b1', 'W2', 'b2')}
    del _L0_ffn_all

    def _L1_xattn_setup():
        import jax, jax.numpy as jnp
        import numpy as np
        DIM = 128
        N_HEAD = 16
        BS, QLEN, KLEN = (4, 256, 256)
        key = jax.random.key(seed)
        ks = jax.random.split(key, 12)
        s = 1.0 / np.sqrt(DIM)
        inp = {'q_in': jax.random.normal(ks[0], (BS, QLEN, DIM), jnp.float32), 'k_in': jax.random.normal(ks[1], (BS, KLEN, DIM), jnp.float32), 'v_in': jax.random.normal(ks[2], (BS, KLEN, DIM), jnp.float32), 'key_padding_mask': jnp.zeros((BS, KLEN), dtype=bool), 'Wq': jax.random.normal(ks[3], (DIM, DIM), jnp.float32) * s, 'bq': jnp.zeros((DIM,), jnp.float32), 'Wk': jax.random.normal(ks[4], (DIM, DIM), jnp.float32) * s, 'bk': jnp.zeros((DIM,), jnp.float32), 'Wv': jax.random.normal(ks[5], (DIM, DIM), jnp.float32) * s, 'bv': jnp.zeros((DIM,), jnp.float32), 'Wo': jax.random.normal(ks[6], (DIM, DIM), jnp.float32) * s, 'bo': jnp.zeros((DIM,), jnp.float32)}
        return inp
    _L1_xattn_all = _L1_xattn_setup()
    _L1_xattn_in = {k: v for k, v in _L1_xattn_all.items() if k in ('Wq', 'bq', 'Wk', 'bk', 'Wv', 'bv', 'Wo', 'bo')}
    del _L1_xattn_all

    def _L1_ffn_setup():
        import jax, jax.numpy as jnp
        import numpy as np
        B, S, H = (1, 256, 128)
        E = 16
        I = 96
        TOPK = 4
        G = 4
        TOPK_G = 2
        SCALE = 2.5
        N_SHARED = 1

        def _route(x, gate_w, gate_bias):
            n = x.shape[0]
            logits = jnp.einsum('nh,eh->ne', x.astype(jnp.float32), gate_w)
            scores = jax.nn.sigmoid(logits)
            sb = scores + gate_bias
            gs = sb.reshape(n, G, E // G)
            group_scores = jnp.sum(jax.lax.top_k(gs, 2)[0], axis=-1)
            _, gidx = jax.lax.top_k(group_scores, TOPK_G)
            gmask = jnp.sum(jax.nn.one_hot(gidx, G, dtype=sb.dtype), axis=1)
            emask = jnp.repeat(gmask, E // G, axis=-1)
            masked = jnp.where(emask > 0, sb, -jnp.inf)
            _, tidx = jax.lax.top_k(masked, TOPK)
            w = jnp.take_along_axis(scores, tidx, axis=1)
            w = w / (jnp.sum(w, axis=-1, keepdims=True) + 1e-20)
            return (tidx, w * SCALE)
        key = jax.random.key(seed)
        ks = jax.random.split(key, 9)

        def rn(k, shape, scale=0.02):
            return jax.random.normal(k, shape, dtype=jnp.float32) * scale
        return dict(hidden_states=jax.random.normal(ks[0], (B, S, H), dtype=jnp.float32), gate_w=rn(ks[1], (E, H)), gate_bias=jax.random.normal(ks[2], (E,), dtype=jnp.float32) * 0.1, w1=rn(ks[3], (E, I, H)), w2=rn(ks[4], (E, H, I)), w3=rn(ks[5], (E, I, H)), ws1=rn(ks[6], (I * N_SHARED, H)), ws2=rn(ks[7], (H, I * N_SHARED)), ws3=rn(ks[8], (I * N_SHARED, H)))
    _L1_ffn_all = _L1_ffn_setup()
    _L1_ffn_in = {k: v for k, v in _L1_ffn_all.items() if k in ('gate_w', 'gate_bias', 'w1', 'w2', 'w3', 'ws1', 'ws2', 'ws3')}
    del _L1_ffn_all
    return {'x': x, 'ctx_1024': ctx_1024, 'mask_BxS2_bf0': mask_BxS2_bf0, 'L0_xattn_Wq': _L0_xattn_in['Wq'], 'L0_xattn_bq': _L0_xattn_in['bq'], 'L0_xattn_Wk': _L0_xattn_in['Wk'], 'L0_xattn_bk': _L0_xattn_in['bk'], 'L0_xattn_Wv': _L0_xattn_in['Wv'], 'L0_xattn_bv': _L0_xattn_in['bv'], 'L0_xattn_Wo': _L0_xattn_in['Wo'], 'L0_xattn_bo': _L0_xattn_in['bo'], 'L0_ffn_w_red': _L0_ffn_in['w_red'], 'L0_ffn_wg': _L0_ffn_in['wg'], 'L0_ffn_W1': _L0_ffn_in['W1'], 'L0_ffn_b1': _L0_ffn_in['b1'], 'L0_ffn_W2': _L0_ffn_in['W2'], 'L0_ffn_b2': _L0_ffn_in['b2'], 'L1_xattn_Wq': _L1_xattn_in['Wq'], 'L1_xattn_bq': _L1_xattn_in['bq'], 'L1_xattn_Wk': _L1_xattn_in['Wk'], 'L1_xattn_bk': _L1_xattn_in['bk'], 'L1_xattn_Wv': _L1_xattn_in['Wv'], 'L1_xattn_bv': _L1_xattn_in['bv'], 'L1_xattn_Wo': _L1_xattn_in['Wo'], 'L1_xattn_bo': _L1_xattn_in['bo'], 'L1_ffn_gate_w': _L1_ffn_in['gate_w'], 'L1_ffn_gate_bias': _L1_ffn_in['gate_bias'], 'L1_ffn_w1': _L1_ffn_in['w1'], 'L1_ffn_w2': _L1_ffn_in['w2'], 'L1_ffn_w3': _L1_ffn_in['w3'], 'L1_ffn_ws1': _L1_ffn_in['ws1'], 'L1_ffn_ws2': _L1_ffn_in['ws2'], 'L1_ffn_ws3': _L1_ffn_in['ws3']}

def reference(x, ctx_1024, mask_BxS2_bf0, L0_xattn_Wq, L0_xattn_bq, L0_xattn_Wk, L0_xattn_bk, L0_xattn_Wv, L0_xattn_bv, L0_xattn_Wo, L0_xattn_bo, L0_ffn_w_red, L0_ffn_wg, L0_ffn_W1, L0_ffn_b1, L0_ffn_W2, L0_ffn_b2, L1_xattn_Wq, L1_xattn_bq, L1_xattn_Wk, L1_xattn_bk, L1_xattn_Wv, L1_xattn_bv, L1_xattn_Wo, L1_xattn_bo, L1_ffn_gate_w, L1_ffn_gate_bias, L1_ffn_w1, L1_ffn_w2, L1_ffn_w3, L1_ffn_ws1, L1_ffn_ws2, L1_ffn_ws3):
    import jax
    import jax.numpy as jnp

    def _L0_xattn_ref(x, content_embeddings, Wq, bq, Wk, bk, Wv, bv, Wo, bo):
        import jax, jax.numpy as jnp
        import numpy as np
        C = 128
        B, SQ, SKV = (4, 256, 256)
        queries = x @ Wq.T + bq
        keys = content_embeddings @ Wk.T + bk
        values = content_embeddings @ Wv.T + bv
        scale = 1.0 / jnp.sqrt(jnp.asarray(C, x.dtype))
        scores = jnp.einsum('bqc,bkc->bqk', queries, keys) * scale
        attn = jax.nn.softmax(scores, axis=-1)
        attended = jnp.einsum('bqk,bkc->bqc', attn, values)
        out = x + attended
        return out @ Wo.T + bo

    def _L0_ffn_ref(hidden_states, w_red, wg, W1, b1, W2, b2):
        import jax, jax.numpy as jnp
        import numpy as np
        B, T, E, C, H, G = (2, 256, 8, 128, 256, 16)
        b, t, c = hidden_states.shape
        x = hidden_states.reshape(-1, c)
        x_red = x @ w_red
        wg_n = wg / jnp.maximum(jnp.linalg.norm(wg, axis=1, keepdims=True), 0.0001)
        logits = x_red @ wg_n.T
        gates = jax.nn.softmax(logits, axis=1)
        scores = jnp.max(gates, axis=1)
        idx = jnp.argmax(gates, axis=1)
        h = jnp.einsum('nc,ech->neh', x, W1) + b1[None]
        h = jnp.take_along_axis(h, idx[:, None, None], axis=1)[:, 0, :]
        h = jax.nn.gelu(h, approximate=False)
        o = jnp.einsum('nh,ehc->nec', h, W2) + b2[None]
        o = jnp.take_along_axis(o, idx[:, None, None], axis=1)[:, 0, :]
        o = o * scores[:, None]
        return o.reshape(b, t, c)

    def _L1_xattn_ref(q_in, k_in, v_in, key_padding_mask, Wq, bq, Wk, bk, Wv, bv, Wo, bo):
        import jax, jax.numpy as jnp
        import numpy as np
        DIM = 128
        N_HEAD = 16
        BS, QLEN, KLEN = (4, 256, 256)
        bs, q_len, _ = q_in.shape
        k_len = k_in.shape[1]
        h = N_HEAD
        d = DIM // h
        q = (q_in @ Wq + bq).reshape(bs, q_len, h, d).transpose(0, 2, 1, 3)
        k = (k_in @ Wk + bk).reshape(bs, k_len, h, d).transpose(0, 2, 1, 3)
        v = (v_in @ Wv + bv).reshape(bs, k_len, h, d).transpose(0, 2, 1, 3)
        score = jnp.einsum('bhqd,bhkd->bhqk', q, k) / jnp.sqrt(jnp.float32(d))
        mask = key_padding_mask[:, None, None, :]
        score = jnp.where(mask, jnp.float32(-1e+30), score)
        attn = jax.nn.softmax(score, axis=-1)
        out = jnp.einsum('bhqk,bhkd->bhqd', attn, v).transpose(0, 2, 1, 3).reshape(bs, q_len, DIM)
        return out @ Wo + bo

    def _L1_ffn_ref(hidden_states, gate_w, gate_bias, w1, w2, w3, ws1, ws2, ws3):
        import jax, jax.numpy as jnp
        import numpy as np
        B, S, H = (1, 256, 128)
        E = 16
        I = 96
        TOPK = 4
        G = 4
        TOPK_G = 2
        SCALE = 2.5
        N_SHARED = 1

        def _route(x, gate_w, gate_bias):
            n = x.shape[0]
            logits = jnp.einsum('nh,eh->ne', x.astype(jnp.float32), gate_w)
            scores = jax.nn.sigmoid(logits)
            sb = scores + gate_bias
            gs = sb.reshape(n, G, E // G)
            group_scores = jnp.sum(jax.lax.top_k(gs, 2)[0], axis=-1)
            _, gidx = jax.lax.top_k(group_scores, TOPK_G)
            gmask = jnp.sum(jax.nn.one_hot(gidx, G, dtype=sb.dtype), axis=1)
            emask = jnp.repeat(gmask, E // G, axis=-1)
            masked = jnp.where(emask > 0, sb, -jnp.inf)
            _, tidx = jax.lax.top_k(masked, TOPK)
            w = jnp.take_along_axis(scores, tidx, axis=1)
            w = w / (jnp.sum(w, axis=-1, keepdims=True) + 1e-20)
            return (tidx, w * SCALE)
        b, s, h = hidden_states.shape
        x = hidden_states.reshape(-1, h)
        tidx, tw = _route(x, gate_w, gate_bias)
        n = x.shape[0]
        combine = jnp.zeros((n, E), x.dtype).at[jnp.arange(n)[:, None], tidx].add(tw)
        g = jnp.einsum('nh,eih->nei', x, w1)
        u = jnp.einsum('nh,eih->nei', x, w3)
        hact = jax.nn.silu(g) * u * combine[:, :, None]
        y = jnp.einsum('nei,ehi->nh', hact, w2)
        shared = jnp.einsum('ni,hi->nh', jax.nn.silu(x @ ws1.T) * (x @ ws3.T), ws2)
        return (y + shared).reshape(b, s, h)
    x = x + _L0_xattn_ref(_layernorm(x, axis=-1), ctx_1024, L0_xattn_Wq, L0_xattn_bq, L0_xattn_Wk, L0_xattn_bk, L0_xattn_Wv, L0_xattn_bv, L0_xattn_Wo, L0_xattn_bo)
    x = x + _L0_ffn_ref(_layernorm(x, axis=-1), L0_ffn_w_red, L0_ffn_wg, L0_ffn_W1, L0_ffn_b1, L0_ffn_W2, L0_ffn_b2)
    x = x + _L1_xattn_ref(_layernorm(x, axis=-1), ctx_1024, ctx_1024, mask_BxS2_bf0, L1_xattn_Wq, L1_xattn_bq, L1_xattn_Wk, L1_xattn_bk, L1_xattn_Wv, L1_xattn_bv, L1_xattn_Wo, L1_xattn_bo)
    x = x + _L1_ffn_ref(_layernorm(x, axis=-1), L1_ffn_gate_w, L1_ffn_gate_bias, L1_ffn_w1, L1_ffn_w2, L1_ffn_w3, L1_ffn_ws1, L1_ffn_ws2, L1_ffn_ws3)
    return x

_drawn_inputs = setup_inputs


def setup_inputs(seed=0):
    import zlib

    import numpy as np

    out = dict(_drawn_inputs(seed))
    spreads = {'L0_xattn_bq': (0.0, 0.379),
     'L0_xattn_bk': (0.0, 0.8),
     'L0_xattn_bv': (0.0, 0.1),
     'L0_xattn_bo': (0.0, 0.1),
     'L1_xattn_bq': (0.0, 0.518),
     'L1_xattn_bk': (0.0, 0.8),
     'L1_xattn_bv': (0.0, 0.1),
     'L1_xattn_bo': (0.0, 0.1)}
    factors = {'L0_ffn_w_red': 8.0,
     'L0_ffn_wg': 8.0,
     'L0_ffn_W1': 8.0,
     'L0_ffn_b1': 8.0,
     'L0_ffn_W2': 8.0,
     'L0_ffn_b2': 8.0,
     'L1_ffn_gate_w': 8.0,
     'L1_ffn_gate_bias': 8.0,
     'L1_ffn_w1': 8.0,
     'L1_ffn_w2': 8.0,
     'L1_ffn_w3': 8.0,
     'L1_ffn_ws1': 8.0,
     'L1_ffn_ws2': 8.0,
     'L1_ffn_ws3': 8.0}
    for name, (base, spread) in spreads.items():
        noise = np.random.default_rng([zlib.crc32(name.encode()), seed]).standard_normal(out[name].shape)
        drawn = base * np.exp(spread * noise) if base else spread * noise
        out[name] = jnp.asarray(drawn.astype(out[name].dtype))
    for name, factor in factors.items():
        out[name] = (out[name] * factor).astype(out[name].dtype)
    return out
```

```python
from contextlib import ExitStack

import concourse.bass as bass
from concourse import mybir

F32 = mybir.dt.float32
F32R = mybir.dt.float32r
BF16 = mybir.dt.bfloat16
U8 = mybir.dt.uint8
ALU = mybir.AluOpType
ACT = mybir.ActivationFunctionType
AX = mybir.AxisListType.X

P = 128
C = 128
B = 4
TPB = 4
NT = B * TPB
CH = TPB * P
KV = 32
H1 = 16
D1 = C // H1
E0 = 8
R0 = 16
G0 = 16
E1 = 16
I1 = 96
R1 = E1 * I1 // P
NG = 4
TOPG = 2
TOPK = 4
SCALE = 2.5
EPS = 1e-5
BIG = 1e30
LAG = 2


def xattn_moe_kernel(nc, a, out):
    with ExitStack() as ctx:
        def sb(name, shape, dt=F32):
            return ctx.enter_context(nc.sbuf_tensor(name, shape, dt))

        def sem(name):
            return ctx.enter_context(nc.semaphore(name))

        bank = [ctx.enter_context(nc.psum_tensor(f"bank{i}", [P, 512], F32)) for i in range(8)]

        x = sb("x", [P, NT, C])
        ctxT = sb("ctxT", [C, B * KV])
        ident = sb("ident", [P, P])
        attn0_w = sb("attn0_w", [P, 4, C])
        attn1_w = sb("attn1_w", [P, 4, C])
        cols = sb("cols", [P, 6])
        b1col = sb("b1col", [P, R0])
        bo_rows = sb("bo_rows", [P, 2, C])
        small0 = sb("small0", [G0, C])
        wg_sb = sb("wg_sb", [E0, G0])
        gate1T = sb("gate1T", [C, E1])
        gbias = sb("gbias", [P, E1])
        mask8 = sb("mask8", [P, B * KV], U8)
        blk = sb("blk", [P, H1])
        below = sb("below", [P, NG, NG])
        order8 = sb("order8", [P, E0])
        b2_sb = sb("b2_sb", [2 * E0, C])
        wf = sb("wf", [C, 2 * (R1 * P + I1)])
        w1f = wf[:, 0:R0 * P]
        gu1f = wf[:, :].rearrange("p (w n) -> p w n", w=2)
        w2_0 = sb("w2_0", [P, R0, C])
        late = sb("late", [P, NT * C])
        attn0 = late[:, :].rearrange("p (t n) -> p t n", t=NT)
        w2_1 = late[:, 0:R1 * C].rearrange("p (r n) -> p r n", r=R1)
        ws2 = late[0:I1, R1 * C:(R1 + 1) * C]

        w1h = sb("w1h", [C, R0 * P], F32R)
        w1l = sb("w1l", [C, R0 * P], F32R)
        gu1h = sb("gu1h", [C, 2, R1 * P + I1], F32R)
        gu1l = sb("gu1l", [C, 2, R1 * P + I1], F32R)
        sel0 = sb("sel0", [2 * E0, E0, P], F32R)
        sel1 = sb("sel1", [2 * E1, R1, P], F32R)
        xTh = sb("xTh", [C, NT * P], F32R)
        xTl = sb("xTl", [C, NT * P], F32R)
        gT = sb("gT", [2 * E1, NT * P], F32R)
        gT0 = gT[0:2 * E0, :]
        gT1 = gT[:, :]

        kT0 = sb("kT0", [C, B * KV])
        vT0 = sb("vT0", [C, B * KV])
        A0 = sb("A0", [C, B * KV])
        bqrep = sb("bqrep", [P, C])
        s0bias = sb("s0bias", [P, B * KV])
        V0 = sb("V0", [B * KV, C])
        kT1 = sb("kT1", [C, B * KV])
        vT1 = sb("vT1", [C, B * KV])
        Kblk = sb("Kblk", [C, B, H1, KV])
        V1 = sb("V1", [P, B, 4, C])
        maskrow = sb("maskrow", [P, B, H1, KV], BF16)
        onesb = sb("onesb", [P, P], BF16)
        ones = sb("ones", [P, P])
        bq1s = sb("bq1s", [P, 1])
        bo16 = sb("bo16", [P, C])
        wgsq = sb("wgsq", [E0, G0])
        wgss = sb("wgss", [E0, 1])
        wginv = sb("wginv", [E0, 1])
        wgn = sb("wgn", [E0, G0])
        wgnT = sb("wgnT", [G0, E0])
        R0w = sb("R0w", [C, P])
        R1w = sb("R1w", [C, P])
        mhalf = sb("mhalf", [P, NT])

        st = sb("st", [P, NT, 6])
        mv = sb("mv", [P, NT, 2])
        ve = sb("ve", [P, NT])
        rstd = sb("rstd", [P, NT])
        xn = sb("xn", [P, NT, C])
        xT = sb("xT", [C, NT * P])
        s0 = sb("s0", [P, NT, KV])
        m0 = sb("m0", [P, NT])
        z0 = sb("z0", [P, NT])
        rz0 = sb("rz0", [P, NT])
        lg0 = sb("lg0", [P, NT, E0])
        lt0 = sb("lt0", [P, NT, E0])
        oh0 = sb("oh0", [P, NT, E0])
        ex0 = sb("ex0", [P, NT, E0])
        gate0 = sb("gate0", [P, NT, 2, E0])
        gateh0 = sb("gateh0", [P, NT, E0], F32R)
        act = sb("act", [P, 4, 512])
        hm = sb("hm", [P, 4, 512])
        Vblk = hm[:, :, :].rearrange("p b (h k) -> p b h k", h=H1)
        sel1f = act[0:2 * E1, :, :].rearrange("p a n -> p (a n)")[:, 0:R1 * P].rearrange("p (r n) -> p r n", r=R1)
        aT1 = act[:, 0:2, :].rearrange("p a (g n) -> p a g n", g=4)
        qT = act[:, 2:4, :]
        soft = sb("soft", [P, 4, H1, KV])
        sc1 = soft[:, 0:2, :, :]
        at1 = soft[:, 2:4, :, :]
        aT0 = soft[:, :, :, :].rearrange("p a h k -> p (a h k)")
        an1 = sb("an1", [P, 2, H1, KV])
        sel0f = an1[0:2 * E0, :, :, :].rearrange("p a h k -> p (a h k)").rearrange("p (e n) -> p e n", e=E0)
        route = an1[:, :, :, :].rearrange("p a h k -> p (a h k)").rearrange("p (r t e) -> p r t e", r=4, e=E1)
        mx1 = sb("mx1", [P, 2, H1])
        z1 = sb("z1", [P, 2, H1])
        rz1 = sb("rz1", [P, 2, H1])
        sg = sb("sg", [P, NT, E1])
        sbs = sb("sbs", [P, NT, E1])
        ra, rb, rc, rd = (route[:, i, :, :] for i in range(4))
        pr = sb("pr", [P, 2, NT * NG, 2])
        gq = sb("gq", [P, 4, NT, NG])
        gs = sb("gs", [P, NT, NG])
        gk = sb("gk", [P, NT, NG])
        thr = sb("thr", [P, NT])
        top8 = sb("top8", [P, NT, 8])
        gate1 = sb("gate1", [P, NT, 2, E1])
        gateh1 = sb("gateh1", [P, NT, E1], F32R)

        class Stages:
            pass

        s = Stages()
        s.ld_ident = sem("ld_ident")
        s.ld_attn0 = sem("ld_attn0")
        s.ld_attn1 = sem("ld_attn1")
        s.ld_small = sem("ld_small")
        s.ld_w1 = sem("ld_w1")
        s.ld_w2_0 = sem("ld_w2_0")
        s.ld_gu = sem("ld_gu")
        s.ld_w2_1 = sem("ld_w2_1")
        s.stored = sem("stored")
        s.pool_const = sem("pool_const")
        s.pool_zero = sem("pool_zero")
        s.pool_step = sem("pool_step")
        s.kblk_ready = sem("kblk_ready")
        s.vblk_ready = sem("vblk_ready")
        s.bo16_ready = sem("bo16_ready")
        s.dve_link = sem("dve_link")
        s.dve_const = sem("dve_const")
        s.ln_stats = sem("ln_stats")
        s.ln_var = sem("ln_var")
        s.ln_rstd = sem("ln_rstd")
        s.xn_ready = sem("xn_ready")
        s.tr_ready = sem("tr_ready")
        s.xT_ready = sem("xT_ready")
        s.xTh_ready = sem("xTh_ready")
        s.xTl_ready = sem("xTl_ready")
        s.kv_mm = sem("kv_mm")
        s.kv_ready = sem("kv_ready")
        s.a0_mm = sem("a0_mm")
        s.a0_ready = sem("a0_ready")
        s.v0_mm = sem("v0_mm")
        s.v0_ready = sem("v0_ready")
        s.wginv_ready = sem("wginv_ready")
        s.wgss_ready = sem("wgss_ready")
        s.wgn_ready = sem("wgn_ready")
        s.wgT_mm = sem("wgT_mm")
        s.wgT_ready = sem("wgT_ready")
        s.r0_mm = sem("r0_mm")
        s.r0_ready = sem("r0_ready")
        s.mask_ready = sem("mask_ready")
        s.s0_mm = sem("s0_mm")
        s.s0_shifted = sem("s0_shifted")
        s.exp0_ready = sem("exp0_ready")
        s.attn0_ready = sem("attn0_ready")
        s.aT0_mm = sem("aT0_mm")
        s.aT0_ready = sem("aT0_ready")
        s.out0_mm = sem("out0_mm")
        s.x1_ready = sem("x1_ready")
        s.v1_mm = sem("v1_mm")
        s.v1_copied = sem("v1_copied")
        s.v1_ready = sem("v1_ready")
        s.lg0_mm = sem("lg0_mm")
        s.gate0_ready = sem("gate0_ready")
        s.gT0_mm = sem("gT0_mm")
        s.gT0_ready = sem("gT0_ready")
        s.b2_mm = sem("b2_mm")
        s.b2_added = sem("b2_added")
        s.w1h_ready = sem("w1h_ready")
        s.w1l_ready = sem("w1l_ready")
        s.sel_ready = sem("sel_ready")
        s.guh_ready = sem("guh_ready")
        s.gul_ready = sem("gul_ready")
        s.h_ready = sem("h_ready")
        s.act_ready = sem("act_ready")
        s.e_ready = sem("e_ready")
        s.hm_ready = sem("hm_ready")
        s.hm_used = sem("hm_used")
        s.o_added = sem("o_added")
        s.q_mm = sem("q_mm")
        s.qT_ready = sem("qT_ready")
        s.s1_mm = sem("s1_mm")
        s.mx1_ready = sem("mx1_ready")
        s.s1_shifted = sem("s1_shifted")
        s.exp1_ready = sem("exp1_ready")
        s.z1_ready = sem("z1_ready")
        s.rz1_ready = sem("rz1_ready")
        s.an1_ready = sem("an1_ready")
        s.t1_mm = sem("t1_mm")
        s.aT1_ready = sem("aT1_ready")
        s.av_mm = sem("av_mm")
        s.x3_ready = sem("x3_ready")
        s.lg1_mm = sem("lg1_mm")
        s.sg_ready = sem("sg_ready")
        s.gate1_ready = sem("gate1_ready")
        s.gT1_mm = sem("gT1_mm")
        s.gT1_ready = sem("gT1_ready")
        s.h_ready1 = sem("h_ready1")
        s.act_ready1 = sem("act_ready1")
        s.e_ready1 = sem("e_ready1")
        s.prod_ready1 = sem("prod_ready1")
        s.hm_ready1 = sem("hm_ready1")
        s.hm_used1 = sem("hm_used1")
        s.o_added1 = sem("o_added1")
        s.ld_x = [sem(f"ld_x{b}") for b in range(B)]

        x_dram = a["x"].rearrange("b (p j) c -> b p j c", p=P)
        out_dram = out.rearrange("b (p j) c -> b p j c", p=P)
        block = ctx.enter_context(nc.Block())

        def tiles(buf, b):
            return buf[:, TPB * b:TPB * (b + 1)]

        def tok(buf, t):
            return buf[:, t * P:(t + 1) * P]

        def chunk(buf, b):
            return buf[:, b * CH:(b + 1) * CH]

        def quarters(n):
            return bank[n][:, :].rearrange("p (j c) -> p j c", j=TPB)

        @block.sync
        def _(sp):
            for b in range(B):
                sp.dma_start(tiles(x, b), x_dram[b]).then_inc(s.ld_x[b], 16)
            sp.dma_start(attn0_w[:, :, :], a["attn0_w"]).then_inc(s.ld_attn0, 16)
            sp.dma_start(w1f[:, :], a["w1"]).then_inc(s.ld_w1, 16)
            sp.dma_start(w2_0[:, :, :], a["w2_0"]).then_inc(s.ld_w2_0, 16)
            sp.wait_ge(s.w1l_ready, 4)
            sp.dma_start(gu1f, a["gu1"]).then_inc(s.ld_gu, 16)
            sp.wait_ge(s.aT0_mm, B)
            sp.dma_start(w2_1[:, :, :], a["w2_1"]).then_inc(s.ld_w2_1, 16)
            sp.dma_start(ws2, a["ws2"]).then_inc(s.ld_w2_1, 16)
            for b in range(B):
                sp.wait_ge(s.o_added1, b + 1)
                sp.dma_start(out_dram[b], tiles(x, b)).then_inc(s.stored, 16)
            sp.wait_ge(s.stored, 16 * B)

        SMALL = [(ctxT, "ctxT"), (cols, "cols"), (wg_sb, "wg"), (small0, "w_redT")]
        LATER = [(b1col, "b1col"), (gate1T, "gate1T"), (blk, "blk"), (below, "below"), (order8, "order8"),
                 (sel0f, "sel0"), (sel1f, "sel1")]
        ROWS = [(gbias[:, :], a["gbias"], [P, E1]), (mask8[:, :], a["mask"], [P, B * KV]),
                (bo_rows[:, 0, :], a["bo0"], [P, C]), (bo_rows[:, 1, :], a["bo1"], [P, C])]
        N_SMALL = 16 * (len(SMALL) + len(LATER) + len(ROWS) + 2)

        def whole(t):
            return t[tuple(slice(None) for _ in t.shape)]

        @block.scalar
        def _(act_e):
            act_e.dma_start(ident[:, :], a["ident"]).then_inc(s.ld_ident, 16)
            for buf, name in SMALL:
                act_e.dma_start(whole(buf), a[name]).then_inc(s.ld_small, 16)
            for dst, src, shape in ROWS:
                act_e.dma_start(dst, src.broadcast_to(shape)).then_inc(s.ld_small, 16)
            for buf, name in LATER:
                act_e.dma_start(whole(buf), a[name]).then_inc(s.ld_small, 16)
            for half in range(2):
                act_e.dma_start(b2_sb[half * E0:(half + 1) * E0, :], a["b2"]).then_inc(s.ld_small, 16)
            act_e.dma_start(attn1_w[:, :, :], a["attn1_w"]).then_inc(s.ld_attn1, 16)

            act_e.wait_ge(s.ld_small, N_SMALL)
            for n, (dst, col) in enumerate(((kT0, 0), (vT0, 2), (kT1, 3), (vT1, 5))):
                act_e.wait_ge(s.kv_mm, n + 1)
                nc.scalar.activation(dst[:, :], bank[n][:, 0:P], ACT.Identity, bias=cols[:, col:col + 1]).then_inc(s.kv_ready, 1)
            act_e.wait_ge(s.a0_mm, 1)
            nc.scalar.activation(A0[:, :], bank[4][:, 0:P], ACT.Copy, scale=float(C) ** -0.5).then_inc(s.a0_ready, 1)
            act_e.wait_ge(s.a0_mm, 2)
            nc.scalar.activation(s0bias[:, :], bank[5][:, 0:P], ACT.Copy, scale=float(C) ** -0.5).then_inc(s.a0_ready, 1)
            nc.scalar.activation(bq1s[:, :], cols[:, 4:5], ACT.Copy, scale=float(D1) ** -0.5).then_inc(s.a0_ready, 1)

            def copy_xT(k, b, n):
                act_e.wait_ge(s.tr_ready, B * k + b + 1)
                nc.scalar.copy(chunk(xT, b), bank[n][:, :]).then_inc(s.xT_ready, 1)

            for b in range(B):
                copy_xT(0, b, b)
            act_e.wait_ge(s.s0_shifted, 1)
            nc.scalar.activation(s0[:, :, :], s0[:, :, :], ACT.Exp).then_inc(s.exp0_ready, 1)
            for b in range(B):
                act_e.wait_ge(s.aT0_mm, b + 1)
                nc.scalar.copy(chunk(aT0, b), bank[b][:, :]).then_inc(s.aT0_ready, 1)
            for b in range(B):
                act_e.wait_ge(s.v1_mm, b + 1)
                nc.scalar.copy(V1[:, b, :, :], quarters(b)).then_inc(s.v1_copied, 1)
            nc.scalar.copy(sel0[:, :, :], sel0f[:, :, :]).then_inc(s.sel_ready, 1)
            nc.scalar.copy(sel1[:, :, :], sel1f[:, :, :]).then_inc(s.sel_ready, 1)
            act_e.wait_ge(s.ld_w1, 16)
            for n in range(4):
                nc.scalar.copy(w1h[:, n * 512:(n + 1) * 512], w1f[:, n * 512:(n + 1) * 512]).then_inc(s.w1h_ready, 1)

            def round_xT(k, b):
                act_e.wait_ge(s.xT_ready, B * k + b + 1)
                if k == 3:
                    act_e.wait_ge(s.o_added, B)
                nc.scalar.copy(chunk(xTh, b), chunk(xT, b)).then_inc(s.xTh_ready, 1)

            for b in range(B):
                copy_xT(1, b, b)
                round_xT(1, b)
            act_e.wait_ge(s.gate0_ready, 1)
            nc.scalar.activation(ex0[:, :, :], lt0[:, :, :], ACT.Exp).then_inc(s.gate0_ready, 1)
            for b in range(B):
                act_e.wait_ge(s.gT0_mm, b + 1)
                nc.scalar.copy(chunk(gT0, b), bank[b][0:2 * E0, :]).then_inc(s.gT0_ready, 1)

            with act_e.Fori(0, B) as c:
                for r in range(R0):
                    act_e.wait_ge(s.h_ready, c * R0 + (r + 1))
                    if r >= 4:
                        act_e.wait_ge(s.hm_ready, c * R0 + (r - 3))
                    nc.scalar.activation(act[:, r % 4, :], bank[r % 2][:, :], ACT.Gelu,
                                         bias=b1col[:, r:r + 1]).then_inc(s.act_ready, 1)

            act_e.wait_ge(s.ld_gu, 16)
            for w in range(2):
                nc.scalar.copy(gu1h[:, w, :], gu1f[:, w, :]).then_inc(s.guh_ready, 1)

            def query(b):
                copy_xT(2, b, 6)
                act_e.wait_ge(s.q_mm, b + 1)
                if b >= 2:
                    act_e.wait_ge(s.s1_mm, TPB * (b - 1))
                nc.scalar.activation(qT[:, b % 2, :], bank[7][:, :], ACT.Identity, bias=bq1s[:, :],
                                     scale=float(D1) ** -0.5).then_inc(s.qT_ready, 1)

            def exp1(i):
                act_e.wait_ge(s.s1_shifted, i + 1)
                if i >= 2:
                    act_e.wait_ge(s.an1_ready, i - 1)
                nc.scalar.activation(at1[:, i % 2, :, :], sc1[:, i % 2, :, :], ACT.Exp).then_inc(s.exp1_ready, 1)

            def attn_copy(i):
                act_e.wait_ge(s.t1_mm, i + 1)
                if i >= 2:
                    act_e.wait_ge(s.av_mm, i - 1)
                nc.scalar.copy(aT1[:, i % 2, :, :], quarters(2 + i % 2)).then_inc(s.aT1_ready, 1)

            query(0)
            for i in range(NT + 1):
                if i < NT:
                    exp1(i)
                if i % TPB == 1 and i // TPB + 1 < B:
                    query(i // TPB + 1)
                if i >= 1:
                    attn_copy(i - 1)

            for b in range(B):
                copy_xT(3, b, b)
                round_xT(3, b)
            for b in range(B):
                act_e.wait_ge(s.lg1_mm, b + 1)
                nc.scalar.activation(tiles(sg, b), quarters(4 + b)[:, :, 0:E1], ACT.Exp, scale=-1.0).then_inc(s.sg_ready, 1)
            for b in range(B):
                act_e.wait_ge(s.gT1_mm, b + 1)
                nc.scalar.copy(chunk(gT1, b), bank[b][0:2 * E1, :]).then_inc(s.gT1_ready, 1)

            with act_e.Fori(0, B) as c:
                for r in range(R1 + 1):
                    m = P if r < R1 else I1
                    act_e.wait_ge(s.h_ready1, c * (R1 + 1) + (r + 1))
                    if r >= 4:
                        act_e.wait_ge(s.hm_ready1, c * (R1 + 1) + (r - 3))
                    nc.scalar.activation(act[0:m, r % 4, :], bank[r % 2][0:m, :], ACT.Silu).then_inc(s.act_ready1, 1)

        @block.gpsimd
        def _(pool):
            n = [0]

            def step(ins):
                n[0] += 1
                ins.then_inc(s.pool_step, 1)
                pool.wait_ge(s.pool_step, n[0])

            def rstd_of(k):
                pool.wait_ge(s.ln_var, NT * (k + 1))
                step(nc.gpsimd.tensor_scalar(ve[:, :], mv[:, :, 1], EPS, None, ALU.add))
                nc.gpsimd.tensor_tensor(rstd[:, :], ve[:, :], mhalf[:, :], ALU.pow).then_inc(s.ln_rstd, 1)

            step(nc.gpsimd.memset(mhalf[:, :], -0.5))
            nc.gpsimd.memset(attn0[:, :, :], 0.0).then_inc(s.pool_zero, 1)
            nc.gpsimd.memset(R0w[:, :], 0.0).then_inc(s.pool_zero, 1)
            rstd_of(0)
            step(nc.gpsimd.memset(R1w[:, :], 0.0))
            pool.wait_ge(s.wgss_ready, 1)
            step(nc.gpsimd.tensor_scalar(wgss[:, :], wgss[:, :], 1e-8, None, ALU.max))
            nc.gpsimd.tensor_tensor(wginv[:, :], wgss[:, :], mhalf[0:E0, 0:1], ALU.pow).then_inc(s.wginv_ready, 1)
            pool.wait_ge(s.ld_small, N_SMALL)
            nc.gpsimd.tensor_copy(R1w[:, 0:E1], gate1T[:, :]).then_inc(s.pool_const, 1)
            nc.gpsimd.tensor_scalar(bo16[:, :], bo_rows[:, 1, :], 1.0 / H1, None, ALU.mult).then_inc(s.pool_const, 1)
            pool.wait_ge(s.kv_ready, 4)
            for src, dst, ready in ((vT1, Vblk, s.vblk_ready), (kT1, Kblk, s.kblk_ready)):
                for b in range(B):
                    rows = src[:, b * KV:(b + 1) * KV].unsqueeze(1).broadcast_to([P, H1, KV])
                    nc.gpsimd.tensor_tensor(dst[:, b, :, :], rows, blk[:, :].unsqueeze(2).broadcast_to([P, H1, KV]),
                                            ALU.mult).then_inc(ready, 1)
            rstd_of(1)
            for b in range(B):
                pool.wait_ge(s.v1_copied, b + 1)
                pool.wait_ge(s.pool_const, 2)
                nc.gpsimd.tensor_tensor(V1[:, b, :, :], V1[:, b, :, :],
                                        bo16[:, :].unsqueeze(1).broadcast_to([P, 4, C]), ALU.add).then_inc(s.v1_ready, 1)
            for q in range(4):
                pool.wait_ge(s.w1h_ready, q + 1)
                nc.gpsimd.tensor_tensor(w1l[:, q * 512:(q + 1) * 512], w1f[:, q * 512:(q + 1) * 512],
                                        w1h[:, q * 512:(q + 1) * 512].bitcast(F32), ALU.subtract).then_inc(s.w1l_ready, 1)

            def low_half(k, b):
                pool.wait_ge(s.xTh_ready, B * (k == 3) + b + 1)
                nc.gpsimd.tensor_tensor(chunk(xTl, b), chunk(xT, b), chunk(xTh, b).bitcast(F32),
                                        ALU.subtract).then_inc(s.xTl_ready, 1)

            for b in range(B):
                low_half(1, b)
            rstd_of(2)
            for w in range(2):
                pool.wait_ge(s.guh_ready, w + 1)
                nc.gpsimd.tensor_tensor(gu1l[:, w, :], gu1f[:, w, :], gu1h[:, w, :].bitcast(F32),
                                        ALU.subtract).then_inc(s.gul_ready, 1)
            for i in range(NT):
                pool.wait_ge(s.rz1_ready, i + 1)
                if i >= 2:
                    pool.wait_ge(s.t1_mm, i - 1)
                nc.gpsimd.tensor_tensor(an1[:, i % 2, :, :], at1[:, i % 2, :, :],
                                        rz1[:, i % 2, :].unsqueeze(2).broadcast_to([P, H1, KV]),
                                        ALU.mult).then_inc(s.an1_ready, 1)
            rstd_of(3)
            for b in range(B):
                low_half(3, b)

        @block.vector
        def _(v):
            n = [0]

            def step(ins):
                n[0] += 1
                ins.then_inc(s.dve_link, 1)
                v.wait_ge(s.dve_link, n[0])

            def layernorm(k):
                for t in range(NT):
                    if k == 0 and t % TPB == 0:
                        v.wait_ge(s.ld_x[t // TPB], 16)
                    nc.vector.bn_stats(st[:, t, :], x[:, t, :]).then_inc(s.ln_stats, 1)
                for t in range(NT):
                    v.wait_ge(s.ln_stats, NT * k + t + 1)
                    nc.vector.bn_aggr(mv[:, t, :], st[:, t, :]).then_inc(s.ln_var, 1)
                v.wait_ge(s.ln_rstd, k + 1)
                if k:
                    v.wait_ge(s.tr_ready, B * k)
                for t in range(NT):
                    nc.vector.tensor_scalar(xn[:, t, :], x[:, t, :], mv[:, t, 0:1], rstd[:, t:t + 1],
                                            ALU.subtract, ALU.mult).then_inc(s.xn_ready, 1)

            nc.vector.memset(onesb[:, :], 1.0).then_inc(s.dve_const, 1)
            step(nc.vector.memset(ones[:, :], 1.0))
            layernorm(0)
            v.wait_ge(s.ld_small, N_SMALL)
            nc.vector.tensor_scalar(bqrep[:, :], ones[:, :], cols[:, 1:2], None, ALU.mult).then_inc(s.dve_const, 1)
            step(nc.vector.tensor_tensor(wgsq[:, :], wg_sb[:, :], wg_sb[:, :], ALU.mult))
            nc.vector.tensor_reduce(wgss[:, :], wgsq[:, :], AX, ALU.add).then_inc(s.wgss_ready, 1)
            v.wait_ge(s.wginv_ready, 1)
            nc.vector.tensor_scalar(wgn[:, :], wg_sb[:, :], wginv[:, 0:1], None, ALU.mult).then_inc(s.wgn_ready, 1)
            v.wait_ge(s.wgT_mm, 1)
            nc.vector.tensor_copy(wgnT[:, :], bank[7][0:G0, 0:E0]).then_inc(s.wgT_ready, 1)
            v.wait_ge(s.v0_mm, 1)
            nc.vector.tensor_tensor(V0[:, :], bank[6][:, 0:C], bo_rows[:, 0, :], ALU.add).then_inc(s.v0_ready, 1)
            v.wait_ge(s.r0_mm, 1)
            v.wait_ge(s.pool_zero, 2)
            nc.vector.tensor_copy(R0w[:, 0:E0], bank[7][:, P:P + E0]).then_inc(s.r0_ready, 1)

            v.wait_ge(s.a0_ready, 2)
            for b in range(B):
                v.wait_ge(s.s0_mm, b + 1)
                own = slice(b * KV, (b + 1) * KV)
                bias = s0bias[:, own].unsqueeze(1).broadcast_to([P, TPB, KV])
                step(nc.vector.tensor_tensor(tiles(s0, b), quarters(4 + b)[:, :, own], bias, ALU.add))
            step(nc.vector.tensor_reduce(m0[:, :], s0[:, :, :], AX, ALU.max))
            nc.vector.tensor_tensor(s0[:, :, :], s0[:, :, :], m0[:, :].unsqueeze(2).broadcast_to([P, NT, KV]),
                                    ALU.subtract).then_inc(s.s0_shifted, 1)
            v.wait_ge(s.exp0_ready, 1)
            step(nc.vector.tensor_reduce(z0[:, :], s0[:, :, :], AX, ALU.add))
            step(nc.vector.reciprocal(rz0[:, :], z0[:, :]))
            for b in range(B):
                nc.vector.tensor_tensor(tiles(attn0, b)[:, :, b * KV:(b + 1) * KV], tiles(s0, b),
                                        tiles(rz0, b).unsqueeze(2).broadcast_to([P, TPB, KV]),
                                        ALU.mult).then_inc(s.attn0_ready, 1)
            for b in range(B):
                v.wait_ge(s.out0_mm, b + 1)
                nc.vector.tensor_tensor(tiles(x, b), tiles(x, b), quarters(4 + b), ALU.add).then_inc(s.x1_ready, 1)
            v.wait_ge(s.x1_ready, B)
            layernorm(1)

            for b in range(B):
                v.wait_ge(s.lg0_mm, b + 1)
                step(nc.vector.tensor_copy(tiles(lg0, b), quarters(4 + b)[:, :, 0:E0]))

            def over(col, width):
                return col[:, :].unsqueeze(2).broadcast_to([P, NT, width])

            step(nc.vector.tensor_reduce(m0[:, :], lg0[:, :, :], AX, ALU.max))
            nc.vector.tensor_tensor(lt0[:, :, :], lg0[:, :, :], over(m0, E0), ALU.subtract).then_inc(s.gate0_ready, 1)
            step(nc.vector.tensor_tensor(oh0[:, :, :], lg0[:, :, :], over(m0, E0), ALU.is_equal))
            step(nc.vector.tensor_tensor(oh0[:, :, :], oh0[:, :, :],
                                         order8[:, :].unsqueeze(1).broadcast_to([P, NT, E0]), ALU.mult))
            step(nc.vector.tensor_reduce(m0[:, :], oh0[:, :, :], AX, ALU.max))
            step(nc.vector.tensor_tensor(oh0[:, :, :], oh0[:, :, :], over(m0, E0), ALU.is_equal))
            v.wait_ge(s.gate0_ready, 2)
            step(nc.vector.tensor_reduce(z0[:, :], ex0[:, :, :], AX, ALU.add))
            step(nc.vector.reciprocal(rz0[:, :], z0[:, :]))
            step(nc.vector.tensor_tensor(oh0[:, :, :], oh0[:, :, :], over(rz0, E0), ALU.mult))
            step(nc.vector.tensor_copy(gateh0[:, :, :], oh0[:, :, :]))
            step(nc.vector.tensor_copy(gate0[:, :, 0, :], gateh0[:, :, :].bitcast(F32)))
            nc.vector.tensor_tensor(gate0[:, :, 1, :], oh0[:, :, :], gateh0[:, :, :].bitcast(F32),
                                    ALU.subtract).then_inc(s.gate0_ready, 1)
            for b in range(B):
                v.wait_ge(s.b2_mm, b + 1)
                nc.vector.tensor_tensor(tiles(x, b), tiles(x, b), quarters(4 + b), ALU.add).then_inc(s.b2_added, 1)
            v.wait_ge(s.b2_added, B)

            with v.Fori(0, B) as c:
                for r in range(R0):
                    v.wait_ge(s.act_ready, c * R0 + (r + 1))
                    v.wait_ge(s.e_ready, c * E0 + (r // 2 + 1))
                    if r >= 4:
                        v.wait_ge(s.hm_used, c * R0 + (r - 3))
                    nc.vector.tensor_tensor(hm[:, r % 4, :], act[:, r % 4, :], bank[2 + r // 2 % 2][:, :],
                                            ALU.mult).then_inc(s.hm_ready, 1)
                v.wait_ge(s.hm_used, c * R0 + R0)
                xc = x[:, bass.ds(c * TPB, TPB), :]
                nc.vector.tensor_tensor(xc, xc, quarters(4), ALU.add).then_inc(s.o_added, 1)
            v.wait_ge(s.o_added, B)

            layernorm(2)
            v.wait_ge(s.ld_small, N_SMALL)
            for b in range(B):
                cover = mask8[:, b * KV:(b + 1) * KV].unsqueeze(1).broadcast_to([P, H1, KV])
                nc.vector.tensor_scalar(maskrow[:, b, :, :], cover, -BIG / P, None, ALU.mult).then_inc(s.mask_ready, 1)

            def shift(i):
                v.wait_ge(s.s1_mm, i + 1)
                scores = bank[i % 2][:, :].rearrange("p (h k) -> p h k", h=H1)
                nc.vector.tensor_reduce(mx1[:, i % 2, :], scores, AX, ALU.max).then_inc(s.mx1_ready, 1)
                v.wait_ge(s.mx1_ready, i + 1)
                if i >= 2:
                    v.wait_ge(s.exp1_ready, i - 1)
                nc.vector.tensor_tensor(sc1[:, i % 2, :, :], scores, mx1[:, i % 2, :].unsqueeze(2).broadcast_to(
                    [P, H1, KV]), ALU.subtract).then_inc(s.s1_shifted, 1)

            def total(i):
                v.wait_ge(s.exp1_ready, i + 1)
                nc.vector.tensor_reduce(z1[:, i % 2, :], at1[:, i % 2, :, :], AX, ALU.add).then_inc(s.z1_ready, 1)
                v.wait_ge(s.z1_ready, i + 1)
                nc.vector.reciprocal(rz1[:, i % 2, :], z1[:, i % 2, :]).then_inc(s.rz1_ready, 1)

            def add_attention(b):
                v.wait_ge(s.av_mm, TPB * (b + 1))
                nc.vector.tensor_tensor(tiles(x, b), tiles(x, b), quarters(4 + b % 2), ALU.add).then_inc(s.x3_ready, 1)

            for i in range(NT + 3):
                if i < NT:
                    shift(i)
                if 1 <= i <= NT:
                    total(i - 1)
                if i >= 6 and (i - 6) % TPB == 0:
                    add_attention((i - 6) // TPB)
            v.wait_ge(s.x3_ready, B)
            layernorm(3)

            v.wait_ge(s.sg_ready, B)
            step(nc.vector.tensor_scalar(sg[:, :, :], sg[:, :, :], 1.0, None, ALU.add))
            step(nc.vector.reciprocal(sg[:, :, :], sg[:, :, :]))
            step(nc.vector.tensor_tensor(sbs[:, :, :], sg[:, :, :], gbias[:, :].unsqueeze(1).broadcast_to([P, NT, E1]),
                                         ALU.add))
            pairs = sbs[:, :, :].rearrange("p t (g u w) -> p (t g u) w", g=NG, w=2)
            hi = pr[:, 0, :, :].rearrange("p n u -> p (n u)")
            lo = pr[:, 1, :, :].rearrange("p n u -> p (n u)")
            step(nc.vector.tensor_tensor(hi, pairs[:, :, 0], pairs[:, :, 1], ALU.max))
            step(nc.vector.tensor_tensor(lo, pairs[:, :, 0], pairs[:, :, 1], ALU.min))
            g4 = [gq[:, i, :, :].rearrange("p t g -> p (t g)") for i in range(4)]
            step(nc.vector.tensor_tensor(g4[0], pr[:, 0, :, 0], pr[:, 0, :, 1], ALU.max))
            step(nc.vector.tensor_tensor(g4[1], pr[:, 0, :, 0], pr[:, 0, :, 1], ALU.min))
            step(nc.vector.tensor_tensor(g4[2], pr[:, 1, :, 0], pr[:, 1, :, 1], ALU.max))
            step(nc.vector.tensor_tensor(g4[3], g4[1], g4[2], ALU.max))
            step(nc.vector.tensor_tensor(gs[:, :, :].rearrange("p t g -> p (t g)"), g4[0], g4[3], ALU.add))
            others = gs[:, :, :].unsqueeze(2).broadcast_to([P, NT, NG, NG])
            own = gs[:, :, :].unsqueeze(3).broadcast_to([P, NT, NG, NG])
            above, equal = (z.rearrange("p t (g h) -> p t g h", g=NG) for z in (ra, rb))
            step(nc.vector.tensor_tensor(above, others, own, ALU.is_gt))
            step(nc.vector.tensor_tensor(equal, others, own, ALU.is_equal))
            step(nc.vector.tensor_tensor(equal, equal, below[:, :, :].unsqueeze(1).broadcast_to([P, NT, NG, NG]), ALU.mult))
            step(nc.vector.tensor_tensor(above, above, equal, ALU.add))
            step(nc.vector.tensor_reduce(gk[:, :, :], above, AX, ALU.add))
            step(nc.vector.tensor_scalar(gk[:, :, :], gk[:, :, :], float(TOPG), -BIG, ALU.is_ge, ALU.mult))
            grouped = sbs[:, :, :].rearrange("p t (g w) -> p t g w", g=NG)
            step(nc.vector.tensor_tensor(rc.rearrange("p t (g w) -> p t g w", g=NG), grouped,
                                         gk[:, :, :].unsqueeze(3).broadcast_to([P, NT, NG, NG]), ALU.add))
            for t in range(NT):
                last = nc.vector.max(top8[:, t, :], rc[:, t, :])
                n[0] += 1
                last.then_inc(s.dve_link, 1)
            v.wait_ge(s.dve_link, n[0])
            fourth = top8[:, :, TOPK - 1:TOPK].broadcast_to([P, NT, E1])
            step(nc.vector.tensor_tensor(ra, rc, fourth, ALU.is_gt))
            step(nc.vector.tensor_tensor(rb, rc, fourth, ALU.is_equal))
            step(nc.vector.tensor_reduce(thr[:, :], ra, AX, ALU.add))
            step(nc.vector.tensor_scalar(thr[:, :], thr[:, :], -1.0, float(TOPK), ALU.mult, ALU.add))
            src, dst = rb, rc
            for shift_by in (1, 2, 4, 8):
                step(nc.vector.tensor_copy(dst[:, :, 0:shift_by], src[:, :, 0:shift_by]))
                step(nc.vector.tensor_tensor(dst[:, :, shift_by:], src[:, :, shift_by:], src[:, :, 0:E1 - shift_by], ALU.add))
                src, dst = dst, (rd if dst is rc else rc)
            step(nc.vector.tensor_tensor(src, src, over(thr, E1), ALU.is_le))
            step(nc.vector.tensor_tensor(rb, rb, src, ALU.mult))
            step(nc.vector.tensor_tensor(ra, ra, rb, ALU.add))
            step(nc.vector.tensor_tensor(ra, ra, sg[:, :, :], ALU.mult))
            step(nc.vector.tensor_reduce(thr[:, :], ra, AX, ALU.add))
            step(nc.vector.tensor_scalar(thr[:, :], thr[:, :], 1e-20, None, ALU.add))
            step(nc.vector.reciprocal(thr[:, :], thr[:, :]))
            step(nc.vector.tensor_scalar(thr[:, :], thr[:, :], SCALE, None, ALU.mult))
            step(nc.vector.tensor_tensor(ra, ra, over(thr, E1), ALU.mult))
            step(nc.vector.tensor_copy(gateh1[:, :, :], ra))
            step(nc.vector.tensor_copy(gate1[:, :, 0, :], gateh1[:, :, :].bitcast(F32)))
            nc.vector.tensor_tensor(gate1[:, :, 1, :], ra, gateh1[:, :, :].bitcast(F32), ALU.subtract).then_inc(s.gate1_ready, 1)

            with v.Fori(0, B) as c:
                for r in range(R1 + 1):
                    m = P if r < R1 else I1
                    v.wait_ge(s.act_ready1, c * (R1 + 1) + (r + 1))
                    if r >= 4:
                        v.wait_ge(s.hm_used1, c * (R1 + 1) + (r - 3))
                    if r < R1:
                        nc.vector.tensor_tensor(act[:, r % 4, :], act[:, r % 4, :], bank[2 + r % 2][:, :],
                                                ALU.mult).then_inc(s.prod_ready1, 1)
                        v.wait_ge(s.prod_ready1, c * R1 + (r + 1))
                        v.wait_ge(s.e_ready1, c * R1 + (r + 1))
                        nc.vector.tensor_tensor(hm[:, r % 4, :], act[:, r % 4, :], bank[4 + r % 2][:, :],
                                                ALU.mult).then_inc(s.hm_ready1, 1)
                    else:
                        nc.vector.tensor_tensor(hm[0:m, r % 4, :], act[0:m, r % 4, :], bank[2 + r % 2][0:m, :],
                                                ALU.mult).then_inc(s.hm_ready1, 1)
                v.wait_ge(s.hm_used1, c * (R1 + 1) + (R1 + 1))
                xc = x[:, bass.ds(c * TPB, TPB), :]
                nc.vector.tensor_tensor(xc, xc, quarters(6), ALU.add).then_inc(s.o_added1, 1)

        @block.tensor
        def _(pe):
            def mm(dst, lhsT, rhs, start=True, stop=True):
                return nc.tensor.matmul(dst, lhsT, rhs, start=start, stop=stop, skip_group_check=True)

            def split_mm(dst, wh, wl, xh, xl):
                mm(dst, wh, xh, start=True, stop=False)
                mm(dst, wh, xl, start=False, stop=False)
                return mm(dst, wl, xh, start=False, stop=True)

            def transposes(k, b, n):
                pe.wait_ge(s.xn_ready, NT * k + TPB * (b + 1))
                for j in range(TPB):
                    last = nc.tensor.transpose(quarters(n)[:, j, :], xn[:, TPB * b + j, :], ident[:, :])
                last.then_inc(s.tr_ready, 1)

            pe.wait_ge(s.ld_small, N_SMALL)
            pe.wait_ge(s.ld_attn0, 16)
            pe.wait_ge(s.ld_attn1, 16)
            for i, w in enumerate((attn0_w[:, 0, :], attn0_w[:, 2, :], attn1_w[:, 0, :], attn1_w[:, 2, :])):
                mm(bank[i][:, 0:P], w, ctxT[:, :]).then_inc(s.kv_mm, 1)
            pe.wait_ge(s.kv_ready, 1)
            mm(bank[4][:, 0:P], attn0_w[:, 1, :], kT0[:, :]).then_inc(s.a0_mm, 1)
            pe.wait_ge(s.dve_const, 2)
            mm(bank[5][:, 0:P], bqrep[:, :], kT0[:, :]).then_inc(s.a0_mm, 1)
            pe.wait_ge(s.kv_ready, 4)
            mm(bank[6][:, 0:P], vT0[:, :], attn0_w[:, 3, :]).then_inc(s.v0_mm, 1)
            pe.wait_ge(s.ld_ident, 16)
            for b in range(B):
                transposes(0, b, b)
            pe.wait_ge(s.wgn_ready, 1)
            nc.tensor.transpose(bank[7][0:G0, 0:E0], wgn[:, :], ident[0:E0, 0:E0]).then_inc(s.wgT_mm, 1)
            pe.wait_ge(s.wgT_ready, 1)
            mm(bank[7][:, P:P + E0], small0[:, :], wgnT[:, :]).then_inc(s.r0_mm, 1)
            pe.wait_ge(s.a0_ready, 2)
            pe.wait_ge(s.v0_ready, 1)
            pe.wait_ge(s.r0_ready, 1)
            for b in range(B):
                pe.wait_ge(s.xT_ready, b + 1)
                for j in range(TPB):
                    last = mm(quarters(4 + b)[:, j, :], tok(xT, TPB * b + j), A0[:, :])
                last.then_inc(s.s0_mm, 1)
            for b in range(B):
                pe.wait_ge(s.attn0_ready, b + 1)
                pe.wait_ge(s.pool_zero, 1)
                for j in range(TPB):
                    last = nc.tensor.transpose(quarters(b)[:, j, :], attn0[:, TPB * b + j, :], ident[:, :])
                last.then_inc(s.aT0_mm, 1)
            for b in range(B):
                pe.wait_ge(s.aT0_ready, b + 1)
                for j in range(TPB):
                    mm(quarters(4 + b)[:, j, :], tok(xT, TPB * b + j), attn0_w[:, 3, :], stop=False)
                    last = mm(quarters(4 + b)[:, j, :], tok(aT0, TPB * b + j), V0[:, :], start=False)
                last.then_inc(s.out0_mm, 1)
            for b in range(B):
                pe.wait_ge(s.vblk_ready, b + 1)
                for g in range(4):
                    last = mm(quarters(b)[:, g, :], Vblk[:, b, 4 * g:4 * g + 4, :], attn1_w[:, 3, :])
                last.then_inc(s.v1_mm, 1)
            for b in range(B):
                pe.wait_ge(s.v1_copied, b + 1)
                transposes(1, b, b)
            for b in range(B):
                pe.wait_ge(s.xT_ready, B + b + 1)
                for j in range(TPB):
                    last = mm(quarters(4 + b)[:, j, :], tok(xT, TPB * b + j), R0w[:, :])
                last.then_inc(s.lg0_mm, 1)
            pe.wait_ge(s.gate0_ready, 3)
            for b in range(B):
                for j in range(TPB):
                    pair = gate0[:, TPB * b + j, :, :].rearrange("p u e -> p (u e)")
                    last = nc.tensor.transpose(quarters(b)[0:2 * E0, j, :], pair, ident[:, :])
                last.then_inc(s.gT0_mm, 1)
            for b in range(B):
                pe.wait_ge(s.gT0_ready, b + 1)
                for j in range(TPB):
                    last = mm(quarters(4 + b)[:, j, :], tok(gT0, TPB * b + j).bitcast(F32), b2_sb[:, :])
                last.then_inc(s.b2_mm, 1)

            pe.wait_ge(s.b2_added, B)
            pe.wait_ge(s.w1l_ready, 4)
            pe.wait_ge(s.xTl_ready, B)
            pe.wait_ge(s.sel_ready, 2)
            pe.wait_ge(s.ld_w2_0, 16)
            with pe.Fori(0, B) as c:
                cols_c = bass.ds(c * CH, CH)
                for r in range(R0 + LAG):
                    if r < R0:
                        if r >= 2:
                            pe.wait_ge(s.act_ready, c * R0 + (r - 1))
                        if r >= 4 and r % 2 == 0:
                            pe.wait_ge(s.hm_ready, c * R0 + (r - 2))
                        split_mm(bank[r % 2][:, :], tok(w1h, r), tok(w1l, r), xTh[:, cols_c], xTl[:, cols_c])\
                            .then_inc(s.h_ready, 1)
                        if r % 2 == 0:
                            mm(bank[2 + r // 2 % 2][:, :], sel0[:, r // 2, :], gT[0:2 * E0, cols_c])\
                                .then_inc(s.e_ready, 1)
                    if r >= LAG:
                        q = r - LAG
                        pe.wait_ge(s.hm_ready, c * R0 + (q + 1))
                        for j in range(TPB):
                            last = mm(quarters(4)[:, j, :], hm[:, q % 4, j * P:(j + 1) * P], w2_0[:, q, :],
                                      start=(q == 0 and j == 0), stop=(q == R0 - 1))
                        last.then_inc(s.hm_used, 1)

            def queries(b):
                if b:
                    pe.wait_ge(s.xT_ready, 2 * B + b)
                transposes(2, b, 6)
                pe.wait_ge(s.xT_ready, 2 * B + b + 1)
                if b:
                    pe.wait_ge(s.qT_ready, b)
                mm(bank[7][:, :], attn1_w[:, 1, :], chunk(xT, b)).then_inc(s.q_mm, 1)

            def scores(i):
                b = i // TPB
                pe.wait_ge(s.qT_ready, b + 1)
                if i >= 2:
                    pe.wait_ge(s.s1_shifted, i - 1)
                mm(bank[i % 2][:, :], qT[:, b % 2, (i % TPB) * P:(i % TPB + 1) * P],
                   Kblk[:, b, :, :].rearrange("p h k -> p (h k)"), stop=False)
                pe.wait_ge(s.mask_ready, b + 1)
                mm(bank[i % 2][:, :], onesb[:, :], maskrow[:, b, :, :].rearrange("p h k -> p (h k)"), start=False)\
                    .then_inc(s.s1_mm, 1)

            def attn_transposes(i):
                pe.wait_ge(s.an1_ready, i + 1)
                if i >= 2:
                    pe.wait_ge(s.aT1_ready, i - 1)
                for g in range(4):
                    last = nc.tensor.transpose(quarters(2 + i % 2)[:, g, :],
                                               an1[:, i % 2, 4 * g:4 * g + 4, :].rearrange("p h k -> p (h k)"),
                                               ident[:, :])
                last.then_inc(s.t1_mm, 1)

            def attn_values(i):
                b, j = i // TPB, i % TPB
                pe.wait_ge(s.aT1_ready, i + 1)
                if j == 0 and b >= 2:
                    pe.wait_ge(s.x3_ready, b - 1)
                for g in range(4):
                    last = mm(quarters(4 + b % 2)[:, j, :], aT1[:, i % 2, g, :], V1[:, b, g, :],
                              start=(g == 0), stop=(g == 3))
                last.then_inc(s.av_mm, 1)

            pe.wait_ge(s.o_added, B)
            pe.wait_ge(s.kblk_ready, B)
            pe.wait_ge(s.v1_ready, B)
            queries(0)
            for i in range(NT + 2):
                if i < NT:
                    scores(i)
                if i % TPB == 1 and i // TPB + 1 < B:
                    queries(i // TPB + 1)
                if 1 <= i <= NT:
                    attn_transposes(i - 1)
                if i >= 2:
                    attn_values(i - 2)

            for b in range(B):
                transposes(3, b, b)
            for b in range(B):
                pe.wait_ge(s.xT_ready, 3 * B + b + 1)
                for j in range(TPB):
                    last = mm(quarters(4 + b)[:, j, :], tok(xT, TPB * b + j), R1w[:, :])
                last.then_inc(s.lg1_mm, 1)
            pe.wait_ge(s.gate1_ready, 1)
            for b in range(B):
                for j in range(TPB):
                    pair = gate1[:, TPB * b + j, :, :].rearrange("p u e -> p (u e)")
                    last = nc.tensor.transpose(quarters(b)[0:2 * E1, j, :], pair, ident[:, :])
                last.then_inc(s.gT1_mm, 1)

            pe.wait_ge(s.gT1_ready, B)
            pe.wait_ge(s.sg_ready, B)
            pe.wait_ge(s.xTl_ready, 2 * B)
            pe.wait_ge(s.gul_ready, 2)
            pe.wait_ge(s.ld_w2_1, 32)
            with pe.Fori(0, B) as c:
                cols_c = bass.ds(c * CH, CH)
                base = c * (R1 + 1)
                for r in range(R1 + 1 + LAG):
                    if r <= R1:
                        m = P if r < R1 else I1
                        rows = slice(r * P, r * P + m)
                        if r >= 2:
                            pe.wait_ge(s.hm_ready1, base + (r - 1))
                        for w in range(2):
                            last = split_mm(bank[2 * w + r % 2][0:m, :], gu1h[:, w, rows], gu1l[:, w, rows],
                                            xTh[:, cols_c], xTl[:, cols_c])
                        last.then_inc(s.h_ready1, 1)
                        if r < R1:
                            mm(bank[4 + r % 2][:, :], sel1[:, r, :], gT[:, cols_c]).then_inc(s.e_ready1, 1)
                    if r >= LAG:
                        q = r - LAG
                        m = P if q < R1 else I1
                        pe.wait_ge(s.hm_ready1, base + (q + 1))
                        for j in range(TPB):
                            last = mm(quarters(6)[:, j, :], hm[0:m, q % 4, j * P:(j + 1) * P],
                                      w2_1[:, q, :] if q < R1 else ws2,
                                      start=(q == 0 and j == 0), stop=(q == R1))
                        last.then_inc(s.hm_used1, 1)


def kernel(x, ctx_1024, mask_BxS2_bf0, L0_xattn_Wq, L0_xattn_bq, L0_xattn_Wk, L0_xattn_bk, L0_xattn_Wv, L0_xattn_bv,
           L0_xattn_Wo, L0_xattn_bo, L0_ffn_w_red, L0_ffn_wg, L0_ffn_W1, L0_ffn_b1, L0_ffn_W2, L0_ffn_b2,
           L1_xattn_Wq, L1_xattn_bq, L1_xattn_Wk, L1_xattn_bk, L1_xattn_Wv, L1_xattn_bv, L1_xattn_Wo, L1_xattn_bo,
           L1_ffn_gate_w, L1_ffn_gate_bias, L1_ffn_w1, L1_ffn_w2, L1_ffn_w3, L1_ffn_ws1, L1_ffn_ws2, L1_ffn_ws3):
    import numpy as np
    import concourse.bacc as bacc
    from concourse.bass_utils import run_bass_kernel_spmd

    def up(*parts):
        return np.stack([np.asarray(q) for q in parts], axis=1)

    arrays = {
        "x": np.asarray(x),
        "ctxT": np.asarray(ctx_1024).reshape(B * KV, C).T,
        "ident": np.eye(P, dtype=np.float32),
        "attn0_w": up(np.asarray(L0_xattn_Wk).T, L0_xattn_Wq, np.asarray(L0_xattn_Wv).T, np.asarray(L0_xattn_Wo).T),
        "attn1_w": up(L1_xattn_Wk, L1_xattn_Wq, L1_xattn_Wv, L1_xattn_Wo),
        "cols": up(L0_xattn_bk, L0_xattn_bq, L0_xattn_bv, L1_xattn_bk, L1_xattn_bq, L1_xattn_bv),
        "b1col": np.asarray(L0_ffn_b1).reshape(R0, P).T,
        "bo0": np.asarray(L0_xattn_bo).reshape(1, C),
        "bo1": np.asarray(L1_xattn_bo).reshape(1, C),
        "w_redT": np.asarray(L0_ffn_w_red).T,
        "wg": np.asarray(L0_ffn_wg),
        "gate1T": np.asarray(L1_ffn_gate_w).T,
        "gbias": np.asarray(L1_ffn_gate_bias).reshape(1, E1),
        "mask": np.asarray(mask_BxS2_bf0).reshape(1, B * KV),
        "blk": np.repeat(np.eye(H1, dtype=np.float32), D1, axis=0),
        "below": np.broadcast_to(np.tril(np.ones((NG, NG), np.float32), -1), (P, NG, NG)),
        "order8": np.broadcast_to(np.arange(E0, 0, -1, dtype=np.float32), (P, E0)),
        "sel0": np.broadcast_to(np.tile(np.eye(E0, dtype=np.float32), (2, 1))[:, :, None], (2 * E0, E0, P)),
        "sel1": np.tile(np.repeat(np.eye(E1, dtype=np.float32), I1, axis=1), (2, 1)).reshape(2 * E1, R1, P),
        "b2": np.asarray(L0_ffn_b2),
        "w1": np.asarray(L0_ffn_W1).transpose(1, 0, 2).reshape(C, R0 * P),
        "w2_0": np.asarray(L0_ffn_W2).reshape(R0, P, C).transpose(1, 0, 2),
        "gu1": up(*(np.concatenate([np.asarray(w).reshape(E1 * I1, C), np.asarray(sw)]).T
                    for w, sw in ((L1_ffn_w1, L1_ffn_ws1), (L1_ffn_w3, L1_ffn_ws3)))),
        "w2_1": np.asarray(L1_ffn_w2).transpose(0, 2, 1).reshape(R1, P, C).transpose(1, 0, 2),
        "ws2": np.asarray(L1_ffn_ws2).T,
    }
    arrays = {f"in_{k}": np.ascontiguousarray(v) for k, v in arrays.items()}
    nc = bacc.Bacc("TRN2", target_bir_lowering=False, num_devices=1)
    aps = {k[3:]: nc.dram_tensor(k, v.shape, mybir.dt.from_np(v.dtype), kind="ExternalInput").ap()
           for k, v in arrays.items()}
    out = nc.dram_tensor("out_x", (B, CH, C), F32, kind="ExternalOutput").ap()
    xattn_moe_kernel(nc, aps, out)
    r = run_bass_kernel_spmd(nc, [arrays], core_ids=[0])
    return r.results[0]["out_x"]
```

```python
from contextlib import ExitStack

import concourse.bass as bass
from concourse import mybir

F32 = mybir.dt.float32
F32R = mybir.dt.float32r
BF16 = mybir.dt.bfloat16
U8 = mybir.dt.uint8
ALU = mybir.AluOpType
ACT = mybir.ActivationFunctionType
AX = mybir.AxisListType.X

P = 128
C = 128
B = 4
TPB = 4
NT = B * TPB
CH = TPB * P
KV = 32
H1 = 16
D1 = C // H1
E0 = 8
R0 = 16
G0 = 16
E1 = 16
I1 = 96
R1 = E1 * I1 // P
NG = 4
TOPG = 2
TOPK = 4
SCALE = 2.5
EPS = 1e-5
BIG = 1e30
LAG = 2
CTX_COLS, W_COLS = B * KV, 4 * C

(STATS, NORM, XT, SCORES, SOFTMAX, ATTN_T, OUT, NORM2, XT2, LOGITS, GATES, GATES_T, BIAS2) = ITEMS = range(13)
LINKS0 = 14

PACK_A = {"ident": P, "ctxT": B * KV, "attn0_w": 4 * C, "cols": 6, "order8": E0, "bo0": C}
PACK_B = {"attn1_w": 4 * C, "b1col": R0, "gate1T": E1, "gbias": E1, "blk": H1, "below": NG * NG, "bo1": C}


def xattn_moe_kernel(nc, a, out):
    with ExitStack() as ctx:
        def sb(name, shape, dt=F32):
            return ctx.enter_context(nc.sbuf_tensor(name, shape, dt))

        def sem(name):
            return ctx.enter_context(nc.semaphore(name))

        bank = [ctx.enter_context(nc.psum_tensor(f"bank{i}", [P, 512], F32)) for i in range(8)]

        x = sb("x", [P, NT, C])
        pack_a = sb("pack_a", [P, sum(PACK_A.values())])
        pack_b = sb("pack_b", [P, sum(PACK_B.values())])

        def part(buf, widths, name):
            at = 0
            for n, w in widths.items():
                if n == name:
                    return buf[:, at:at + w]
                at += w

        ident = part(pack_a, PACK_A, "ident")
        ctxT = part(pack_a, PACK_A, "ctxT")
        attn0_w = part(pack_a, PACK_A, "attn0_w").rearrange("p (w c) -> p w c", w=4)
        cols = part(pack_a, PACK_A, "cols")
        order8 = part(pack_a, PACK_A, "order8")
        bo0 = part(pack_a, PACK_A, "bo0")
        attn1_w = part(pack_b, PACK_B, "attn1_w").rearrange("p (w c) -> p w c", w=4)
        b1col = part(pack_b, PACK_B, "b1col")
        gate1T = part(pack_b, PACK_B, "gate1T")
        gbias = part(pack_b, PACK_B, "gbias")
        blk = part(pack_b, PACK_B, "blk")
        below = part(pack_b, PACK_B, "below").rearrange("p (g h) -> p g h", g=NG)
        bo1 = part(pack_b, PACK_B, "bo1")
        rows16 = sb("rows16", [G0, C + G0 + C])
        w_redT = rows16[:, 0:C]
        wg_sb = rows16[0:E0, C:C + G0]
        b2_sb = rows16[:, C + G0:]
        mask8 = sb("mask8", [P, B * KV], U8)
        wf = sb("wf", [C, 2 * (R1 * P + I1)])
        w1f = wf[:, 0:R0 * P]
        gu1f = wf[:, :].rearrange("p (w n) -> p w n", w=2)
        w2_0 = sb("w2_0", [P, R0, C])
        w2_1 = sb("w2_1", [P, R1, C])
        ws2 = sb("ws2", [I1, C])

        w1h = sb("w1h", [C, R0 * P], F32R)
        w1l = sb("w1l", [C, R0 * P], F32R)
        gu1h = sb("gu1h", [C, 2, R1 * P + I1], F32R)
        gu1l = sb("gu1l", [C, 2, R1 * P + I1], F32R)
        sel0 = sb("sel0", [2 * E0, E0, P], F32R)
        sel1 = sb("sel1", [P, R1, P], F32R)
        xTh = sb("xTh", [C, NT * P], F32R)
        xTl = sb("xTl", [C, NT * P], F32R)
        gT = sb("gT", [P, NT * P], F32R)
        gTs = sb("gTs", [2 * E0, CH])

        kT0 = sb("kT0", [C, B * KV])
        vT0 = sb("vT0", [C, B * KV])
        A0 = sb("A0", [C, B * KV])
        bqrep = sb("bqrep", [P, C])
        s0bias = sb("s0bias", [P, B * KV])
        V0 = sb("V0", [KV, B, C])
        kT1 = sb("kT1", [C, B * KV])
        vT1 = sb("vT1", [C, B * KV])
        Kblk = sb("Kblk", [C, B, H1, KV])
        V1 = sb("V1", [P, B, 4, C])
        maskrow = sb("maskrow", [P, B, H1, KV], BF16)
        onesb = sb("onesb", [P, P], BF16)
        ones = sb("ones", [P, P])
        bq1s = sb("bq1s", [P, 1])
        bo16 = sb("bo16", [P, C])
        wgsq = sb("wgsq", [E0, G0])
        wgss = sb("wgss", [E0, 1])
        wginv = sb("wginv", [E0, 1])
        wgn = sb("wgn", [E0, G0])
        wgnT = sb("wgnT", [G0, E0])
        R0w = sb("R0w", [C, P])
        R1w = sb("R1w", [C, P])
        mhalf = sb("mhalf", [P, NT])

        st = sb("st", [P, 2, TPB, 6])
        mv = sb("mv", [P, 2, TPB, 2])
        ve = sb("ve", [P, 2, TPB])
        rstd = sb("rstd", [P, 2, TPB])
        xn = sb("xn", [P, 2, TPB, C])
        xT = sb("xT", [C, 2, CH])
        s0 = sb("s0", [P, TPB, KV])
        m0 = sb("m0", [P, TPB])
        z0 = sb("z0", [P, TPB])
        attn0 = sb("attn0", [P, TPB, KV])
        aT0 = sb("aT0", [KV, CH])
        lg0 = sb("lg0", [P, TPB, E0])
        lt0 = sb("lt0", [P, TPB, E0])
        oh0 = sb("oh0", [P, TPB, E0])
        gate0 = sb("gate0", [P, TPB, 2, E0])
        gateh0 = sb("gateh0", [P, TPB, E0], F32R)
        act = sb("act", [P, 4, 512])
        hm = sb("hm", [P, 4, 512])
        Vblk = hm[:, :, :].rearrange("p b (h k) -> p b h k", h=H1)
        sel1f = act[0:2 * E1, :, :].rearrange("p a n -> p (a n)")[:, 0:R1 * P].rearrange("p (r n) -> p r n", r=R1)
        aT1 = act[:, 0:2, :].rearrange("p a (g n) -> p a g n", g=4)
        qT = act[:, 2:4, :]
        sc1 = sb("sc1", [P, 2, H1, KV])
        at1 = sb("at1", [P, 2, H1, KV])
        an1 = sb("an1", [P, 2, H1, KV])
        sel0f = an1[0:2 * E0, :, :, :].rearrange("p a h k -> p (a h k)").rearrange("p (e n) -> p e n", e=E0)
        mx1 = sb("mx1", [P, 2, H1])
        z1 = sb("z1", [P, 2, H1])
        rz1 = sb("rz1", [P, 2, H1])
        sg = sb("sg", [P, NT, E1])
        sbs = sb("sbs", [P, NT, E1])
        ra, rb, rc, rd = (sb(f"route{i}", [P, NT, E1]) for i in range(4))
        pr = sb("pr", [P, 2, NT * NG, 2])
        gq = sb("gq", [P, 4, NT, NG])
        gs = sb("gs", [P, NT, NG])
        gk = sb("gk", [P, NT, NG])
        thr = sb("thr", [P, NT])
        top8 = sb("top8", [P, NT, 8])
        gate1 = sb("gate1", [P, NT, 2, E1])
        gateh1 = sb("gateh1", [P, NT, E1], F32R)

        class Stages:
            pass

        s = Stages()
        s.ld_a = sem("ld_a")
        s.ld_b = sem("ld_b")
        s.ld_rows = sem("ld_rows")
        s.ld_sel = sem("ld_sel")
        s.ld_mask = sem("ld_mask")
        s.ld_w1 = sem("ld_w1")
        s.ld_w2_0 = sem("ld_w2_0")
        s.ld_gu = sem("ld_gu")
        s.ld_w2_1 = sem("ld_w2_1")
        s.stored = sem("stored")
        s.pool_step = sem("pool_step")
        s.dve_link = sem("dve_link")
        s.item_link = sem("item_link")
        s.dve_const = sem("dve_const")
        s.kv_mm = sem("kv_mm")
        s.kv_ready = sem("kv_ready")
        s.a0_mm = sem("a0_mm")
        s.a0_ready = sem("a0_ready")
        s.bq1_ready = sem("bq1_ready")
        s.v0_mm = sem("v0_mm")
        s.v0_ready = sem("v0_ready")
        s.wgss_ready = sem("wgss_ready")
        s.wginv_ready = sem("wginv_ready")
        s.wgn_ready = sem("wgn_ready")
        s.wgT_mm = sem("wgT_mm")
        s.wgT_ready = sem("wgT_ready")
        s.r0_mm = sem("r0_mm")
        s.r0_ready = sem("r0_ready")
        s.r1_ready = sem("r1_ready")
        s.bo16_ready = sem("bo16_ready")
        s.vblk_ready = sem("vblk_ready")
        s.kblk_ready = sem("kblk_ready")
        s.v1_mm = sem("v1_mm")
        s.v1_copied = sem("v1_copied")
        s.v1_ready = sem("v1_ready")
        s.mask_ready = sem("mask_ready")
        s.w1h_ready = sem("w1h_ready")
        s.w1l_ready = sem("w1l_ready")
        s.guh_ready = sem("guh_ready")
        s.gul_ready = sem("gul_ready")
        s.cleared = sem("cleared")
        s.sel_ready = sem("sel_ready")
        s.s0_mm = sem("s0_mm")
        s.s0_shifted = sem("s0_shifted")
        s.exp0_ready = sem("exp0_ready")
        s.attn0_ready = sem("attn0_ready")
        s.aT0_mm = sem("aT0_mm")
        s.aT0_ready = sem("aT0_ready")
        s.out0_mm = sem("out0_mm")
        s.x1_ready = sem("x1_ready")
        s.lg0_mm = sem("lg0_mm")
        s.lt0_ready = sem("lt0_ready")
        s.ex0_ready = sem("ex0_ready")
        s.gate0_ready = sem("gate0_ready")
        s.gT0_mm = sem("gT0_mm")
        s.gTs_ready = sem("gTs_ready")
        s.gT0_ready = sem("gT0_ready")
        s.b2_mm = sem("b2_mm")
        s.b2_added = sem("b2_added")
        s.h_ready = sem("h_ready")
        s.act_ready = sem("act_ready")
        s.e_ready = sem("e_ready")
        s.hm_ready = sem("hm_ready")
        s.hm_used = sem("hm_used")
        s.o_added = sem("o_added")
        s.q_mm = sem("q_mm")
        s.qT_ready = sem("qT_ready")
        s.s1_mm = sem("s1_mm")
        s.mx1_ready = sem("mx1_ready")
        s.s1_shifted = sem("s1_shifted")
        s.exp1_ready = sem("exp1_ready")
        s.z1_ready = sem("z1_ready")
        s.rz1_ready = sem("rz1_ready")
        s.an1_ready = sem("an1_ready")
        s.t1_mm = sem("t1_mm")
        s.aT1_ready = sem("aT1_ready")
        s.av_mm = sem("av_mm")
        s.x3_ready = sem("x3_ready")
        s.lg1_mm = sem("lg1_mm")
        s.sg_ready = sem("sg_ready")
        s.gate1_ready = sem("gate1_ready")
        s.gT1_mm = sem("gT1_mm")
        s.gT1_ready = sem("gT1_ready")
        s.h_ready1 = sem("h_ready1")
        s.act_ready1 = sem("act_ready1")
        s.prod_ready1 = sem("prod_ready1")
        s.e_ready1 = sem("e_ready1")
        s.hm_ready1 = sem("hm_ready1")
        s.hm_used1 = sem("hm_used1")
        s.o_added1 = sem("o_added1")
        s.ld_x = [sem(f"ld_x{b}") for b in range(B)]
        s.ln_stats = [sem(f"ln_stats{k}") for k in range(4)]
        s.ln_var = [sem(f"ln_var{k}") for k in range(4)]
        s.ln_eps = [sem(f"ln_eps{k}") for k in range(4)]
        s.ln_rstd = [sem(f"ln_rstd{k}") for k in range(4)]
        s.xn_ready = [sem(f"xn_ready{k}") for k in range(4)]
        s.tr_ready = [sem(f"tr_ready{k}") for k in range(4)]
        s.xT_ready = [sem(f"xT_ready{k}") for k in range(4)]
        s.xTh_ready = [sem(f"xTh_ready{k}") for k in range(4)]
        s.xTl_ready = [sem(f"xTl_ready{k}") for k in range(4)]
        x_dram = a["x"].rearrange("b (p j) c -> b p j c", p=P)
        out_dram = out.rearrange("b (p j) c -> b p j c", p=P)
        block = ctx.enter_context(nc.Block())

        def tiles(buf, b):
            return buf[:, bass.ds(b * TPB, TPB)]

        def chunk(buf, b):
            return buf[:, bass.ds(b * CH, CH)]

        def cut(buf, r):
            return buf[:, r * P:(r + 1) * P]

        def quarters(n):
            return bank[n][:, :].rearrange("p (j c) -> p j c", j=TPB)

        def over(col, width):
            return col.unsqueeze(2).broadcast_to([P, col.shape[1], width])

        def rows_of(row, n):
            return row.unsqueeze(1).broadcast_to([P, n, row.shape[1]])

        def side(r, last_chunk):
            return [r - 1] if 1 <= r <= len(ITEMS) and not last_chunk else []

        def starts(i, first):
            b, off = divmod(i - first, TPB)
            return [b] if off == 0 and 0 <= b < B else []

        QUERY, LN3, ADD, LN4, T4, LG4 = -1, -2, 7, 8, 9, 10
        LATE = {0: "add", 1: "norm", 2: "transpose", 3: "logits", 4: "scores", 5: "groups", 6: "pick", 7: "gates", 9: "turn"}
        REST = range(1, B)

        @block.sync
        def _(sp):
            sp.dma_start(tiles(x, 0), x_dram[0]).then_inc(s.ld_x[0], 16)
            sp.dma_start(pack_a[:, :], a["pack_a"]).then_inc(s.ld_a, 16)
            sp.dma_start(pack_b[:, :], a["pack_b"]).then_inc(s.ld_b, 16)
            for b in range(1, B):
                sp.dma_start(tiles(x, b), x_dram[b]).then_inc(s.ld_x[b], 16)
            sp.dma_start(w2_0[:, :, :], a["w2_0"]).then_inc(s.ld_w2_0, 16)
            sp.dma_start(w2_1[:, :, :], a["w2_1"]).then_inc(s.ld_w2_1, 16)
            sp.dma_start(ws2[:, :], a["ws2"]).then_inc(s.ld_w2_1, 16)
            sp.wait_ge(s.w1l_ready, 4)
            sp.dma_start(gu1f, a["gu1"]).then_inc(s.ld_gu, 16)
            for b in range(B):
                sp.wait_ge(s.o_added1, b + 1)
                sp.dma_start(out_dram[b], tiles(x, b)).then_inc(s.stored, 16)
            sp.wait_ge(s.stored, 16 * B)

        @block.scalar
        def _(act_e):
            act_e.dma_start(rows16[:, :], a["rows16"]).then_inc(s.ld_rows, 16)
            act_e.dma_start(w1f, a["w1"]).then_inc(s.ld_w1, 16)
            act_e.dma_start(sel0f, a["sel0"]).then_inc(s.ld_sel, 16)
            act_e.dma_start(sel1f, a["sel1"]).then_inc(s.ld_sel, 16)
            act_e.dma_start(mask8[:, :], a["mask"].broadcast_to([P, B * KV])).then_inc(s.ld_mask, 16)

            def copy_xT(k, b, n):
                act_e.wait_ge(s.tr_ready[k], b + 1)
                nc.scalar.copy(xT[:, k % 2, :], bank[n][:, :]).then_inc(s.xT_ready[k], 1)

            def round_xT(k, b):
                act_e.wait_ge(s.xT_ready[k], b + 1)
                nc.scalar.copy(chunk(xTh, b), xT[:, k % 2, :]).then_inc(s.xTh_ready[k], 1)

            def item(n, b):
                if n == XT:
                    copy_xT(0, b, 5)
                elif n == SCORES:
                    act_e.wait_ge(s.s0_shifted, b + 1)
                    nc.scalar.activation(s0[:, :, :], s0[:, :, :], ACT.Exp).then_inc(s.exp0_ready, 1)
                elif n == ATTN_T:
                    act_e.wait_ge(s.aT0_mm, b + 1)
                    nc.scalar.copy(aT0[:, :], bank[7][0:KV, :]).then_inc(s.aT0_ready, 1)
                elif n == XT2:
                    copy_xT(1, b, 6)
                    round_xT(1, b)
                elif n == LOGITS:
                    act_e.wait_ge(s.lt0_ready, b + 1)
                    nc.scalar.activation(lt0[:, :, :], lt0[:, :, :], ACT.Exp).then_inc(s.ex0_ready, 1)
                elif n == GATES_T:
                    act_e.wait_ge(s.gT0_mm, b + 1)
                    nc.scalar.copy(gTs[:, :], bank[5][0:2 * E0, :]).then_inc(s.gTs_ready, 1)
                    act_e.wait_ge(s.gTs_ready, b + 1)
                    nc.scalar.copy(chunk(gT, b)[0:2 * E0], gTs[:, :]).then_inc(s.gT0_ready, 1)

            act_e.wait_ge(s.ld_a, 16)
            for n, (dst, col) in enumerate(((kT0, 0), (vT0, 2), (kT1, 3), (vT1, 5))):
                act_e.wait_ge(s.kv_mm, n + 1)
                nc.scalar.activation(dst[:, :], bank[n][:, 0:P], ACT.Identity, bias=cols[:, col:col + 1]).then_inc(s.kv_ready, 1)
                if n == 0:
                    copy_xT(0, 0, 5)
                    act_e.wait_ge(s.a0_mm, 1)
                    nc.scalar.activation(A0[:, :], bank[4][:, 0:P], ACT.Copy, scale=float(C) ** -0.5).then_inc(s.a0_ready, 1)
                    act_e.wait_ge(s.a0_mm, 2)
                    nc.scalar.activation(s0bias[:, :], bank[6][:, 0:P], ACT.Copy, scale=float(C) ** -0.5).then_inc(s.a0_ready, 1)
            nc.scalar.activation(bq1s[:, :], cols[:, 4:5], ACT.Copy, scale=float(D1) ** -0.5).then_inc(s.bq1_ready, 1)
            for n in range(SCORES, len(ITEMS)):
                item(n, 0)
                if n == SCORES:
                    act_e.wait_ge(s.ld_w1, 16)
                    for q in range(2):
                        nc.scalar.copy(w1h[:, q * 512:(q + 1) * 512], w1f[:, q * 512:(q + 1) * 512]).then_inc(s.w1h_ready, 1)
                if n == ATTN_T:
                    for q in range(2, 4):
                        nc.scalar.copy(w1h[:, q * 512:(q + 1) * 512], w1f[:, q * 512:(q + 1) * 512]).then_inc(s.w1h_ready, 1)
                if n == XT2:
                    act_e.wait_ge(s.ld_sel, 32)
                    nc.scalar.copy(sel0[:, :, :], sel0f).then_inc(s.sel_ready, 1)
                    act_e.wait_ge(s.cleared, 2)
                    nc.scalar.copy(sel1[0:2 * E1, :, :], sel1f).then_inc(s.sel_ready, 1)
                if n == LOGITS:
                    for b in range(B):
                        act_e.wait_ge(s.v1_mm, b + 1)
                        nc.scalar.copy(V1[:, b, :, :], quarters(b)).then_inc(s.v1_copied, 1)

            act_e.wait_ge(s.ld_b, 16)

            def experts0(c, last_chunk=False):
                for r in range(R0):
                    act_e.wait_ge(s.h_ready, c * R0 + (r + 1))
                    if r >= 4:
                        act_e.wait_ge(s.hm_ready, c * R0 + (r - 3))
                    nc.scalar.activation(act[:, r % 4, :], bank[r % 2][:, :], ACT.Gelu,
                                         bias=b1col[:, r:r + 1]).then_inc(s.act_ready, 1)
                    for n in side(r, last_chunk):
                        item(n, c + 1)

            for c in range(B - 1):
                experts0(c)
            experts0(B - 1, last_chunk=True)

            def query(b):
                copy_xT(2, b, 6)
                act_e.wait_ge(s.q_mm, b + 1)
                if b >= 2:
                    act_e.wait_ge(s.s1_mm, TPB * (b - 1))
                nc.scalar.activation(qT[:, b % 2, :], bank[7][:, :], ACT.Identity, bias=bq1s[:, :],
                                     scale=float(D1) ** -0.5).then_inc(s.qT_ready, 1)

            def exp1(i):
                act_e.wait_ge(s.s1_shifted, i + 1)
                if i >= 2:
                    act_e.wait_ge(s.an1_ready, i - 1)
                nc.scalar.activation(at1[:, i % 2, :, :], sc1[:, i % 2, :, :], ACT.Exp).then_inc(s.exp1_ready, 1)

            def attn_copy(i):
                act_e.wait_ge(s.t1_mm, i + 1)
                if i >= 2:
                    act_e.wait_ge(s.av_mm, i - 1)
                nc.scalar.copy(aT1[:, i % 2, :, :], quarters(2 + i % 2)).then_inc(s.aT1_ready, 1)

            def logits1(b):
                act_e.wait_ge(s.lg1_mm, b + 1)
                nc.scalar.activation(tiles(sg, b), quarters(7)[:, :, 0:E1], ACT.Exp, scale=-1.0).then_inc(s.sg_ready, 1)

            def round_gu(n):
                w, q = divmod(n, 4)
                act_e.wait_ge(s.ld_gu, 16)
                width = (R1 * P + I1) // 4
                nc.scalar.copy(gu1h[:, w, q * width:(q + 1) * width], gu1f[:, w, q * width:(q + 1) * width]).then_inc(s.guh_ready, 1)

            query(0)
            for i in range(NT + 3):
                if 2 <= i < NT + 2:
                    attn_copy(i - 2)
                for b in starts(i, TPB + QUERY):
                    if b + 1 < B:
                        query(b + 1)
                if i < NT:
                    exp1(i)
                if i % 2 == 0 and i // 2 < 8:
                    round_gu(i // 2)
                for b in starts(i, T4):
                    copy_xT(3, b, 6)
                    round_xT(3, b)
                for b in starts(i, LG4):
                    logits1(b)

            def turn_copy(b, n):
                act_e.wait_ge(s.gT1_mm, b + 1)
                nc.scalar.copy(chunk(gT, b)[0:2 * E1], bank[n][0:2 * E1, :]).then_inc(s.gT1_ready, 1)

            turn_copy(0, 6)

            def experts1(c, first=False):
                for r in range(R1 + 1):
                    m = P if r < R1 else I1
                    act_e.wait_ge(s.h_ready1, c * (R1 + 1) + (r + 1))
                    if r >= 4:
                        act_e.wait_ge(s.hm_ready1, c * (R1 + 1) + (r - 3))
                    nc.scalar.activation(act[0:m, r % 4, :], bank[r % 2][0:m, :], ACT.Silu).then_inc(s.act_ready1, 1)
                    if first and LATE.get(r) == "transpose":
                        copy_xT(3, B - 1, 6)
                        round_xT(3, B - 1)
                    if first and LATE.get(r) == "logits":
                        logits1(B - 1)
                    if first and LATE.get(r) == "turn":
                        for b in REST:
                            turn_copy(b, 6 + (b + 1) % 2)

            experts1(0, first=True)
            with act_e.Fori(1, B) as c:
                experts1(c)

        @block.gpsimd
        def _(pool):
            n_step = [0]

            def step(ins):
                n_step[0] += 1
                ins.then_inc(s.pool_step, 1)
                pool.wait_ge(s.pool_step, n_step[0])

            def rstd_of(k, b):
                pool.wait_ge(s.ln_var[k], b + 1)
                pool.wait_ge(s.pool_step, 1)
                nc.gpsimd.tensor_scalar(ve[:, k % 2, :], mv[:, k % 2, :, 1], EPS, None, ALU.add).then_inc(s.ln_eps[k], 1)
                pool.wait_ge(s.ln_eps[k], b + 1)
                nc.gpsimd.tensor_tensor(rstd[:, k % 2, :], ve[:, k % 2, :], mhalf[:, 0:TPB], ALU.pow).then_inc(s.ln_rstd[k], 1)

            def low_half(k, b):
                pool.wait_ge(s.xTh_ready[k], b + 1)
                nc.gpsimd.tensor_tensor(chunk(xTl, b), xT[:, k % 2, :], chunk(xTh, b).bitcast(F32),
                                        ALU.subtract).then_inc(s.xTl_ready[k], 1)

            def low_w1(q):
                pool.wait_ge(s.w1h_ready, q + 1)
                nc.gpsimd.tensor_tensor(w1l[:, q * 512:(q + 1) * 512], w1f[:, q * 512:(q + 1) * 512],
                                        w1h[:, q * 512:(q + 1) * 512].bitcast(F32), ALU.subtract).then_inc(s.w1l_ready, 1)

            def block_diagonal(src, dst, b, ready):
                nc.gpsimd.tensor_tensor(dst[:, b, :, :], rows_of(src[:, b * KV:(b + 1) * KV], H1),
                                        over(blk, KV), ALU.mult).then_inc(ready, 1)

            step(nc.gpsimd.memset(mhalf[:, :], -0.5))
            step(nc.gpsimd.memset(R0w[:, :], 0.0))
            step(nc.gpsimd.memset(R1w[:, :], 0.0))
            rstd_of(0, 0)
            nc.gpsimd.memset(gT[:, :].bitcast(F32), 0.0).then_inc(s.cleared, 1)
            nc.gpsimd.memset(sel1[:, :, :].bitcast(F32), 0.0).then_inc(s.cleared, 1)
            pool.wait_ge(s.wgss_ready, 1)
            step(nc.gpsimd.tensor_scalar(wgss[:, :], wgss[:, :], 1e-8, None, ALU.max))
            nc.gpsimd.tensor_tensor(wginv[:, :], wgss[:, :], mhalf[0:E0, 0:1], ALU.pow).then_inc(s.wginv_ready, 1)
            pool.wait_ge(s.ld_b, 16)
            pool.wait_ge(s.kv_ready, 4)
            for b in range(B):
                block_diagonal(vT1, Vblk, b, s.vblk_ready)
            rstd_of(1, 0)
            low_w1(0)
            low_half(1, 0)
            for q in range(1, 4):
                low_w1(q)
            nc.gpsimd.tensor_copy(R1w[:, 0:E1], gate1T).then_inc(s.r1_ready, 1)
            nc.gpsimd.tensor_scalar(bo16[:, :], bo1, 1.0 / H1, None, ALU.mult).then_inc(s.bo16_ready, 1)
            pool.wait_ge(s.bo16_ready, 1)
            for b in range(B):
                pool.wait_ge(s.v1_copied, b + 1)
                nc.gpsimd.tensor_tensor(V1[:, b, :, :], V1[:, b, :, :],
                                        bo16[:, :].unsqueeze(1).broadcast_to([P, 4, C]), ALU.add).then_inc(s.v1_ready, 1)
                block_diagonal(kT1, Kblk, b, s.kblk_ready)
            for b in range(1, B):
                rstd_of(0, b)
                rstd_of(1, b)
                low_half(1, b)
            pool.wait_ge(s.ld_mask, 16)
            for b in range(B):
                nc.gpsimd.tensor_scalar(maskrow[:, b, :, :], rows_of(mask8[:, b * KV:(b + 1) * KV], H1), -BIG / P, None,
                                        ALU.mult).then_inc(s.mask_ready, 1)

            rstd_of(2, 0)
            for i in range(NT + 3):
                if 1 <= i <= NT:
                    t = i - 1
                    pool.wait_ge(s.rz1_ready, t + 1)
                    if t >= 2:
                        pool.wait_ge(s.t1_mm, t - 1)
                    nc.gpsimd.tensor_tensor(an1[:, t % 2, :, :], at1[:, t % 2, :, :], over(rz1[:, t % 2, :], KV),
                                            ALU.mult).then_inc(s.an1_ready, 1)
                for b in starts(i, TPB + LN3):
                    if b + 1 < B:
                        rstd_of(2, b + 1)
                for b in starts(i, LN4):
                    rstd_of(3, b)
                for b in starts(i, T4):
                    low_half(3, b)
                if i % 2 == 0 and i // 2 < 8:
                    n = i // 2
                    w, q = divmod(n, 4)
                    width = (R1 * P + I1) // 4
                    own = slice(q * width, (q + 1) * width)
                    pool.wait_ge(s.guh_ready, n + 1)
                    nc.gpsimd.tensor_tensor(gu1l[:, w, own], gu1f[:, w, own], gu1h[:, w, own].bitcast(F32),
                                            ALU.subtract).then_inc(s.gul_ready, 1)
            rstd_of(3, B - 1)
            low_half(3, B - 1)

        @block.vector
        def _(v):
            n_link = [0]

            def step(ins):
                n_link[0] += 1
                ins.then_inc(s.dve_link, 1)
                v.wait_ge(s.dve_link, n_link[0])

            def statistics(k, b):
                xc = tiles(x, b)
                for j in range(TPB):
                    last = nc.vector.bn_stats(st[:, k % 2, j, :], xc[:, j, :])
                last.then_inc(s.ln_stats[k], 1)
                v.wait_ge(s.ln_stats[k], b + 1)
                for j in range(TPB):
                    last = nc.vector.bn_aggr(mv[:, k % 2, j, :], st[:, k % 2, j, :])
                last.then_inc(s.ln_var[k], 1)

            def normalise(k, b):
                xc = tiles(x, b)
                v.wait_ge(s.ln_rstd[k], b + 1)
                for j in range(TPB):
                    last = nc.vector.tensor_scalar(xn[:, k % 2, j, :], xc[:, j, :], mv[:, k % 2, j, 0:1],
                                                   rstd[:, k % 2, j:j + 1], ALU.subtract, ALU.mult)
                last.then_inc(s.xn_ready[k], 1)

            def add_to_x(b, n, ready, signal):
                v.wait_ge(ready, b + 1)
                nc.vector.tensor_tensor(tiles(x, b), tiles(x, b), quarters(n), ALU.add).then_inc(signal, 1)
                v.wait_ge(signal, b + 1)

            n_item = [0]

            def item_step(b, ins):
                n_item[0] += 1
                ins.then_inc(s.item_link, 1)
                v.wait_ge(s.item_link, b * LINKS0 + n_item[0])

            def item(n, b):
                if n == STATS:
                    n_item[0] = 0
                    statistics(0, b)
                elif n == NORM:
                    normalise(0, b)
                elif n == SCORES:
                    v.wait_ge(s.s0_mm, b + 1)
                    own = bass.ds(b * KV, KV)
                    item_step(b, nc.vector.tensor_tensor(s0[:, :, :], quarters(6)[:, :, own],
                                                         rows_of(s0bias[:, own], TPB), ALU.add))
                    item_step(b, nc.vector.tensor_reduce(m0[:, :], s0[:, :, :], AX, ALU.max))
                    nc.vector.tensor_tensor(s0[:, :, :], s0[:, :, :], over(m0[:, :], KV), ALU.subtract).then_inc(s.s0_shifted, 1)
                elif n == SOFTMAX:
                    v.wait_ge(s.exp0_ready, b + 1)
                    item_step(b, nc.vector.tensor_reduce(z0[:, :], s0[:, :, :], AX, ALU.add))
                    item_step(b, nc.vector.reciprocal(z0[:, :], z0[:, :]))
                    nc.vector.tensor_tensor(attn0[:, :, :], s0[:, :, :], over(z0[:, :], KV), ALU.mult).then_inc(s.attn0_ready, 1)
                elif n == OUT:
                    add_to_x(b, 5, s.out0_mm, s.x1_ready)
                    statistics(1, b)
                elif n == NORM2:
                    normalise(1, b)
                elif n == LOGITS:
                    v.wait_ge(s.lg0_mm, b + 1)
                    item_step(b, nc.vector.tensor_copy(lg0[:, :, :], quarters(7)[:, :, 0:E0]))
                    item_step(b, nc.vector.tensor_reduce(m0[:, :], lg0[:, :, :], AX, ALU.max))
                    nc.vector.tensor_tensor(lt0[:, :, :], lg0[:, :, :], over(m0[:, :], E0), ALU.subtract).then_inc(s.lt0_ready, 1)
                elif n == GATES:
                    item_step(b, nc.vector.tensor_tensor(oh0[:, :, :], lg0[:, :, :], over(m0[:, :], E0), ALU.is_equal))
                    item_step(b, nc.vector.tensor_tensor(oh0[:, :, :], oh0[:, :, :], rows_of(order8, TPB), ALU.mult))
                    item_step(b, nc.vector.tensor_reduce(m0[:, :], oh0[:, :, :], AX, ALU.max))
                    item_step(b, nc.vector.tensor_tensor(oh0[:, :, :], oh0[:, :, :], over(m0[:, :], E0), ALU.is_equal))
                    v.wait_ge(s.ex0_ready, b + 1)
                    item_step(b, nc.vector.tensor_reduce(z0[:, :], lt0[:, :, :], AX, ALU.add))
                    item_step(b, nc.vector.reciprocal(z0[:, :], z0[:, :]))
                    item_step(b, nc.vector.tensor_tensor(oh0[:, :, :], oh0[:, :, :], over(z0[:, :], E0), ALU.mult))
                    item_step(b, nc.vector.tensor_copy(gateh0[:, :, :], oh0[:, :, :]))
                    nc.vector.tensor_copy(gate0[:, :, 0, :], gateh0[:, :, :].bitcast(F32))
                    nc.vector.tensor_tensor(gate0[:, :, 1, :], oh0[:, :, :], gateh0[:, :, :].bitcast(F32),
                                            ALU.subtract).then_inc(s.gate0_ready, 1)
                    assert n_item[0] == LINKS0
                elif n == BIAS2:
                    add_to_x(b, 6, s.b2_mm, s.b2_added)

            nc.vector.memset(onesb[:, :], 1.0).then_inc(s.dve_const, 1)
            step(nc.vector.memset(ones[:, :], 1.0))
            v.wait_ge(s.ld_x[0], 16)
            item(STATS, 0)
            v.wait_ge(s.ld_a, 16)
            nc.vector.tensor_scalar(bqrep[:, :], ones[:, :], cols[:, 1:2], None, ALU.mult).then_inc(s.dve_const, 1)
            item(NORM, 0)
            v.wait_ge(s.ld_rows, 16)
            step(nc.vector.tensor_tensor(wgsq[:, :], wg_sb, wg_sb, ALU.mult))
            nc.vector.tensor_reduce(wgss[:, :], wgsq[:, :], AX, ALU.add).then_inc(s.wgss_ready, 1)
            v.wait_ge(s.a0_ready, 2)
            item(SCORES, 0)
            v.wait_ge(s.wginv_ready, 1)
            nc.vector.tensor_scalar(wgn[:, :], wg_sb, wginv[:, 0:1], None, ALU.mult).then_inc(s.wgn_ready, 1)
            v.wait_ge(s.v0_mm, 1)
            nc.vector.tensor_tensor(V0[:, :, :], quarters(4)[0:KV], bo0[0:KV].unsqueeze(1).broadcast_to([KV, B, C]),
                                    ALU.add).then_inc(s.v0_ready, 1)
            item(SOFTMAX, 0)
            v.wait_ge(s.wgT_mm, 1)
            nc.vector.tensor_copy(wgnT[:, :], bank[4][0:G0, 0:E0]).then_inc(s.wgT_ready, 1)
            v.wait_ge(s.r0_mm, 1)
            v.wait_ge(s.ln_rstd[0], 1)
            nc.vector.tensor_copy(R0w[:, 0:E0], bank[4][:, P:P + E0]).then_inc(s.r0_ready, 1)
            for n in range(OUT, len(ITEMS)):
                item(n, 0)
            for b in range(1, B):
                v.wait_ge(s.ld_x[b], 16)

            def experts0(c, last_chunk=False):
                for r in range(R0):
                    v.wait_ge(s.act_ready, c * R0 + (r + 1))
                    v.wait_ge(s.e_ready, c * E0 + (r // 2 + 1))
                    if r >= 4:
                        v.wait_ge(s.hm_used, c * R0 + (r - 3))
                    nc.vector.tensor_tensor(hm[:, r % 4, :], act[:, r % 4, :], bank[2 + r // 2 % 2][:, :],
                                            ALU.mult).then_inc(s.hm_ready, 1)
                    for n in side(r, last_chunk):
                        item(n, c + 1)
                v.wait_ge(s.hm_used, c * R0 + R0)
                nc.vector.tensor_tensor(tiles(x, c), tiles(x, c), quarters(4), ALU.add).then_inc(s.o_added, 1)

            for c in range(B - 1):
                experts0(c)
            v.wait_ge(s.o_added, B - 1)
            statistics(2, 0)
            experts0(B - 1, last_chunk=True)
            v.wait_ge(s.o_added, B)
            normalise(2, 0)

            def shift(i):
                v.wait_ge(s.s1_mm, i + 1)
                scores = bank[i % 2][:, :].rearrange("p (h k) -> p h k", h=H1)
                nc.vector.tensor_reduce(mx1[:, i % 2, :], scores, AX, ALU.max).then_inc(s.mx1_ready, 1)
                v.wait_ge(s.mx1_ready, i + 1)
                if i >= 2:
                    v.wait_ge(s.exp1_ready, i - 1)
                nc.vector.tensor_tensor(sc1[:, i % 2, :, :], scores, over(mx1[:, i % 2, :], KV),
                                        ALU.subtract).then_inc(s.s1_shifted, 1)

            def total(i):
                v.wait_ge(s.exp1_ready, i + 1)
                nc.vector.tensor_reduce(z1[:, i % 2, :], at1[:, i % 2, :, :], AX, ALU.add).then_inc(s.z1_ready, 1)
                v.wait_ge(s.z1_ready, i + 1)
                nc.vector.reciprocal(rz1[:, i % 2, :], z1[:, i % 2, :]).then_inc(s.rz1_ready, 1)

            def add_attention(b):
                v.wait_ge(s.av_mm, TPB * (b + 1))
                nc.vector.tensor_tensor(tiles(x, b), tiles(x, b), quarters(4 + b % 2), ALU.add).then_inc(s.x3_ready, 1)
                v.wait_ge(s.x3_ready, b + 1)

            def route_scores(t0, t1):
                t, n = slice(t0, t1), t1 - t0
                step(nc.vector.tensor_scalar(sg[:, t, :], sg[:, t, :], 1.0, None, ALU.add))
                step(nc.vector.reciprocal(sg[:, t, :], sg[:, t, :]))
                step(nc.vector.tensor_tensor(sbs[:, t, :], sg[:, t, :], rows_of(gbias, n), ALU.add))
                pairs = sbs[:, t, :].rearrange("p t (g u w) -> p (t g u) w", g=NG, w=2)
                pr_t = pr[:, :, t0 * NG:t1 * NG, :]
                nc.vector.tensor_tensor(pr_t[:, 0, :, :].rearrange("p n u -> p (n u)"), pairs[:, :, 0], pairs[:, :, 1], ALU.max)
                step(nc.vector.tensor_tensor(pr_t[:, 1, :, :].rearrange("p n u -> p (n u)"), pairs[:, :, 0], pairs[:, :, 1],
                                             ALU.min))
                g4 = [gq[:, i, t, :].rearrange("p t g -> p (t g)") for i in range(4)]
                nc.vector.tensor_tensor(g4[0], pr_t[:, 0, :, 0], pr_t[:, 0, :, 1], ALU.max)
                nc.vector.tensor_tensor(g4[1], pr_t[:, 0, :, 0], pr_t[:, 0, :, 1], ALU.min)
                step(nc.vector.tensor_tensor(g4[2], pr_t[:, 1, :, 0], pr_t[:, 1, :, 1], ALU.max))
                step(nc.vector.tensor_tensor(g4[3], g4[1], g4[2], ALU.max))
                step(nc.vector.tensor_tensor(gs[:, t, :].rearrange("p t g -> p (t g)"), g4[0], g4[3], ALU.add))

            def route_groups(t0, t1):
                t, n = slice(t0, t1), t1 - t0
                others = gs[:, t, :].unsqueeze(2).broadcast_to([P, n, NG, NG])
                own = gs[:, t, :].unsqueeze(3).broadcast_to([P, n, NG, NG])
                above, equal = (z[:, t, :].rearrange("p t (g h) -> p t g h", g=NG) for z in (ra, rb))
                nc.vector.tensor_tensor(above, others, own, ALU.is_gt)
                step(nc.vector.tensor_tensor(equal, others, own, ALU.is_equal))
                step(nc.vector.tensor_tensor(equal, equal, below.unsqueeze(1).broadcast_to([P, n, NG, NG]), ALU.mult))
                step(nc.vector.tensor_tensor(above, above, equal, ALU.add))
                step(nc.vector.tensor_reduce(gk[:, t, :], above, AX, ALU.add))
                step(nc.vector.tensor_scalar(gk[:, t, :], gk[:, t, :], float(TOPG), -BIG, ALU.is_ge, ALU.mult))
                step(nc.vector.tensor_tensor(rc[:, t, :].rearrange("p t (g w) -> p t g w", g=NG),
                                             sbs[:, t, :].rearrange("p t (g w) -> p t g w", g=NG),
                                             gk[:, t, :].unsqueeze(3).broadcast_to([P, n, NG, NG]), ALU.add))

            def route_pick(t0, t1):
                t = slice(t0, t1)
                for tt in range(t0, t1):
                    last = nc.vector.max(top8[:, tt, :], rc[:, tt, :])
                step(last)
                fourth = top8[:, t, TOPK - 1:TOPK].broadcast_to([P, t1 - t0, E1])
                nc.vector.tensor_tensor(ra[:, t, :], rc[:, t, :], fourth, ALU.is_gt)
                step(nc.vector.tensor_tensor(rb[:, t, :], rc[:, t, :], fourth, ALU.is_equal))
                step(nc.vector.tensor_reduce(thr[:, t], ra[:, t, :], AX, ALU.add))
                step(nc.vector.tensor_scalar(thr[:, t], thr[:, t], -1.0, float(TOPK), ALU.mult, ALU.add))
                src, dst = rb, rc
                for by in (1, 2, 4, 8):
                    nc.vector.tensor_copy(dst[:, t, 0:by], src[:, t, 0:by])
                    step(nc.vector.tensor_tensor(dst[:, t, by:], src[:, t, by:], src[:, t, 0:E1 - by], ALU.add))
                    src, dst = dst, (rd if dst is rc else rc)
                step(nc.vector.tensor_tensor(src[:, t, :], src[:, t, :], over(thr[:, t], E1), ALU.is_le))
                step(nc.vector.tensor_tensor(rb[:, t, :], rb[:, t, :], src[:, t, :], ALU.mult))
                step(nc.vector.tensor_tensor(ra[:, t, :], ra[:, t, :], rb[:, t, :], ALU.add))

            def route_gates(t0, t1):
                t = slice(t0, t1)
                step(nc.vector.tensor_tensor(ra[:, t, :], ra[:, t, :], sg[:, t, :], ALU.mult))
                step(nc.vector.tensor_reduce(thr[:, t], ra[:, t, :], AX, ALU.add))
                step(nc.vector.tensor_scalar(thr[:, t], thr[:, t], 1e-20, None, ALU.add))
                step(nc.vector.reciprocal(thr[:, t], thr[:, t]))
                step(nc.vector.tensor_scalar(thr[:, t], thr[:, t], SCALE, None, ALU.mult))
                step(nc.vector.tensor_tensor(ra[:, t, :], ra[:, t, :], over(thr[:, t], E1), ALU.mult))
                step(nc.vector.tensor_copy(gateh1[:, t, :], ra[:, t, :]))
                nc.vector.tensor_copy(gate1[:, t, 0, :], gateh1[:, t, :].bitcast(F32))
                nc.vector.tensor_tensor(gate1[:, t, 1, :], ra[:, t, :], gateh1[:, t, :].bitcast(F32),
                                        ALU.subtract).then_inc(s.gate1_ready, 1)

            for i in range(NT + 3):
                if i < NT:
                    shift(i)
                for b in starts(i, TPB + LN3):
                    if b + 1 < B:
                        statistics(2, b + 1)
                if 1 <= i <= NT:
                    total(i - 1)
                for b in starts(i, TPB + LN3):
                    if b + 1 < B:
                        normalise(2, b + 1)
                for b in starts(i, ADD):
                    add_attention(b)
                for b in starts(i, LN4):
                    statistics(3, b)
                    normalise(3, b)
                if i == LG4 + 1:
                    v.wait_ge(s.sg_ready, 1)
                    route_scores(0, TPB)
                if i == LG4 + 2:
                    route_groups(0, TPB)
                if i == LG4 + 3:
                    route_pick(0, TPB)
                if i == LG4 + 4:
                    route_gates(0, TPB)

            def experts1(c, first=False):
                for r in range(R1 + 1):
                    m = P if r < R1 else I1
                    v.wait_ge(s.act_ready1, c * (R1 + 1) + (r + 1))
                    if r >= 4:
                        v.wait_ge(s.hm_used1, c * (R1 + 1) + (r - 3))
                    if r < R1:
                        nc.vector.tensor_tensor(act[:, r % 4, :], act[:, r % 4, :], bank[2 + r % 2][:, :],
                                                ALU.mult).then_inc(s.prod_ready1, 1)
                        v.wait_ge(s.prod_ready1, c * R1 + (r + 1))
                        v.wait_ge(s.e_ready1, c * R1 + (r + 1))
                        nc.vector.tensor_tensor(hm[:, r % 4, :], act[:, r % 4, :], bank[5][:, :],
                                                ALU.mult).then_inc(s.hm_ready1, 1)
                    else:
                        nc.vector.tensor_tensor(hm[0:m, r % 4, :], act[0:m, r % 4, :], bank[2 + r % 2][0:m, :],
                                                ALU.mult).then_inc(s.hm_ready1, 1)
                    late = LATE.get(r) if first else None
                    if late == "add":
                        statistics(3, B - 1)
                    elif late == "norm":
                        normalise(3, B - 1)
                    elif late == "scores":
                        v.wait_ge(s.sg_ready, B)
                        route_scores(TPB, NT)
                    elif late == "groups":
                        route_groups(TPB, NT)
                    elif late == "pick":
                        route_pick(TPB, NT)
                    elif late == "gates":
                        route_gates(TPB, NT)
                v.wait_ge(s.hm_used1, c * (R1 + 1) + (R1 + 1))
                nc.vector.tensor_tensor(tiles(x, c), tiles(x, c), quarters(4), ALU.add).then_inc(s.o_added1, 1)

            add_attention(B - 1)
            experts1(0, first=True)
            with v.Fori(1, B) as c:
                experts1(c)

        @block.tensor
        def _(pe):
            def mm(dst, lhsT, rhs, start=True, stop=True):
                return nc.tensor.matmul(dst, lhsT, rhs, start=start, stop=stop, skip_group_check=True)

            def split_mm(dst, wh, wl, xh, xl):
                mm(dst, wh, xh, start=True, stop=False)
                mm(dst, wh, xl, start=False, stop=False)
                return mm(dst, wl, xh, start=False, stop=True)

            def transposes(k, b, n):
                pe.wait_ge(s.xn_ready[k], b + 1)
                for j in range(TPB):
                    last = nc.tensor.transpose(quarters(n)[:, j, :], xn[:, k % 2, j, :], ident)
                last.then_inc(s.tr_ready[k], 1)

            def item(n, b):
                if n == XT:
                    transposes(0, b, 5)
                elif n == SCORES:
                    pe.wait_ge(s.xT_ready[0], b + 1)
                    for j in range(TPB):
                        last = mm(quarters(6)[:, j, :], cut(xT[:, 0, :], j), A0[:, :])
                    last.then_inc(s.s0_mm, 1)
                elif n == ATTN_T:
                    pe.wait_ge(s.attn0_ready, b + 1)
                    for j in range(TPB):
                        last = nc.tensor.transpose(quarters(7)[0:KV, j, :], attn0[:, j, :], ident)
                    last.then_inc(s.aT0_mm, 1)
                elif n == OUT:
                    pe.wait_ge(s.aT0_ready, b + 1)
                    for j in range(TPB):
                        mm(quarters(5)[:, j, :], cut(xT[:, 0, :], j), attn0_w[:, 3, :], stop=False)
                        last = mm(quarters(5)[:, j, :], cut(aT0, j), V0[:, bass.ds(b, 1), :].rearrange("p o c -> p (o c)"),
                                  start=False)
                    last.then_inc(s.out0_mm, 1)
                elif n == XT2:
                    transposes(1, b, 6)
                elif n == LOGITS:
                    pe.wait_ge(s.xT_ready[1], b + 1)
                    for j in range(TPB):
                        last = mm(quarters(7)[:, j, :], cut(xT[:, 1, :], j), R0w[:, :])
                    last.then_inc(s.lg0_mm, 1)
                elif n == GATES_T:
                    pe.wait_ge(s.gate0_ready, b + 1)
                    for j in range(TPB):
                        last = nc.tensor.transpose(quarters(5)[0:2 * E0, j, :], gate0[:, j, :, :].rearrange("p u e -> p (u e)"),
                                                   ident)
                    last.then_inc(s.gT0_mm, 1)
                elif n == BIAS2:
                    pe.wait_ge(s.gTs_ready, b + 1)
                    for j in range(TPB):
                        last = mm(quarters(6)[:, j, :], cut(gTs, j), b2_sb)
                    last.then_inc(s.b2_mm, 1)

            def values1(b):
                pe.wait_ge(s.vblk_ready, b + 1)
                for g in range(4):
                    last = mm(quarters(b)[:, g, :], Vblk[:, b, 4 * g:4 * g + 4, :], attn1_w[:, 3, :])
                last.then_inc(s.v1_mm, 1)

            pe.wait_ge(s.ld_a, 16)
            mm(bank[0][:, 0:P], attn0_w[:, 0, :], ctxT).then_inc(s.kv_mm, 1)
            item(XT, 0)
            pe.wait_ge(s.kv_ready, 1)
            mm(bank[4][:, 0:P], attn0_w[:, 1, :], kT0[:, :]).then_inc(s.a0_mm, 1)
            pe.wait_ge(s.dve_const, 2)
            mm(bank[6][:, 0:P], bqrep[:, :], kT0[:, :]).then_inc(s.a0_mm, 1)
            mm(bank[1][:, 0:P], attn0_w[:, 2, :], ctxT).then_inc(s.kv_mm, 1)
            pe.wait_ge(s.a0_ready, 2)
            item(SCORES, 0)
            pe.wait_ge(s.ld_b, 16)
            mm(bank[2][:, 0:P], attn1_w[:, 0, :], ctxT).then_inc(s.kv_mm, 1)
            mm(bank[3][:, 0:P], attn1_w[:, 2, :], ctxT).then_inc(s.kv_mm, 1)
            pe.wait_ge(s.kv_ready, 2)
            for b in range(B):
                last = mm(quarters(4)[0:KV, b, :], vT0[:, b * KV:(b + 1) * KV], attn0_w[:, 3, :])
            last.then_inc(s.v0_mm, 1)
            item(ATTN_T, 0)
            pe.wait_ge(s.wgn_ready, 1)
            pe.wait_ge(s.v0_ready, 1)
            nc.tensor.transpose(bank[4][0:G0, 0:E0], wgn[:, :], ident[0:E0, 0:E0]).then_inc(s.wgT_mm, 1)
            item(OUT, 0)
            pe.wait_ge(s.wgT_ready, 1)
            mm(bank[4][:, P:P + E0], w_redT, wgnT[:, :]).then_inc(s.r0_mm, 1)
            pe.wait_ge(s.kv_ready, 4)
            values1(0)
            item(XT2, 0)
            values1(1)
            pe.wait_ge(s.r0_ready, 1)
            item(LOGITS, 0)
            values1(2)
            values1(3)
            item(GATES_T, 0)
            item(BIAS2, 0)

            pe.wait_ge(s.v1_copied, B)
            pe.wait_ge(s.sel_ready, 2)
            pe.wait_ge(s.ld_w2_0, 16)

            def experts0(c, last_chunk=False):
                pe.wait_ge(s.xTl_ready[1], c + 1)
                pe.wait_ge(s.gT0_ready, c + 1)
                for r in range(R0 + LAG):
                    if r < R0:
                        if r % 4 == 0:
                            pe.wait_ge(s.w1l_ready, r // 4 + 1)
                        if r >= 2:
                            pe.wait_ge(s.act_ready, c * R0 + (r - 1))
                        if r >= 4 and r % 2 == 0:
                            pe.wait_ge(s.hm_ready, c * R0 + (r - 2))
                        split_mm(bank[r % 2][:, :], cut(w1h, r), cut(w1l, r), chunk(xTh, c), chunk(xTl, c))\
                            .then_inc(s.h_ready, 1)
                        if r % 2 == 0:
                            mm(bank[2 + r // 2 % 2][:, :], sel0[:, r // 2, :], chunk(gT, c)[0:2 * E0])\
                                .then_inc(s.e_ready, 1)
                    if r >= LAG:
                        q = r - LAG
                        pe.wait_ge(s.hm_ready, c * R0 + (q + 1))
                        for j in range(TPB):
                            last = mm(quarters(4)[:, j, :], hm[:, q % 4, j * P:(j + 1) * P], w2_0[:, q, :],
                                      start=(q == 0 and j == 0), stop=(q == R0 - 1))
                        last.then_inc(s.hm_used, 1)
                    for n in side(r, last_chunk):
                        item(n, c + 1)

            for c in range(B - 1):
                experts0(c)
            experts0(B - 1, last_chunk=True)

            def queries(b):
                if b:
                    pe.wait_ge(s.xT_ready[2], b)
                if b >= 3:
                    pe.wait_ge(s.xT_ready[3], b - 2)
                transposes(2, b, 6)
                pe.wait_ge(s.xT_ready[2], b + 1)
                if b:
                    pe.wait_ge(s.qT_ready, b)
                if b >= 3:
                    pe.wait_ge(s.sg_ready, b - 2)
                mm(bank[7][:, :], attn1_w[:, 1, :], xT[:, 0, :]).then_inc(s.q_mm, 1)

            def scores(i):
                b = i // TPB
                pe.wait_ge(s.qT_ready, b + 1)
                if i >= 2:
                    pe.wait_ge(s.s1_shifted, i - 1)
                mm(bank[i % 2][:, :], qT[:, b % 2, (i % TPB) * P:(i % TPB + 1) * P],
                   Kblk[:, b, :, :].rearrange("p h k -> p (h k)"), stop=False)
                pe.wait_ge(s.mask_ready, b + 1)
                mm(bank[i % 2][:, :], onesb[:, :], maskrow[:, b, :, :].rearrange("p h k -> p (h k)"), start=False)\
                    .then_inc(s.s1_mm, 1)

            def attn_transposes(i):
                pe.wait_ge(s.an1_ready, i + 1)
                if i >= 2:
                    pe.wait_ge(s.aT1_ready, i - 1)
                for g in range(4):
                    last = nc.tensor.transpose(quarters(2 + i % 2)[:, g, :],
                                               an1[:, i % 2, 4 * g:4 * g + 4, :].rearrange("p h k -> p (h k)"), ident)
                last.then_inc(s.t1_mm, 1)

            def attn_values(i):
                b, j = i // TPB, i % TPB
                pe.wait_ge(s.aT1_ready, i + 1)
                if j == 0 and b >= 2:
                    pe.wait_ge(s.x3_ready, b - 1)
                for g in range(4):
                    last = mm(quarters(4 + b % 2)[:, j, :], aT1[:, i % 2, g, :], V1[:, b, g, :],
                              start=(g == 0), stop=(g == 3))
                last.then_inc(s.av_mm, 1)

            def logits1(b):
                pe.wait_ge(s.xT_ready[3], b + 1)
                for j in range(TPB):
                    last = mm(quarters(7)[:, j, :], cut(xT[:, 1, :], j), R1w[:, :])
                last.then_inc(s.lg1_mm, 1)

            def turn_gates(b, n):
                for j in range(TPB):
                    last = nc.tensor.transpose(quarters(n)[0:2 * E1, j, :],
                                               gate1[:, TPB * b + j, :, :].rearrange("p u e -> p (u e)"), ident)
                last.then_inc(s.gT1_mm, 1)

            pe.wait_ge(s.o_added, B)
            pe.wait_ge(s.kblk_ready, B)
            pe.wait_ge(s.v1_ready, B)
            pe.wait_ge(s.r1_ready, 1)
            queries(0)
            for i in range(NT + 3):
                if i < NT:
                    scores(i)
                if 2 <= i < NT + 2:
                    attn_transposes(i - 2)
                if i >= 3:
                    attn_values(i - 3)
                for b in starts(i, TPB + QUERY):
                    if b + 1 < B:
                        queries(b + 1)
                for b in starts(i, T4):
                    if b + 2 < B:
                        pe.wait_ge(s.xT_ready[2], b + 3)
                    transposes(3, b, 6)
                for b in starts(i, LG4):
                    if b + 2 < B:
                        pe.wait_ge(s.qT_ready, b + 3)
                    logits1(b)

            pe.wait_ge(s.gate1_ready, 1)
            turn_gates(0, 6)
            pe.wait_ge(s.x3_ready, B)
            pe.wait_ge(s.gul_ready, 8)
            pe.wait_ge(s.ld_w2_1, 32)

            def experts1(c, first=False):
                base = c * (R1 + 1)
                pe.wait_ge(s.xTl_ready[3], c + 1)
                pe.wait_ge(s.gT1_ready, c + 1)
                for r in range(R1 + 1 + LAG):
                    if r <= R1:
                        m = P if r < R1 else I1
                        rows = slice(r * P, r * P + m)
                        if r >= 2:
                            pe.wait_ge(s.hm_ready1, base + (r - 1))
                        for w in range(2):
                            last = split_mm(bank[2 * w + r % 2][0:m, :], gu1h[:, w, rows], gu1l[:, w, rows],
                                            chunk(xTh, c), chunk(xTl, c))
                        last.then_inc(s.h_ready1, 1)
                    if r >= LAG:
                        q = r - LAG
                        m = P if q < R1 else I1
                        pe.wait_ge(s.hm_ready1, base + (q + 1))
                        for j in range(TPB):
                            last = mm(quarters(4)[:, j, :], hm[0:m, q % 4, j * P:(j + 1) * P],
                                      w2_1[:, q, :] if q < R1 else ws2[:, :],
                                      start=(q == 0 and j == 0), stop=(q == R1))
                        last.then_inc(s.hm_used1, 1)
                    if r < R1:
                        if r >= 1:
                            pe.wait_ge(s.hm_ready1, base + r)
                        mm(bank[5][:, :], sel1[:, r, :], chunk(gT, c)).then_inc(s.e_ready1, 1)
                    late = LATE.get(r) if first else None
                    if late == "transpose":
                        transposes(3, B - 1, 6)
                    elif late == "logits":
                        logits1(B - 1)
                    elif late == "turn":
                        pe.wait_ge(s.gate1_ready, 2)
                        pe.wait_ge(s.sg_ready, B)
                        for b in REST:
                            if b == B - 1:
                                pe.wait_ge(s.gT1_ready, B - 2)
                            turn_gates(b, 6 + (b + 1) % 2)

            experts1(0, first=True)
            with pe.Fori(1, B) as c:
                experts1(c)


def kernel(x, ctx_1024, mask_BxS2_bf0, L0_xattn_Wq, L0_xattn_bq, L0_xattn_Wk, L0_xattn_bk, L0_xattn_Wv, L0_xattn_bv,
           L0_xattn_Wo, L0_xattn_bo, L0_ffn_w_red, L0_ffn_wg, L0_ffn_W1, L0_ffn_b1, L0_ffn_W2, L0_ffn_b2,
           L1_xattn_Wq, L1_xattn_bq, L1_xattn_Wk, L1_xattn_bk, L1_xattn_Wv, L1_xattn_bv, L1_xattn_Wo, L1_xattn_bo,
           L1_ffn_gate_w, L1_ffn_gate_bias, L1_ffn_w1, L1_ffn_w2, L1_ffn_w3, L1_ffn_ws1, L1_ffn_ws2, L1_ffn_ws3):
    import numpy as np
    import concourse.bacc as bacc
    from concourse.bass_utils import run_bass_kernel_spmd

    def up(*parts):
        return np.stack([np.asarray(q) for q in parts], axis=1)

    def rows(v, n=P):
        return np.broadcast_to(np.asarray(v).reshape(1, -1), (n, np.asarray(v).size))

    def pack(widths, parts):
        return np.concatenate([np.asarray(parts[n]).reshape(P, w) for n, w in widths.items()], axis=1)

    parts = {
        "ctxT": np.asarray(ctx_1024).reshape(B * KV, C).T,
        "attn0_w": up(np.asarray(L0_xattn_Wk).T, L0_xattn_Wq, np.asarray(L0_xattn_Wv).T, np.asarray(L0_xattn_Wo).T),
        "attn1_w": up(L1_xattn_Wk, L1_xattn_Wq, L1_xattn_Wv, L1_xattn_Wo),
        "cols": up(L0_xattn_bk, L0_xattn_bq, L0_xattn_bv, L1_xattn_bk, L1_xattn_bq, L1_xattn_bv),
        "b1col": np.asarray(L0_ffn_b1).reshape(R0, P).T,
        "bo0": rows(L0_xattn_bo),
        "bo1": rows(L1_xattn_bo),
        "gate1T": np.asarray(L1_ffn_gate_w).T,
        "gbias": rows(L1_ffn_gate_bias),
        "ident": np.eye(P, dtype=np.float32),
        "blk": np.repeat(np.eye(H1, dtype=np.float32), D1, axis=0),
        "below": rows(np.tril(np.ones((NG, NG), np.float32), -1)),
        "order8": rows(np.arange(E0, 0, -1, dtype=np.float32)),
    }
    wg16 = np.zeros((G0, G0), np.float32)
    wg16[:E0] = np.asarray(L0_ffn_wg)
    arrays = {
        "x": np.asarray(x),
        "pack_a": pack(PACK_A, parts),
        "pack_b": pack(PACK_B, parts),
        "rows16": np.concatenate([np.asarray(L0_ffn_w_red).T, wg16, np.tile(np.asarray(L0_ffn_b2), (2, 1))], axis=1),
        "mask": np.asarray(mask_BxS2_bf0).reshape(1, B * KV),
        "sel0": np.broadcast_to(np.tile(np.eye(E0, dtype=np.float32), (2, 1))[:, :, None], (2 * E0, E0, P)),
        "sel1": np.tile(np.repeat(np.eye(E1, dtype=np.float32), I1, axis=1), (2, 1)).reshape(2 * E1, R1, P),
        "w1": np.asarray(L0_ffn_W1).transpose(1, 0, 2).reshape(C, R0 * P),
        "w2_0": np.asarray(L0_ffn_W2).reshape(R0, P, C).transpose(1, 0, 2),
        "gu1": up(*(np.concatenate([np.asarray(w).reshape(E1 * I1, C), np.asarray(sw)]).T
                    for w, sw in ((L1_ffn_w1, L1_ffn_ws1), (L1_ffn_w3, L1_ffn_ws3)))),
        "w2_1": np.asarray(L1_ffn_w2).transpose(0, 2, 1).reshape(R1, P, C).transpose(1, 0, 2),
        "ws2": np.asarray(L1_ffn_ws2).T,
    }
    arrays = {f"in_{k}": np.ascontiguousarray(v) for k, v in arrays.items()}
    nc = bacc.Bacc("TRN2", target_bir_lowering=False, num_devices=1)
    aps = {k[3:]: nc.dram_tensor(k, v.shape, mybir.dt.from_np(v.dtype), kind="ExternalInput").ap()
           for k, v in arrays.items()}
    out = nc.dram_tensor("out_x", (B, CH, C), F32, kind="ExternalOutput").ap()
    xattn_moe_kernel(nc, aps, out)
    r = run_bass_kernel_spmd(nc, [arrays], core_ids=[0])
    return r.results[0]["out_x"]
```

```python
from contextlib import ExitStack

import concourse.bass as bass
from concourse import mybir

F32 = mybir.dt.float32
F32R = mybir.dt.float32r
BF16 = mybir.dt.bfloat16
U8 = mybir.dt.uint8
ALU = mybir.AluOpType
ACT = mybir.ActivationFunctionType
AX = mybir.AxisListType.X

P = 128
C = 128
B = 4
TPB = 4
NT = B * TPB
CH = TPB * P
KV = 32
H1 = 16
D1 = C // H1
E0 = 8
R0 = 16
G0 = 16
E1 = 16
I1 = 96
R1 = E1 * I1 // P
NG = 4
TOPG = 2
TOPK = 4
SCALE = 2.5
EPS = 1e-5
BIG = 1e30
N1 = R1 + 1
LAG = 2
LAG1 = 3
ON_POOL = 5
OUT_BLOCK = 4
CTX_COLS, W_COLS = B * KV, 4 * C

(STATS, NORM, XT, SCORES, EXP0, SOFTMAX, ATTN_T, OUT, NORM2, XT2, LOGITS, EXP0G, GATES, GATES_T, BIAS2) = ITEMS = range(15)
AFTER = {XT: 0, SCORES: 1, EXP0: 2, SOFTMAX: 3, ATTN_T: 5, OUT: 6, NORM2: 7, XT2: 9, LOGITS: 10, EXP0G: 11, GATES: 12,
         GATES_T: 14, BIAS2: 15, STATS: 14, NORM: 15}
LINKS0 = 14

PACK_A = {"ident": P, "ctxT": B * KV, "attn0_w": 4 * C, "cols": 6, "order8": E0, "bo0": C}
PACK_B = {"attn1_w": 4 * C, "b1col": R0, "gate1T": E1, "gbias": E1, "blk": H1, "below": NG * NG, "bo1": C}


def xattn_moe_kernel(nc, a, out):
    with ExitStack() as ctx:
        def sb(name, shape, dt=F32):
            return ctx.enter_context(nc.sbuf_tensor(name, shape, dt))

        def sem(name):
            return ctx.enter_context(nc.semaphore(name))

        bank = [ctx.enter_context(nc.psum_tensor(f"bank{i}", [P, 512], F32)) for i in range(8)]

        x = sb("x", [P, NT, C])
        pack_a = sb("pack_a", [P, sum(PACK_A.values())])
        pack_b = sb("pack_b", [P, sum(PACK_B.values())])

        def part(buf, widths, name):
            at = 0
            for n, w in widths.items():
                if n == name:
                    return buf[:, at:at + w]
                at += w

        ident = part(pack_a, PACK_A, "ident")
        ctxT = part(pack_a, PACK_A, "ctxT")
        attn0_w = part(pack_a, PACK_A, "attn0_w").rearrange("p (w c) -> p w c", w=4)
        cols = part(pack_a, PACK_A, "cols")
        order8 = part(pack_a, PACK_A, "order8")
        bo0 = part(pack_a, PACK_A, "bo0")
        attn1_w = part(pack_b, PACK_B, "attn1_w").rearrange("p (w c) -> p w c", w=4)
        b1col = part(pack_b, PACK_B, "b1col")
        gate1T = part(pack_b, PACK_B, "gate1T")
        gbias = part(pack_b, PACK_B, "gbias")
        blk = part(pack_b, PACK_B, "blk")
        below = part(pack_b, PACK_B, "below").rearrange("p (g h) -> p g h", g=NG)
        bo1 = part(pack_b, PACK_B, "bo1")
        rows16 = sb("rows16", [G0, C + G0 + C])
        w_redT = rows16[:, 0:C]
        wg_sb = rows16[0:E0, C:C + G0]
        b2_sb = rows16[:, C + G0:]
        mask8 = sb("mask8", [P, B * KV], U8)
        w2_1 = sb("w2_1", [P, R1, C])
        ws2 = sb("ws2", [I1, C])

        w1h = sb("w1h", [C, R0 * P], F32R)
        w1l = sb("w1l", [C, R0 * P], F32R)
        gu1h = sb("gu1h", [C, 2, R1 * P + I1], F32R)
        gu1l = sb("gu1l", [C, 2, R1 * P + I1], F32R)
        sel0 = sb("sel0", [2 * E0, E0, P], F32R)
        sel1 = sb("sel1", [P, R1, P], F32R)
        xTh = sb("xTh", [C, NT * P], F32R)
        xTl = sb("xTl", [C, NT * P], F32R)
        gT = sb("gT", [P, NT * P], F32R)
        gTs = sb("gTs", [2 * E0, CH])

        kT0 = sb("kT0", [C, B * KV])
        vT0 = sb("vT0", [C, B * KV])
        A0 = sb("A0", [C, B * KV])
        bqrep = sb("bqrep", [P, C])
        s0bias = sb("s0bias", [P, B * KV])
        V0 = sb("V0", [KV, B, C])
        kT1 = sb("kT1", [C, B * KV])
        vT1 = sb("vT1", [C, B * KV])
        Kblk = sb("Kblk", [C, B, H1, KV])
        V1 = sb("V1", [P, B, 4, C])
        maskrow = sb("maskrow", [P, B, H1, KV], BF16)
        onesb = sb("onesb", [P, P], BF16)
        ones = sb("ones", [P, P])
        warm = sb("warm", [P, 1])
        bq1s = sb("bq1s", [P, 1])
        bo16 = sb("bo16", [P, C])
        wgsq = sb("wgsq", [E0, G0])
        wgss = sb("wgss", [E0, 1])
        wginv = sb("wginv", [E0, 1])
        wgn = sb("wgn", [E0, G0])
        wgnT = sb("wgnT", [G0, E0])
        R0w = sb("R0w", [C, P])
        R1w = sb("R1w", [C, P])
        mhalf = sb("mhalf", [P, NT])

        st = sb("st", [P, 2, TPB, 6])
        mv = sb("mv", [P, 2, TPB, 2])
        ve = sb("ve", [P, 2, TPB])
        rstd = sb("rstd", [P, 2, TPB])
        xn = sb("xn", [P, 2, TPB, C])
        xT = sb("xT", [C, 2, CH])
        s0 = sb("s0", [P, TPB, KV])
        m0 = sb("m0", [P, TPB])
        z0 = sb("z0", [P, TPB])
        attn0 = sb("attn0", [P, TPB, KV])
        aT0 = sb("aT0", [KV, CH])
        lg0 = sb("lg0", [P, TPB, E0])
        lt0 = sb("lt0", [P, TPB, E0])
        oh0 = sb("oh0", [P, TPB, E0])
        gate0 = sb("gate0", [P, TPB, 2, E0], F32R)
        act = sb("act", [P, 4, 512])
        hm = sb("hm", [P, 4, 512])
        Vblk = hm[:, :, :].rearrange("p b (h k) -> p b h k", h=H1)
        sel1f = act[0:2 * E1, :, :].rearrange("p a n -> p (a n)")[:, 0:R1 * P].rearrange("p (r n) -> p r n", r=R1)
        outT = xT[:, 0, :]
        aT1 = act[:, 0:2, :].rearrange("p a (g n) -> p a g n", g=4)
        qT = sb("qT", [C, B - 1, CH])
        sc1 = sb("sc1", [P, 2, H1, KV])
        gx = sc1[:, :, :, :].rearrange("p b h k -> p b (h k)")
        at1 = sb("at1", [P, 2, H1, KV])
        an1 = sb("an1", [P, 2, H1, KV])
        sel0f = an1[0:2 * E0, :, :, :].rearrange("p a h k -> p (a h k)").rearrange("p (e n) -> p e n", e=E0)

        def ring(main, extra, r):
            return main[:, r % 4, :] if r < R1 else extra

        def flat(buf):
            return buf.rearrange("p h k -> p (h k)")

        def act_slot(r):
            return ring(act, flat(at1[:, 0, :, :]), r)

        def hm_slot(r):
            return ring(hm, flat(at1[:, 1, :, :]), r)

        def hmh_slot(r):
            return ring(w1h[:, :].rearrange("p (a n) -> p a n", a=4), hmh4[:, :], r)

        def hml_slot(r):
            return ring(w1l[:, :].rearrange("p (a n) -> p a n", a=4), hml4[:, :], r)

        mx1 = sb("mx1", [P, 2, H1])
        z1 = sb("z1", [P, 2, H1])
        rz1 = sb("rz1", [P, 2, H1])
        sg = sb("sg", [P, NT, E1])
        sbs = sb("sbs", [P, NT, E1])
        ra, rb, rc, rd = (sb(f"route{i}", [P, NT, E1]) for i in range(4))
        pr = sb("pr", [P, 2, NT * NG, 2])
        gq = sb("gq", [P, 4, NT, NG])
        gs = sb("gs", [P, NT, NG])
        gk = sb("gk", [P, NT, NG])
        thr = sb("thr", [P, NT])
        top8 = sb("top8", [P, NT, 8])
        gate1 = sb("gate1", [P, NT, 2, E1], F32R)

        with nc.sbuf_tensor("wf", [C, 2 * (R1 * P + I1)], F32) as wf, nc.sbuf_tensor("w2_0", [P, R0, C], F32) as w2_0:
            w1f = wf[:, 0:R0 * P]
            gu1f = wf[:, :].rearrange("p (w n) -> p w n", w=2)
        w2h = sb("w2h", [P, N1, C], F32R)
        w2l = sb("w2l", [P, N1, C], F32R)
        hmh4 = sb("hmh4", [P, CH], F32R)
        hml4 = sb("hml4", [P, CH], F32R)

        class Stages:
            pass

        s = Stages()
        s.ld_a = sem("ld_a")
        s.ld_b = sem("ld_b")
        s.ld_rows = sem("ld_rows")
        s.ld_sel = sem("ld_sel")
        s.ld_mask = sem("ld_mask")
        s.ld_w1 = sem("ld_w1")
        s.ld_w2_0 = sem("ld_w2_0")
        s.ld_gu = sem("ld_gu")
        s.ld_w2_1 = sem("ld_w2_1")
        s.stored = sem("stored")
        s.pool_step = sem("pool_step")
        s.dve_link = sem("dve_link")
        s.item_link = sem("item_link")
        s.dve_const = sem("dve_const")
        s.kv_mm = sem("kv_mm")
        s.kv_ready = sem("kv_ready")
        s.a0_mm = sem("a0_mm")
        s.a0_ready = sem("a0_ready")
        s.bq1_ready = sem("bq1_ready")
        s.v0_mm = sem("v0_mm")
        s.v0_ready = sem("v0_ready")
        s.wgss_ready = sem("wgss_ready")
        s.wginv_ready = sem("wginv_ready")
        s.wgn_ready = sem("wgn_ready")
        s.wgT_mm = sem("wgT_mm")
        s.wgT_ready = sem("wgT_ready")
        s.r0_mm = sem("r0_mm")
        s.r0_ready = sem("r0_ready")
        s.r1_ready = sem("r1_ready")
        s.bo16_ready = sem("bo16_ready")
        s.vblk_ready = sem("vblk_ready")
        s.kblk_ready = sem("kblk_ready")
        s.v1_mm = sem("v1_mm")
        s.v1_copied = sem("v1_copied")
        s.v1_ready = sem("v1_ready")
        s.mask_ready = sem("mask_ready")
        s.w1h_ready = sem("w1h_ready")
        s.w1l_ready = sem("w1l_ready")
        s.guh_ready = sem("guh_ready")
        s.gul_ready = sem("gul_ready")
        s.cleared = sem("cleared")
        s.sel_ready = sem("sel_ready")
        s.s0_mm = sem("s0_mm")
        s.s0_shifted = sem("s0_shifted")
        s.exp0_ready = sem("exp0_ready")
        s.attn0_ready = sem("attn0_ready")
        s.aT0_mm = sem("aT0_mm")
        s.aT0_ready = sem("aT0_ready")
        s.out0_mm = sem("out0_mm")
        s.x1_ready = sem("x1_ready")
        s.lg0_mm = sem("lg0_mm")
        s.lt0_ready = sem("lt0_ready")
        s.ex0_ready = sem("ex0_ready")
        s.gate0_ready = sem("gate0_ready")
        s.gT0_mm = sem("gT0_mm")
        s.gTs_ready = sem("gTs_ready")
        s.gT0_ready = sem("gT0_ready")
        s.b2_mm = sem("b2_mm")
        s.b2_added = sem("b2_added")
        s.h_ready = sem("h_ready")
        s.act_ready = sem("act_ready")
        s.e_ready = sem("e_ready")
        s.hm_ready = sem("hm_ready")
        s.hm_used = sem("hm_used")
        s.o_added = sem("o_added")
        s.q_mm = sem("q_mm")
        s.qT_ready = sem("qT_ready")
        s.s1_mm = sem("s1_mm")
        s.mx1_ready = sem("mx1_ready")
        s.s1_shifted = sem("s1_shifted")
        s.exp1_ready = sem("exp1_ready")
        s.z1_ready = sem("z1_ready")
        s.rz1_ready = sem("rz1_ready")
        s.an1_ready = sem("an1_ready")
        s.t1_mm = sem("t1_mm")
        s.aT1_ready = sem("aT1_ready")
        s.av_mm = sem("av_mm")
        s.x3_ready = sem("x3_ready")
        s.lg1_mm = sem("lg1_mm")
        s.sg_ready = sem("sg_ready")
        s.gate1_ready = sem("gate1_ready")
        s.gT1_mm = sem("gT1_mm")
        s.gT1_ready = sem("gT1_ready")
        s.h_ready1 = sem("h_ready1")
        s.act_ready1 = sem("act_ready1")
        s.prod_ready1 = sem("prod_ready1")
        s.e_ready1 = sem("e_ready1")
        s.gx_ready = sem("gx_ready")
        s.hm_ready1 = sem("hm_ready1")
        s.hmh_ready = sem("hmh_ready")
        s.hml_ready = sem("hml_ready")
        s.hm_used1 = sem("hm_used1")
        s.w2h_ready = sem("w2h_ready")
        s.w2l_ready = sem("w2l_ready")
        s.outT_ready = sem("outT_ready")
        s.out_mm = sem("out_mm")
        s.o_added1 = sem("o_added1")
        s.ld_x = [sem(f"ld_x{b}") for b in range(B)]
        s.ln_stats = [sem(f"ln_stats{k}") for k in range(4)]
        s.ln_var = [sem(f"ln_var{k}") for k in range(4)]
        s.ln_eps = [sem(f"ln_eps{k}") for k in range(4)]
        s.ln_rstd = [sem(f"ln_rstd{k}") for k in range(4)]
        s.xn_ready = [sem(f"xn_ready{k}") for k in range(4)]
        s.tr_ready = [sem(f"tr_ready{k}") for k in range(4)]
        s.xT_ready = [sem(f"xT_ready{k}") for k in range(4)]
        s.xTh_ready = [sem(f"xTh_ready{k}") for k in range(4)]
        s.xTl_ready = [sem(f"xTl_ready{k}") for k in range(4)]
        x_dram = a["x"].rearrange("b (p j) c -> b p j c", p=P)
        out_dram = out.rearrange("b (p j) c -> b p j c", p=P)
        block = ctx.enter_context(nc.Block())

        def tiles(buf, b):
            return buf[:, bass.ds(b * TPB, TPB)]

        def chunk(buf, b):
            return buf[:, bass.ds(b * CH, CH)]

        def cut(buf, r):
            return buf[:, r * P:(r + 1) * P]

        def quarters(n):
            return bank[n][:, :].rearrange("p (j c) -> p j c", j=TPB)

        def over(col, width):
            return col.unsqueeze(2).broadcast_to([P, col.shape[1], width])

        def rows_of(row, n):
            return row.unsqueeze(1).broadcast_to([P, n, row.shape[1]])

        def side(r, c):
            ahead = [(n, c + (2 if n in (STATS, NORM) else 1)) for n in ITEMS if AFTER[n] == r]
            return [(n, b) for n, b in ahead if b < B]

        def starts(i, first):
            b, off = divmod(i - first, TPB)
            return [b] if off == 0 and 0 <= b < B else []

        ADD, NORM4, T4, LG4 = 8, 10, 11, 12
        LN3, NORM3, T3, QUERY = 4, 6, 7, 8

        def score_bank(i):
            return bank[{0: 5, 1: 7}.get(i, i % 2)]

        LOOPED = B - 2

        def looped(i, first):
            return [b for b in starts(i, first) if b < LOOPED]

        EARLY_LN3, EARLY_NORM3, EARLY_T3, EARLY_QUERY = 0, 2, 4, 6

        def early(r, first):
            b, off = divmod(r - first, 4)
            return [b] if off == 0 and 0 <= b < B - 1 else []

        ROUTE0 = {13: (0,), 14: (1,), 15: (2, 3), 16: (4, 5), 17: (6, 7, 8)}
        LATE_NORM4 = {0: B - 2, 2: B - 1}
        LATE_T4 = {1: B - 2, 3: B - 1}
        LATE_LG4 = {2: B - 2, 4: B - 1}
        ROUTE = {4: (0,), 5: (1,), 6: (2,), 7: (3,), 8: (4,), 9: (5,), 10: (6,), 11: (7, 8)}
        REST = range(1, B)

        def gate_bank(r, first=False):
            return r % 2 if r < R1 or first else 6

        def up_bank(r, first=False):
            return 2 + r % 2 if r < R1 or first else 7

        def before(r, c, first):
            if r >= 4:
                return c * N1 + (r - 3)
            return None if first else c * N1 + (r - 4)

        def w2_piece(n):
            q = R1 // 4
            if n < 4:
                return w2_1[:, n * q:(n + 1) * q, :], slice(0, P), slice(n * q, (n + 1) * q)
            return ws2[:, :].unsqueeze(1), slice(0, I1), slice(R1, N1)

        @block.sync
        def _(sp):
            sp.dma_start(tiles(x, 0), x_dram[0]).then_inc(s.ld_x[0], 16)
            sp.dma_start(pack_a[:, :], a["pack_a"]).then_inc(s.ld_a, 16)
            sp.dma_start(pack_b[:, :], a["pack_b"]).then_inc(s.ld_b, 16)
            for b in range(1, B):
                sp.dma_start(tiles(x, b), x_dram[b]).then_inc(s.ld_x[b], 16)
            sp.dma_start(w2_0[:, :, :], a["w2_0"]).then_inc(s.ld_w2_0, 16)
            sp.dma_start(w2_1[:, :, :], a["w2_1"]).then_inc(s.ld_w2_1, 16)
            sp.dma_start(ws2[:, :], a["ws2"]).then_inc(s.ld_w2_1, 16)
            sp.wait_ge(s.w1l_ready, 4)
            sp.dma_start(gu1f, a["gu1"]).then_inc(s.ld_gu, 16)
            for b in range(B):
                sp.wait_ge(s.o_added1, b + 1)
                sp.dma_start(out_dram[b], tiles(x, b)).then_inc(s.stored, 16)
            sp.wait_ge(s.stored, 16 * B)

        @block.scalar
        def _(act_e):
            act_e.dma_start(rows16[:, :], a["rows16"]).then_inc(s.ld_rows, 16)
            act_e.dma_start(w1f, a["w1"]).then_inc(s.ld_w1, 16)
            act_e.dma_start(sel0f, a["sel0"]).then_inc(s.ld_sel, 16)
            act_e.dma_start(sel1f, a["sel1"]).then_inc(s.ld_sel, 16)
            act_e.dma_start(mask8[:, :], a["mask"].broadcast_to([P, B * KV])).then_inc(s.ld_mask, 16)

            def copy_xT(k, b, n):
                act_e.wait_ge(s.tr_ready[k], b + 1)
                nc.scalar.copy(xT[:, k % 2, :], bank[n][:, :]).then_inc(s.xT_ready[k], 1)

            def round_xT(k, b):
                act_e.wait_ge(s.xT_ready[k], b + 1)
                nc.scalar.copy(chunk(xTh, b), xT[:, k % 2, :]).then_inc(s.xTh_ready[k], 1)

            def item(n, b):
                if n == XT:
                    copy_xT(0, b, 5)
                elif n == EXP0:
                    act_e.wait_ge(s.s0_shifted, b + 1)
                    nc.scalar.activation(s0[:, :, :], s0[:, :, :], ACT.Exp).then_inc(s.exp0_ready, 1)
                elif n == ATTN_T:
                    act_e.wait_ge(s.aT0_mm, b + 1)
                    nc.scalar.copy(aT0[:, :], bank[7][0:KV, :]).then_inc(s.aT0_ready, 1)
                elif n == XT2:
                    copy_xT(1, b, 6)
                    round_xT(1, b)
                elif n == EXP0G:
                    act_e.wait_ge(s.lt0_ready, b + 1)
                    nc.scalar.activation(lt0[:, :, :], lt0[:, :, :], ACT.Exp).then_inc(s.ex0_ready, 1)
                elif n == GATES_T:
                    act_e.wait_ge(s.gT0_mm, b + 1)
                    nc.scalar.copy(gTs[:, :], bank[7][0:2 * E0, :]).then_inc(s.gTs_ready, 1)
                    act_e.wait_ge(s.gTs_ready, b + 1)
                    nc.scalar.copy(chunk(gT, b)[0:2 * E0], gTs[:, :]).then_inc(s.gT0_ready, 1)

            act_e.wait_ge(s.dve_const, 1)
            nc.scalar.activation(warm[:, :], onesb[:, 0:1], ACT.Exp)

            act_e.wait_ge(s.ld_a, 16)
            for n, (dst, col) in enumerate(((kT0, 0), (vT0, 2), (kT1, 3), (vT1, 5))):
                act_e.wait_ge(s.kv_mm, n + 1)
                nc.scalar.activation(dst[:, :], bank[n][:, 0:P], ACT.Identity, bias=cols[:, col:col + 1]).then_inc(s.kv_ready, 1)
                if n == 0:
                    copy_xT(0, 0, 5)
                    act_e.wait_ge(s.a0_mm, 1)
                    nc.scalar.activation(A0[:, :], bank[4][:, 0:P], ACT.Copy, scale=float(C) ** -0.5).then_inc(s.a0_ready, 1)
                    act_e.wait_ge(s.a0_mm, 2)
                    nc.scalar.activation(s0bias[:, :], bank[6][:, 0:P], ACT.Copy, scale=float(C) ** -0.5).then_inc(s.a0_ready, 1)
            nc.scalar.activation(bq1s[:, :], cols[:, 4:5], ACT.Copy, scale=float(D1) ** -0.5).then_inc(s.bq1_ready, 1)
            for n in range(SCORES, len(ITEMS)):
                item(n, 0)
                if n == EXP0:
                    act_e.wait_ge(s.ld_w1, 16)
                    for q in range(2):
                        nc.scalar.copy(w1h[:, q * 512:(q + 1) * 512], w1f[:, q * 512:(q + 1) * 512]).then_inc(s.w1h_ready, 1)
                if n == ATTN_T:
                    for q in range(2, 4):
                        nc.scalar.copy(w1h[:, q * 512:(q + 1) * 512], w1f[:, q * 512:(q + 1) * 512]).then_inc(s.w1h_ready, 1)
                if n == XT2:
                    act_e.wait_ge(s.ld_sel, 32)
                    nc.scalar.copy(sel0[:, :, :], sel0f).then_inc(s.sel_ready, 1)
                    act_e.wait_ge(s.cleared, 2)
                    nc.scalar.copy(sel1[0:2 * E1, :, :], sel1f).then_inc(s.sel_ready, 1)
                if n == EXP0G:
                    for b in range(B):
                        act_e.wait_ge(s.v1_mm, b + 1)
                        nc.scalar.copy(V1[:, b, :, :], quarters(b)).then_inc(s.v1_copied, 1)

            act_e.wait_ge(s.ld_b, 16)

            def experts0(c, last_chunk=False):
                for r in range(R0):
                    act_e.wait_ge(s.h_ready, c * R0 + (r + 1))
                    if r >= 4:
                        act_e.wait_ge(s.hm_ready, c * R0 + (r - 3))
                    nc.scalar.activation(act[:, r % 4, :], bank[r % 2][:, :], ACT.Gelu,
                                         bias=b1col[:, r:r + 1]).then_inc(s.act_ready, 1)
                    for n, b in side(r, c):
                        item(n, b)
                    if last_chunk:
                        for b in early(r, EARLY_T3):
                            copy_xT(2, b, 6)
                        for b in early(r, EARLY_QUERY):
                            query(b)
                        if r % 2 == 0:
                            round_gu(r // 2)

            def query(b):
                act_e.wait_ge(s.q_mm, b + 1)
                if b == B - 1:
                    act_e.wait_ge(s.s1_mm, TPB)
                nc.scalar.activation(qT[:, b % (B - 1), :], bank[7][:, :], ACT.Identity, bias=bq1s[:, :],
                                     scale=float(D1) ** -0.5).then_inc(s.qT_ready, 1)

            def exp1(i):
                act_e.wait_ge(s.s1_shifted, i + 1)
                if i >= 2:
                    act_e.wait_ge(s.an1_ready, i - 1)
                nc.scalar.activation(at1[:, i % 2, :, :], sc1[:, i % 2, :, :], ACT.Exp).then_inc(s.exp1_ready, 1)

            def attn_copy(i):
                act_e.wait_ge(s.t1_mm, i + 1)
                if i >= 2:
                    act_e.wait_ge(s.av_mm, i - 1)
                nc.scalar.copy(aT1[:, i % 2, :, :], quarters(2 + i % 2)).then_inc(s.aT1_ready, 1)

            def logits1(b):
                act_e.wait_ge(s.lg1_mm, b + 1)
                n = 6 if b == B - 1 else 7
                nc.scalar.activation(tiles(sg, b), quarters(n)[:, :, 0:E1], ACT.Exp, scale=-1.0).then_inc(s.sg_ready, 1)

            def round_gu(n):
                w, q = divmod(n, 4)
                act_e.wait_ge(s.ld_gu, 16)
                width = (R1 * P + I1) // 4
                nc.scalar.copy(gu1h[:, w, q * width:(q + 1) * width], gu1f[:, w, q * width:(q + 1) * width]).then_inc(s.guh_ready, 1)

            for c in range(B - 1):
                experts0(c)
            experts0(B - 1, last_chunk=True)

            for i in range(NT + 4):
                if 3 <= i < NT + 3:
                    attn_copy(i - 3)
                if i < NT:
                    exp1(i)
                if i == T3:
                    copy_xT(2, B - 1, 6)
                if i == QUERY:
                    query(B - 1)
                for b in looped(i, T4):
                    copy_xT(3, b, 6)
                    round_xT(3, b)
                for b in looped(i, LG4):
                    logits1(b)
                if i % 2 == 0 and 1 <= i // 2 <= 5:
                    n = i // 2 - 1
                    if n == 0:
                        act_e.wait_ge(s.o_added, B)
                        act_e.wait_ge(s.gul_ready, 8)
                        act_e.wait_ge(s.ld_w2_1, 32)
                    src, rows, own = w2_piece(n)
                    nc.scalar.copy(w2h[rows, own, :], src).then_inc(s.w2h_ready, 1)

            def turn_copy(b, n):
                act_e.wait_ge(s.gT1_mm, b + 1)
                nc.scalar.copy(chunk(gT, b)[0:2 * E1], bank[n][0:2 * E1, :]).then_inc(s.gT1_ready, 1)


            def high(r, c, first=False):
                act_e.wait_ge(s.hm_ready1, c * N1 + (r + 1))
                if before(r, c, first) is not None:
                    act_e.wait_ge(s.hm_used1, before(r, c, first))
                m = P if r < R1 else I1
                nc.scalar.copy(hmh_slot(r)[0:m], hm_slot(r)[0:m]).then_inc(s.hmh_ready, 1)

            def copy_out(c):
                act_e.wait_ge(s.hm_used1, c * N1)
                nc.scalar.copy(outT, bank[4][:, :]).then_inc(s.outT_ready, 1)

            def experts1(c, first=False):
                for r in range(N1):
                    m = P if r < R1 else I1
                    if r == LAG1 and not first:
                        copy_out(c)
                    act_e.wait_ge(s.h_ready1, c * N1 + (r + 1))
                    if before(r, c, first) is not None:
                        act_e.wait_ge(s.hm_ready1, before(r, c, first))
                    nc.scalar.activation(act_slot(r)[0:m], bank[gate_bank(r, first)][0:m, :], ACT.Silu).then_inc(s.act_ready1, 1)
                    if first and r == 0:
                        turn_copy(0, 7)
                    if first and ON_POOL <= r < R1:
                        act_e.wait_ge(s.e_ready1, r + 1)
                        if r >= ON_POOL + 2:
                            act_e.wait_ge(s.hm_ready1, r - 1)
                        nc.scalar.copy(gx[:, r % 2, :], bank[5][:, :]).then_inc(s.gx_ready, 1)
                    if r >= 1:
                        high(r - 1, c, first)
                    elif not first:
                        high(N1 - 1, c - 1)
                    if first and r in LATE_T4:
                        b = LATE_T4[r]
                        act_e.wait_ge(s.xTl_ready[3], b)
                        copy_xT(3, b, 6)
                        round_xT(3, b)
                    if first and LATE_LG4.get(r) == B - 1:
                        for b in LATE_LG4.values():
                            logits1(b)
                if first:
                    for b in REST:
                        turn_copy(b, 6 + (b + 1) % 2)

            experts1(0, first=True)
            with act_e.Fori(1, B) as c:
                experts1(c)
            high(N1 - 1, B - 1)
            copy_out(B)

        @block.gpsimd
        def _(pool):
            n_step = [0]

            def step(ins):
                n_step[0] += 1
                ins.then_inc(s.pool_step, 1)
                pool.wait_ge(s.pool_step, n_step[0])

            def rstd_of(k, b):
                pool.wait_ge(s.ln_var[k], b + 1)
                pool.wait_ge(s.pool_step, 1)
                nc.gpsimd.tensor_scalar(ve[:, k % 2, :], mv[:, k % 2, :, 1], EPS, None, ALU.add).then_inc(s.ln_eps[k], 1)
                pool.wait_ge(s.ln_eps[k], b + 1)
                nc.gpsimd.tensor_tensor(rstd[:, k % 2, :], ve[:, k % 2, :], mhalf[:, 0:TPB], ALU.pow).then_inc(s.ln_rstd[k], 1)

            def low_half(k, b):
                pool.wait_ge(s.xTh_ready[k], b + 1)
                nc.gpsimd.tensor_tensor(chunk(xTl, b), xT[:, k % 2, :], chunk(xTh, b).bitcast(F32),
                                        ALU.subtract).then_inc(s.xTl_ready[k], 1)

            def low_gu(n):
                w, q = divmod(n, 4)
                width = (R1 * P + I1) // 4
                own = slice(q * width, (q + 1) * width)
                pool.wait_ge(s.guh_ready, n + 1)
                nc.gpsimd.tensor_tensor(gu1l[:, w, own], gu1f[:, w, own], gu1h[:, w, own].bitcast(F32),
                                        ALU.subtract).then_inc(s.gul_ready, 1)

            def low_w1(q):
                pool.wait_ge(s.w1h_ready, q + 1)
                nc.gpsimd.tensor_tensor(w1l[:, q * 512:(q + 1) * 512], w1f[:, q * 512:(q + 1) * 512],
                                        w1h[:, q * 512:(q + 1) * 512].bitcast(F32), ALU.subtract).then_inc(s.w1l_ready, 1)

            def block_diagonal(src, dst, b, ready):
                nc.gpsimd.tensor_tensor(dst[:, b, :, :], rows_of(src[:, b * KV:(b + 1) * KV], H1),
                                        over(blk, KV), ALU.mult).then_inc(ready, 1)

            step(nc.gpsimd.memset(mhalf[:, :], -0.5))
            step(nc.gpsimd.memset(R0w[:, :], 0.0))
            step(nc.gpsimd.memset(R1w[:, :], 0.0))
            rstd_of(0, 0)
            nc.gpsimd.memset(gT[:, :].bitcast(F32), 0.0).then_inc(s.cleared, 1)
            nc.gpsimd.memset(sel1[:, :, :].bitcast(F32), 0.0).then_inc(s.cleared, 1)
            pool.wait_ge(s.wgss_ready, 1)
            step(nc.gpsimd.tensor_scalar(wgss[:, :], wgss[:, :], 1e-8, None, ALU.max))
            nc.gpsimd.tensor_tensor(wginv[:, :], wgss[:, :], mhalf[0:E0, 0:1], ALU.pow).then_inc(s.wginv_ready, 1)
            rstd_of(0, 1)
            pool.wait_ge(s.ld_b, 16)
            pool.wait_ge(s.kv_ready, 4)
            for b in range(B):
                block_diagonal(vT1, Vblk, b, s.vblk_ready)
            low_w1(0)
            rstd_of(1, 0)
            low_half(1, 0)
            for q in range(1, 4):
                low_w1(q)
            nc.gpsimd.tensor_copy(R1w[:, 0:E1], gate1T).then_inc(s.r1_ready, 1)
            nc.gpsimd.tensor_scalar(bo16[:, :], bo1, 1.0 / H1, None, ALU.mult).then_inc(s.bo16_ready, 1)
            pool.wait_ge(s.bo16_ready, 1)
            for b in range(B):
                pool.wait_ge(s.v1_copied, b + 1)
                nc.gpsimd.tensor_tensor(V1[:, b, :, :], V1[:, b, :, :],
                                        bo16[:, :].unsqueeze(1).broadcast_to([P, 4, C]), ALU.add).then_inc(s.v1_ready, 1)
                block_diagonal(kT1, Kblk, b, s.kblk_ready)
            for b in range(1, B):
                if b >= 2:
                    rstd_of(0, b)
                rstd_of(1, b)
                low_half(1, b)
            pool.wait_ge(s.ld_mask, 16)
            for b in range(B):
                nc.gpsimd.tensor_scalar(maskrow[:, b, :, :], rows_of(mask8[:, b * KV:(b + 1) * KV], H1), -BIG / P, None,
                                        ALU.mult).then_inc(s.mask_ready, 1)

            for b in range(B - 1):
                rstd_of(2, b)
                for n in range(2 * b, 2 * b + 2 if b < B - 2 else 8):
                    low_gu(n)
            for i in range(NT + 4):
                if 1 <= i <= NT:
                    t = i - 1
                    pool.wait_ge(s.rz1_ready, t + 1)
                    if t >= 2:
                        pool.wait_ge(s.t1_mm, t - 1)
                    nc.gpsimd.tensor_tensor(an1[:, t % 2, :, :], at1[:, t % 2, :, :], over(rz1[:, t % 2, :], KV),
                                            ALU.mult).then_inc(s.an1_ready, 1)
                if i == LN3:
                    rstd_of(2, B - 1)
                for b in starts(i, ADD):
                    rstd_of(3, b)
                for b in looped(i, T4):
                    low_half(3, b)
                if i % 2 == 0 and 1 <= i // 2 <= 5:
                    n = i // 2 - 1
                    src, rows, own = w2_piece(n)
                    pool.wait_ge(s.w2h_ready, n + 1)
                    nc.gpsimd.tensor_tensor(w2l[rows, own, :], src, w2h[rows, own, :].bitcast(F32),
                                            ALU.subtract).then_inc(s.w2l_ready, 1)

            def low(r, c, first=False):
                pool.wait_ge(s.hmh_ready, c * N1 + (r + 1))
                if before(r, c, first) is not None:
                    pool.wait_ge(s.hm_used1, before(r, c, first))
                m = P if r < R1 else I1
                nc.gpsimd.tensor_tensor(hml_slot(r)[0:m], hm_slot(r)[0:m], hmh_slot(r)[0:m].bitcast(F32),
                                        ALU.subtract).then_inc(s.hml_ready, 1)

            for r in range(R1):
                if r >= ON_POOL:
                    pool.wait_ge(s.hm_ready1, r)
                    pool.wait_ge(s.prod_ready1, r + 1)
                    pool.wait_ge(s.gx_ready, r - ON_POOL + 1)
                    if r >= 4:
                        pool.wait_ge(s.hml_ready, r - 3)
                    nc.gpsimd.tensor_tensor(hm[:, r % 4, :], act[:, r % 4, :], gx[:, r % 2, :],
                                            ALU.mult).then_inc(s.hm_ready1, 1)
                if r == 0:
                    rstd_of(3, B - 1)
                if r >= 1:
                    low(r - 1, 0, first=True)
                if r - 1 in LATE_T4:
                    low_half(3, LATE_T4[r - 1])
            low(R1 - 1, 0, first=True)
            low(R1, 0, first=True)
            with pool.Fori(1, B) as c:
                for r in range(N1):
                    low(r, c)

        @block.vector
        def _(v):
            n_link = [0]

            def step(ins):
                n_link[0] += 1
                ins.then_inc(s.dve_link, 1)
                v.wait_ge(s.dve_link, n_link[0])

            def statistics(k, b):
                xc = tiles(x, b)
                for j in range(TPB):
                    last = nc.vector.bn_stats(st[:, k % 2, j, :], xc[:, j, :])
                last.then_inc(s.ln_stats[k], 1)
                v.wait_ge(s.ln_stats[k], b + 1)
                for j in range(TPB):
                    last = nc.vector.bn_aggr(mv[:, k % 2, j, :], st[:, k % 2, j, :])
                last.then_inc(s.ln_var[k], 1)

            def normalise(k, b):
                xc = tiles(x, b)
                v.wait_ge(s.ln_rstd[k], b + 1)
                for j in range(TPB):
                    last = nc.vector.tensor_scalar(xn[:, k % 2, j, :], xc[:, j, :], mv[:, k % 2, j, 0:1],
                                                   rstd[:, k % 2, j:j + 1], ALU.subtract, ALU.mult)
                last.then_inc(s.xn_ready[k], 1)

            def add_to_x(b, n, ready, signal):
                v.wait_ge(ready, b + 1)
                nc.vector.tensor_tensor(tiles(x, b), tiles(x, b), quarters(n), ALU.add).then_inc(signal, 1)
                v.wait_ge(signal, b + 1)

            n_item = [0]

            def item_step(b, ins):
                n_item[0] += 1
                ins.then_inc(s.item_link, 1)
                v.wait_ge(s.item_link, b * LINKS0 + n_item[0])

            def item(n, b):
                if n == STATS:
                    statistics(0, b)
                elif n == NORM:
                    normalise(0, b)
                elif n == SCORES:
                    n_item[0] = 0
                    v.wait_ge(s.s0_mm, b + 1)
                    own = bass.ds(b * KV, KV)
                    item_step(b, nc.vector.tensor_tensor(s0[:, :, :], quarters(6)[:, :, own],
                                                         rows_of(s0bias[:, own], TPB), ALU.add))
                    item_step(b, nc.vector.tensor_reduce(m0[:, :], s0[:, :, :], AX, ALU.max))
                    nc.vector.tensor_tensor(s0[:, :, :], s0[:, :, :], over(m0[:, :], KV), ALU.subtract).then_inc(s.s0_shifted, 1)
                elif n == SOFTMAX:
                    v.wait_ge(s.exp0_ready, b + 1)
                    item_step(b, nc.vector.tensor_reduce(z0[:, :], s0[:, :, :], AX, ALU.add))
                    item_step(b, nc.vector.reciprocal(z0[:, :], z0[:, :]))
                    nc.vector.tensor_tensor(attn0[:, :, :], s0[:, :, :], over(z0[:, :], KV), ALU.mult).then_inc(s.attn0_ready, 1)
                elif n == OUT:
                    add_to_x(b, 5, s.out0_mm, s.x1_ready)
                    statistics(1, b)
                elif n == NORM2:
                    normalise(1, b)
                elif n == LOGITS:
                    v.wait_ge(s.lg0_mm, b + 1)
                    item_step(b, nc.vector.tensor_copy(lg0[:, :, :], quarters(7)[:, :, 0:E0]))
                    item_step(b, nc.vector.tensor_reduce(m0[:, :], lg0[:, :, :], AX, ALU.max))
                    nc.vector.tensor_tensor(lt0[:, :, :], lg0[:, :, :], over(m0[:, :], E0), ALU.subtract).then_inc(s.lt0_ready, 1)
                    item_step(b, nc.vector.tensor_tensor(oh0[:, :, :], lg0[:, :, :], over(m0[:, :], E0), ALU.is_equal))
                    item_step(b, nc.vector.tensor_tensor(oh0[:, :, :], oh0[:, :, :], rows_of(order8, TPB), ALU.mult))
                    item_step(b, nc.vector.tensor_reduce(m0[:, :], oh0[:, :, :], AX, ALU.max))
                    item_step(b, nc.vector.tensor_tensor(oh0[:, :, :], oh0[:, :, :], over(m0[:, :], E0), ALU.is_equal))
                elif n == GATES:
                    v.wait_ge(s.ex0_ready, b + 1)
                    item_step(b, nc.vector.tensor_reduce(z0[:, :], lt0[:, :, :], AX, ALU.add))
                    item_step(b, nc.vector.reciprocal(z0[:, :], z0[:, :]))
                    item_step(b, nc.vector.tensor_tensor(oh0[:, :, :], oh0[:, :, :], over(z0[:, :], E0), ALU.mult))
                    item_step(b, nc.vector.tensor_copy(gate0[:, :, 0, :], oh0[:, :, :]))
                    nc.vector.tensor_tensor(gate0[:, :, 1, :], oh0[:, :, :], gate0[:, :, 0, :].bitcast(F32),
                                            ALU.subtract).then_inc(s.gate0_ready, 1)
                    assert n_item[0] == LINKS0
                elif n == BIAS2:
                    add_to_x(b, 6, s.b2_mm, s.b2_added)

            nc.vector.memset(onesb[:, :], 1.0).then_inc(s.dve_const, 1)
            step(nc.vector.memset(ones[:, :], 1.0))
            v.wait_ge(s.ld_x[0], 16)
            item(STATS, 0)
            v.wait_ge(s.ld_a, 16)
            nc.vector.tensor_scalar(bqrep[:, :], ones[:, :], cols[:, 1:2], None, ALU.mult).then_inc(s.dve_const, 1)
            item(NORM, 0)
            v.wait_ge(s.ld_rows, 16)
            step(nc.vector.tensor_tensor(wgsq[:, :], wg_sb, wg_sb, ALU.mult))
            nc.vector.tensor_reduce(wgss[:, :], wgsq[:, :], AX, ALU.add).then_inc(s.wgss_ready, 1)
            v.wait_ge(s.ld_x[1], 16)
            item(STATS, 1)
            v.wait_ge(s.a0_ready, 2)
            item(SCORES, 0)
            v.wait_ge(s.wginv_ready, 1)
            nc.vector.tensor_scalar(wgn[:, :], wg_sb, wginv[:, 0:1], None, ALU.mult).then_inc(s.wgn_ready, 1)
            item(SOFTMAX, 0)
            v.wait_ge(s.v0_mm, 1)
            nc.vector.tensor_tensor(V0[:, :, :], quarters(4)[0:KV], bo0[0:KV].unsqueeze(1).broadcast_to([KV, B, C]),
                                    ALU.add).then_inc(s.v0_ready, 1)
            v.wait_ge(s.wgT_mm, 1)
            nc.vector.tensor_copy(wgnT[:, :], bank[4][0:G0, 0:E0]).then_inc(s.wgT_ready, 1)
            v.wait_ge(s.r0_mm, 1)
            v.wait_ge(s.ln_rstd[0], 1)
            nc.vector.tensor_copy(R0w[:, 0:E0], bank[4][:, P:P + E0]).then_inc(s.r0_ready, 1)
            item(OUT, 0)
            item(NORM, 1)
            for n in range(NORM2, len(ITEMS)):
                item(n, 0)
            for b in range(2, B):
                v.wait_ge(s.ld_x[b], 16)

            def experts0(c, last_chunk=False):
                for r in range(R0):
                    v.wait_ge(s.act_ready, c * R0 + (r + 1))
                    v.wait_ge(s.e_ready, c * E0 + (r // 2 + 1))
                    if r >= 4:
                        v.wait_ge(s.hm_used, c * R0 + (r - 3))
                    nc.vector.tensor_tensor(hm[:, r % 4, :], act[:, r % 4, :], bank[2 + r // 2 % 2][:, :],
                                            ALU.mult).then_inc(s.hm_ready, 1)
                    for n, b in side(r, c):
                        item(n, b)
                    if last_chunk:
                        for b in early(r, EARLY_LN3):
                            statistics(2, b)
                        for b in early(r, EARLY_NORM3):
                            if b:
                                v.wait_ge(s.tr_ready[2], b)
                            normalise(2, b)
                if last_chunk:
                    maxima(0)
                    shift(0)
                v.wait_ge(s.hm_used, c * R0 + R0)
                nc.vector.tensor_tensor(tiles(x, c), tiles(x, c), quarters(4), ALU.add).then_inc(s.o_added, 1)

            for c in range(B - 1):
                experts0(c)

            def maxima(i):
                v.wait_ge(s.s1_mm, i + 1)
                scores = score_bank(i)[:, :].rearrange("p (h k) -> p h k", h=H1)
                nc.vector.tensor_reduce(mx1[:, i % 2, :], scores, AX, ALU.max).then_inc(s.mx1_ready, 1)

            def shift(i):
                scores = score_bank(i)[:, :].rearrange("p (h k) -> p h k", h=H1)
                v.wait_ge(s.mx1_ready, i + 1)
                if i >= 2:
                    v.wait_ge(s.exp1_ready, i - 1)
                nc.vector.tensor_tensor(sc1[:, i % 2, :, :], scores, over(mx1[:, i % 2, :], KV),
                                        ALU.subtract).then_inc(s.s1_shifted, 1)

            def total(i):
                v.wait_ge(s.exp1_ready, i + 1)
                nc.vector.tensor_reduce(z1[:, i % 2, :], at1[:, i % 2, :, :], AX, ALU.add).then_inc(s.z1_ready, 1)

            def inverse(i):
                v.wait_ge(s.z1_ready, i + 1)
                nc.vector.reciprocal(rz1[:, i % 2, :], z1[:, i % 2, :]).then_inc(s.rz1_ready, 1)

            def add_attention(b):
                v.wait_ge(s.av_mm, TPB * (b + 1))
                nc.vector.tensor_tensor(tiles(x, b), tiles(x, b), quarters(4 + b % 2), ALU.add).then_inc(s.x3_ready, 1)
                v.wait_ge(s.x3_ready, b + 1)

            def route(piece, t0, t1):
                t, n = slice(t0, t1), t1 - t0
                pairs = sbs[:, t, :].rearrange("p t (g u w) -> p (t g u) w", g=NG, w=2)
                pr_t = pr[:, :, t0 * NG:t1 * NG, :]
                large, small = (pr_t[:, i, :, :].rearrange("p n u -> p (n u)") for i in range(2))
                g4 = [gq[:, i, t, :].rearrange("p t g -> p (t g)") for i in range(4)]
                fourth = top8[:, t, TOPK - 1:TOPK].broadcast_to([P, n, E1])

                def running(src, dst, by):
                    nc.vector.tensor_copy(dst[:, t, 0:by], src[:, t, 0:by])
                    step(nc.vector.tensor_tensor(dst[:, t, by:], src[:, t, by:], src[:, t, 0:E1 - by], ALU.add))

                if piece == 0:
                    step(nc.vector.tensor_scalar(sg[:, t, :], sg[:, t, :], 1.0, None, ALU.add))
                    step(nc.vector.reciprocal(sg[:, t, :], sg[:, t, :]))
                    step(nc.vector.tensor_tensor(sbs[:, t, :], sg[:, t, :], rows_of(gbias, n), ALU.add))
                elif piece == 1:
                    nc.vector.tensor_tensor(large, pairs[:, :, 0], pairs[:, :, 1], ALU.max)
                    step(nc.vector.tensor_tensor(small, pairs[:, :, 0], pairs[:, :, 1], ALU.min))
                    nc.vector.tensor_tensor(g4[0], pr_t[:, 0, :, 0], pr_t[:, 0, :, 1], ALU.max)
                    nc.vector.tensor_tensor(g4[1], pr_t[:, 0, :, 0], pr_t[:, 0, :, 1], ALU.min)
                    step(nc.vector.tensor_tensor(g4[2], pr_t[:, 1, :, 0], pr_t[:, 1, :, 1], ALU.max))
                    step(nc.vector.tensor_tensor(g4[3], g4[1], g4[2], ALU.max))
                    step(nc.vector.tensor_tensor(gs[:, t, :].rearrange("p t g -> p (t g)"), g4[0], g4[3], ALU.add))
                elif piece == 2:
                    others = gs[:, t, :].unsqueeze(2).broadcast_to([P, n, NG, NG])
                    own = gs[:, t, :].unsqueeze(3).broadcast_to([P, n, NG, NG])
                    above, equal = (z[:, t, :].rearrange("p t (g h) -> p t g h", g=NG) for z in (ra, rb))
                    nc.vector.tensor_tensor(above, others, own, ALU.is_gt)
                    step(nc.vector.tensor_tensor(equal, others, own, ALU.is_equal))
                    step(nc.vector.tensor_tensor(equal, equal, below.unsqueeze(1).broadcast_to([P, n, NG, NG]), ALU.mult))
                    step(nc.vector.tensor_tensor(above, above, equal, ALU.add))
                    step(nc.vector.tensor_reduce(gk[:, t, :], above, AX, ALU.add))
                elif piece == 3:
                    step(nc.vector.tensor_scalar(gk[:, t, :], gk[:, t, :], float(TOPG), -BIG, ALU.is_ge, ALU.mult))
                    step(nc.vector.tensor_tensor(rc[:, t, :].rearrange("p t (g w) -> p t g w", g=NG),
                                                 sbs[:, t, :].rearrange("p t (g w) -> p t g w", g=NG),
                                                 gk[:, t, :].unsqueeze(3).broadcast_to([P, n, NG, NG]), ALU.add))
                    for tt in range(t0, t1):
                        last = nc.vector.max(top8[:, tt, :], rc[:, tt, :])
                    step(last)
                elif piece == 4:
                    nc.vector.tensor_tensor(ra[:, t, :], rc[:, t, :], fourth, ALU.is_gt)
                    step(nc.vector.tensor_tensor(rb[:, t, :], rc[:, t, :], fourth, ALU.is_equal))
                    step(nc.vector.tensor_reduce(thr[:, t], ra[:, t, :], AX, ALU.add))
                    nc.vector.tensor_scalar(thr[:, t], thr[:, t], -1.0, float(TOPK), ALU.mult, ALU.add)
                    running(rb, rc, 1)
                elif piece == 5:
                    running(rc, rd, 2)
                    running(rd, rc, 4)
                    running(rc, rd, 8)
                elif piece == 6:
                    step(nc.vector.tensor_tensor(rd[:, t, :], rd[:, t, :], over(thr[:, t], E1), ALU.is_le))
                    step(nc.vector.tensor_tensor(rb[:, t, :], rb[:, t, :], rd[:, t, :], ALU.mult))
                    step(nc.vector.tensor_tensor(ra[:, t, :], ra[:, t, :], rb[:, t, :], ALU.add))
                    step(nc.vector.tensor_tensor(ra[:, t, :], ra[:, t, :], sg[:, t, :], ALU.mult))
                elif piece == 7:
                    step(nc.vector.tensor_reduce(thr[:, t], ra[:, t, :], AX, ALU.add))
                    step(nc.vector.tensor_scalar(thr[:, t], thr[:, t], 1e-20, 1.0 / SCALE, ALU.add, ALU.mult))
                    step(nc.vector.reciprocal(thr[:, t], thr[:, t]))
                elif piece == 8:
                    step(nc.vector.tensor_tensor(ra[:, t, :], ra[:, t, :], over(thr[:, t], E1), ALU.mult))
                    step(nc.vector.tensor_copy(gate1[:, t, 0, :], ra[:, t, :]))
                    nc.vector.tensor_tensor(gate1[:, t, 1, :], ra[:, t, :], gate1[:, t, 0, :].bitcast(F32),
                                            ALU.subtract).then_inc(s.gate1_ready, 1)

            v.wait_ge(s.o_added, B - 1)
            experts0(B - 1, last_chunk=True)
            v.wait_ge(s.o_added, B)
            for i in range(NT + 4):
                if 1 <= i < NT:
                    maxima(i)
                if 1 <= i <= NT:
                    total(i - 1)
                if 1 <= i < NT:
                    shift(i)
                if 1 <= i <= NT:
                    inverse(i - 1)
                if i == LN3:
                    statistics(2, B - 1)
                if i == NORM3:
                    normalise(2, B - 1)
                for b in starts(i, ADD):
                    add_attention(b)
                    if b < LOOPED:
                        statistics(3, b)
                for b in looped(i, NORM4):
                    normalise(3, b)
                for piece in ROUTE0.get(i, ()):
                    if piece == 0:
                        v.wait_ge(s.sg_ready, 1)
                    route(piece, 0, TPB)

            def add_out(c):
                v.wait_ge(s.out_mm, c)
                nc.vector.tensor_tensor(tiles(x, c - 1), tiles(x, c - 1), quarters(6), ALU.add).then_inc(s.o_added1, 1)

            def experts1(c, first=False):
                for r in range(N1):
                    m = P if r < R1 else I1
                    v.wait_ge(s.act_ready1, c * N1 + (r + 1))
                    if r < R1:
                        nc.vector.tensor_tensor(act_slot(r), act_slot(r), bank[up_bank(r, first)][:, :],
                                                ALU.mult).then_inc(s.prod_ready1, 1)
                        if not first or r < ON_POOL:
                            v.wait_ge(s.prod_ready1, c * R1 + (r + 1))
                            v.wait_ge(s.e_ready1, c * R1 + (r + 1))
                            if not first:
                                v.wait_ge(s.hml_ready, before(r, c, first))
                            nc.vector.tensor_tensor(hm_slot(r), act_slot(r), bank[5][:, :],
                                                    ALU.mult).then_inc(s.hm_ready1, 1)
                    else:
                        if first:
                            v.wait_ge(s.hm_ready1, R1)
                        else:
                            v.wait_ge(s.hml_ready, c * N1)
                        nc.vector.tensor_tensor(hm_slot(r)[0:m], act_slot(r)[0:m], bank[up_bank(r, first)][0:m, :],
                                                ALU.mult).then_inc(s.hm_ready1, 1)
                    if r == OUT_BLOCK and not first:
                        add_out(c)
                    if first and r in LATE_NORM4:
                        b = LATE_NORM4[r]
                        v.wait_ge(s.tr_ready[3], b)
                        normalise(3, b)
                        if b + 1 < B:
                            statistics(3, b + 1)
                    for piece in ROUTE.get(r, ()) if first else ():
                        if piece == 0:
                            v.wait_ge(s.sg_ready, B)
                        route(piece, TPB, NT)

            add_attention(B - 1)
            statistics(3, B - 2)
            experts1(0, first=True)
            with v.Fori(1, B) as c:
                experts1(c)
            add_out(B)

        @block.tensor
        def _(pe):
            def mm(dst, lhsT, rhs, start=True, stop=True):
                return nc.tensor.matmul(dst, lhsT, rhs, start=start, stop=stop, skip_group_check=True)

            def split_mm(dst, wh, wl, xh, xl):
                mm(dst, wh, xh, start=True, stop=False)
                mm(dst, wh, xl, start=False, stop=False)
                return mm(dst, wl, xh, start=False, stop=True)

            def transposes(k, b, n):
                pe.wait_ge(s.xn_ready[k], b + 1)
                for j in range(TPB):
                    last = nc.tensor.transpose(quarters(n)[:, j, :], xn[:, k % 2, j, :], ident)
                last.then_inc(s.tr_ready[k], 1)

            def item(n, b):
                if n == XT:
                    if b:
                        pe.wait_ge(s.x1_ready, b)
                    transposes(0, b, 5)
                elif n == SCORES:
                    if b:
                        pe.wait_ge(s.b2_added, b)
                    pe.wait_ge(s.xT_ready[0], b + 1)
                    for j in range(TPB):
                        last = mm(quarters(6)[:, j, :], cut(xT[:, 0, :], j), A0[:, :])
                    last.then_inc(s.s0_mm, 1)
                elif n == ATTN_T:
                    pe.wait_ge(s.attn0_ready, b + 1)
                    if b:
                        pe.wait_ge(s.gTs_ready, b)
                    for j in range(TPB):
                        last = nc.tensor.transpose(quarters(7)[0:KV, j, :], attn0[:, j, :], ident)
                    last.then_inc(s.aT0_mm, 1)
                elif n == OUT:
                    pe.wait_ge(s.aT0_ready, b + 1)
                    for j in range(TPB):
                        mm(quarters(5)[:, j, :], cut(xT[:, 0, :], j), attn0_w[:, 3, :], stop=False)
                        last = mm(quarters(5)[:, j, :], cut(aT0, j), V0[:, bass.ds(b, 1), :].rearrange("p o c -> p (o c)"),
                                  start=False)
                    last.then_inc(s.out0_mm, 1)
                elif n == XT2:
                    transposes(1, b, 6)
                elif n == LOGITS:
                    pe.wait_ge(s.xT_ready[1], b + 1)
                    for j in range(TPB):
                        last = mm(quarters(7)[:, j, :], cut(xT[:, 1, :], j), R0w[:, :])
                    last.then_inc(s.lg0_mm, 1)
                elif n == GATES_T:
                    pe.wait_ge(s.gate0_ready, b + 1)
                    for j in range(TPB):
                        last = nc.tensor.transpose(quarters(7)[0:2 * E0, j, :], gate0[:, j, :, :].rearrange("p u e -> p (u e)").bitcast(F32),
                                                   ident)
                    last.then_inc(s.gT0_mm, 1)
                elif n == BIAS2:
                    pe.wait_ge(s.gTs_ready, b + 1)
                    for j in range(TPB):
                        last = mm(quarters(6)[:, j, :], cut(gTs, j), b2_sb)
                    last.then_inc(s.b2_mm, 1)

            def values1(b):
                pe.wait_ge(s.vblk_ready, b + 1)
                for g in range(4):
                    last = mm(quarters(b)[:, g, :], Vblk[:, b, 4 * g:4 * g + 4, :], attn1_w[:, 3, :])
                last.then_inc(s.v1_mm, 1)

            pe.wait_ge(s.ld_a, 16)
            mm(bank[0][:, 0:P], attn0_w[:, 0, :], ctxT).then_inc(s.kv_mm, 1)
            item(XT, 0)
            pe.wait_ge(s.kv_ready, 1)
            mm(bank[4][:, 0:P], attn0_w[:, 1, :], kT0[:, :]).then_inc(s.a0_mm, 1)
            pe.wait_ge(s.dve_const, 2)
            mm(bank[6][:, 0:P], bqrep[:, :], kT0[:, :]).then_inc(s.a0_mm, 1)
            mm(bank[1][:, 0:P], attn0_w[:, 2, :], ctxT).then_inc(s.kv_mm, 1)
            pe.wait_ge(s.a0_ready, 2)
            item(SCORES, 0)
            pe.wait_ge(s.ld_b, 16)
            mm(bank[2][:, 0:P], attn1_w[:, 0, :], ctxT).then_inc(s.kv_mm, 1)
            mm(bank[3][:, 0:P], attn1_w[:, 2, :], ctxT).then_inc(s.kv_mm, 1)
            pe.wait_ge(s.kv_ready, 2)
            for b in range(B):
                last = mm(quarters(4)[0:KV, b, :], vT0[:, b * KV:(b + 1) * KV], attn0_w[:, 3, :])
            last.then_inc(s.v0_mm, 1)
            item(ATTN_T, 0)
            pe.wait_ge(s.wgn_ready, 1)
            pe.wait_ge(s.v0_ready, 1)
            nc.tensor.transpose(bank[4][0:G0, 0:E0], wgn[:, :], ident[0:E0, 0:E0]).then_inc(s.wgT_mm, 1)
            item(OUT, 0)
            pe.wait_ge(s.wgT_ready, 1)
            mm(bank[4][:, P:P + E0], w_redT, wgnT[:, :]).then_inc(s.r0_mm, 1)
            pe.wait_ge(s.kv_ready, 4)
            for b in range(B - 1):
                values1(b)
            item(XT2, 0)
            pe.wait_ge(s.r0_ready, 1)
            item(LOGITS, 0)
            values1(B - 1)

            def expand_gates(c, r):
                mm(bank[2 + r // 2 % 2][:, :], sel0[:, r // 2, :], chunk(gT, c)[0:2 * E0]).then_inc(s.e_ready, 1)

            def experts0(c, last_chunk=False):
                pe.wait_ge(s.xTl_ready[1], c + 1)
                if c:
                    pe.wait_ge(s.gT0_ready, c + 1)
                for r in range(R0 + LAG):
                    if r < R0:
                        if r % 4 == 0:
                            pe.wait_ge(s.w1l_ready, r // 4 + 1)
                        if r >= 2:
                            pe.wait_ge(s.act_ready, c * R0 + (r - 1))
                        if r >= 4 and r % 2 == 0:
                            pe.wait_ge(s.hm_ready, c * R0 + (r - 2))
                        if c == 0 and r < 2:
                            pe.wait_ge(s.v1_copied, r + 1)
                        split_mm(bank[r % 2][:, :], cut(w1h, r), cut(w1l, r), chunk(xTh, c), chunk(xTl, c))\
                            .then_inc(s.h_ready, 1)
                        if c == 0 and r == 0:
                            item(GATES_T, 0)
                        elif c == 0 and r == 1:
                            pe.wait_ge(s.v1_copied, B)
                            pe.wait_ge(s.sel_ready, 2)
                            pe.wait_ge(s.ld_w2_0, 16)
                            pe.wait_ge(s.gT0_ready, 1)
                            expand_gates(c, 0)
                            item(BIAS2, 0)
                        elif r % 2 == 0:
                            expand_gates(c, r)
                    if r >= LAG:
                        q = r - LAG
                        pe.wait_ge(s.hm_ready, c * R0 + (q + 1))
                        for j in range(TPB):
                            last = mm(quarters(4)[:, j, :], hm[:, q % 4, j * P:(j + 1) * P], w2_0[:, q, :],
                                      start=(q == 0 and j == 0), stop=(q == R0 - 1))
                        last.then_inc(s.hm_used, 1)
                    for n, b in side(r, c):
                        item(n, b)
                    if last_chunk:
                        for b in early(r, EARLY_T3):
                            transposes(2, b, 6)
                        for b in early(r, EARLY_QUERY):
                            queries(b)
                        if r >= R0:
                            scores(r - R0)

            def queries(b):
                pe.wait_ge(s.xT_ready[2], b + 1)
                if b:
                    pe.wait_ge(s.qT_ready, b)
                mm(bank[7][:, :], attn1_w[:, 1, :], xT[:, 0, :]).then_inc(s.q_mm, 1)

            def attn_transposes(i):
                pe.wait_ge(s.an1_ready, i + 1)
                if i >= 2:
                    pe.wait_ge(s.aT1_ready, i - 1)
                for g in range(4):
                    last = nc.tensor.transpose(quarters(2 + i % 2)[:, g, :],
                                               an1[:, i % 2, 4 * g:4 * g + 4, :].rearrange("p h k -> p (h k)"), ident)
                last.then_inc(s.t1_mm, 1)

            def attn_values(i):
                b, j = i // TPB, i % TPB
                pe.wait_ge(s.aT1_ready, i + 1)
                if i == 0:
                    pe.wait_ge(s.o_added, B)
                if j == 0 and b >= 2:
                    pe.wait_ge(s.x3_ready, b - 1)
                for g in range(4):
                    last = mm(quarters(4 + b % 2)[:, j, :], aT1[:, i % 2, g, :], V1[:, b, g, :],
                              start=(g == 0), stop=(g == 3))
                last.then_inc(s.av_mm, 1)

            def logits1(b):
                pe.wait_ge(s.xT_ready[3], b + 1)
                for j in range(TPB):
                    last = mm(quarters(6 if b == B - 1 else 7)[:, j, :], cut(xT[:, 1, :], j), R1w[:, :])
                last.then_inc(s.lg1_mm, 1)

            def turn_gates(b, n):
                for j in range(TPB):
                    last = nc.tensor.transpose(quarters(n)[0:2 * E1, j, :],
                                               gate1[:, TPB * b + j, :, :].rearrange("p u e -> p (u e)").bitcast(F32), ident)
                last.then_inc(s.gT1_mm, 1)

            def scores(i):
                b = i // TPB
                pe.wait_ge(s.qT_ready, b + 1)
                if i in (2, 3):
                    pe.wait_ge(s.act_ready, B * R0)
                elif i >= 4:
                    pe.wait_ge(s.s1_shifted, i - 1)
                mm(score_bank(i)[:, :], qT[:, b % (B - 1), (i % TPB) * P:(i % TPB + 1) * P],
                   Kblk[:, b, :, :].rearrange("p h k -> p (h k)"), stop=False)
                pe.wait_ge(s.mask_ready, b + 1)
                mm(score_bank(i)[:, :], onesb[:, :], maskrow[:, b, :, :].rearrange("p h k -> p (h k)"), start=False)\
                    .then_inc(s.s1_mm, 1)

            for c in range(B - 1):
                experts0(c)
            pe.wait_ge(s.kblk_ready, B)
            experts0(B - 1, last_chunk=True)
            pe.wait_ge(s.v1_ready, B)
            pe.wait_ge(s.r1_ready, 1)
            for i in range(NT + 4):
                if 2 <= i < NT:
                    scores(i)
                if 3 <= i < NT + 3:
                    attn_transposes(i - 3)
                if i >= 4:
                    attn_values(i - 4)
                if i == T3:
                    transposes(2, B - 1, 6)
                if i == QUERY:
                    queries(B - 1)
                for b in looped(i, T4):
                    pe.wait_ge(s.xT_ready[2], B)
                    transposes(3, b, 6)
                for b in looped(i, LG4):
                    pe.wait_ge(s.qT_ready, B)
                    logits1(b)

            pe.wait_ge(s.gul_ready, 8)
            pe.wait_ge(s.w2l_ready, 5)

            def second(r, c):
                m = P if r < R1 else I1
                pe.wait_ge(s.hmh_ready, c * N1 + (r + 1))
                mm(bank[4][:, :], w2h[0:m, r, :], hmh_slot(r)[0:m], start=(r == 0), stop=False)
                mm(bank[4][:, :], w2l[0:m, r, :], hmh_slot(r)[0:m], start=False, stop=False)
                pe.wait_ge(s.hml_ready, c * N1 + (r + 1))
                mm(bank[4][:, :], w2h[0:m, r, :], hml_slot(r)[0:m], start=False, stop=(r == R1)).then_inc(s.hm_used1, 1)

            def turn_out(c):
                pe.wait_ge(s.outT_ready, c)
                for j in range(TPB):
                    last = nc.tensor.transpose(quarters(6)[:, j, :], cut(outT, j), ident)
                last.then_inc(s.out_mm, 1)

            def experts1(c, first=False):
                base = c * N1
                pe.wait_ge(s.xTl_ready[3], c + 1)
                for r in range(N1):
                    m = P if r < R1 else I1
                    rows = slice(r * P, r * P + m)
                    if r == R1 and not first:
                        pe.wait_ge(s.o_added1, c)
                    elif r >= 2 or not first:
                        pe.wait_ge(s.prod_ready1, c * R1 + (r - 1))
                    for bk, w in ((gate_bank(r, first), 0), (up_bank(r, first), 1)):
                        last = split_mm(bank[bk][0:m, :], gu1h[:, w, rows], gu1l[:, w, rows], chunk(xTh, c), chunk(xTl, c))
                    last.then_inc(s.h_ready1, 1)
                    if r >= LAG1:
                        if r == LAG1 and not first:
                            pe.wait_ge(s.outT_ready, c)
                        second(r - LAG1, c)
                    elif not first:
                        second(N1 + r - LAG1, c - 1)
                    if r < R1:
                        if r == 0:
                            if first:
                                pe.wait_ge(s.gate1_ready, 1)
                                turn_gates(0, 7)
                                pe.wait_ge(s.x3_ready, B)
                            pe.wait_ge(s.gT1_ready, c + 1)
                        if first and r > ON_POOL:
                            pe.wait_ge(s.gx_ready, r - ON_POOL)
                        elif r >= 1:
                            pe.wait_ge(s.hm_ready1, base + r)
                        elif not first:
                            pe.wait_ge(s.hm_ready1, base - 1)
                        mm(bank[5][:, :], sel1[:, r, :], chunk(gT, c)).then_inc(s.e_ready1, 1)
                    if r == OUT_BLOCK and not first:
                        turn_out(c)
                    if first and r in LATE_T4:
                        transposes(3, LATE_T4[r], 6)
                    if first and r in LATE_LG4:
                        if r == min(LATE_LG4):
                            pe.wait_ge(s.gT1_ready, 1)
                        logits1(LATE_LG4[r])
                    if first and r == R1:
                        pe.wait_ge(s.gate1_ready, 2)
                        pe.wait_ge(s.sg_ready, B)
                        for b in REST:
                            if b == B - 1:
                                pe.wait_ge(s.gT1_ready, B - 2)
                            turn_gates(b, 6 + (b + 1) % 2)

            experts1(0, first=True)
            pe.wait_ge(s.hm_ready1, N1)
            with pe.Fori(1, B) as c:
                experts1(c)
            for r in range(N1 - LAG1, N1):
                second(r, B - 1)
            turn_out(B)


def kernel(x, ctx_1024, mask_BxS2_bf0, L0_xattn_Wq, L0_xattn_bq, L0_xattn_Wk, L0_xattn_bk, L0_xattn_Wv, L0_xattn_bv,
           L0_xattn_Wo, L0_xattn_bo, L0_ffn_w_red, L0_ffn_wg, L0_ffn_W1, L0_ffn_b1, L0_ffn_W2, L0_ffn_b2,
           L1_xattn_Wq, L1_xattn_bq, L1_xattn_Wk, L1_xattn_bk, L1_xattn_Wv, L1_xattn_bv, L1_xattn_Wo, L1_xattn_bo,
           L1_ffn_gate_w, L1_ffn_gate_bias, L1_ffn_w1, L1_ffn_w2, L1_ffn_w3, L1_ffn_ws1, L1_ffn_ws2, L1_ffn_ws3):
    import numpy as np
    import concourse.bacc as bacc
    from concourse.bass_utils import run_bass_kernel_spmd

    def up(*parts):
        return np.stack([np.asarray(q) for q in parts], axis=1)

    def rows(v, n=P):
        return np.broadcast_to(np.asarray(v).reshape(1, -1), (n, np.asarray(v).size))

    def pack(widths, parts):
        return np.concatenate([np.asarray(parts[n]).reshape(P, w) for n, w in widths.items()], axis=1)

    parts = {
        "ctxT": np.asarray(ctx_1024).reshape(B * KV, C).T,
        "attn0_w": up(np.asarray(L0_xattn_Wk).T, L0_xattn_Wq, np.asarray(L0_xattn_Wv).T, np.asarray(L0_xattn_Wo).T),
        "attn1_w": up(L1_xattn_Wk, L1_xattn_Wq, L1_xattn_Wv, L1_xattn_Wo),
        "cols": up(L0_xattn_bk, L0_xattn_bq, L0_xattn_bv, L1_xattn_bk, L1_xattn_bq, L1_xattn_bv),
        "b1col": np.asarray(L0_ffn_b1).reshape(R0, P).T,
        "bo0": rows(L0_xattn_bo),
        "bo1": rows(L1_xattn_bo),
        "gate1T": np.asarray(L1_ffn_gate_w).T,
        "gbias": rows(L1_ffn_gate_bias),
        "ident": np.eye(P, dtype=np.float32),
        "blk": np.repeat(np.eye(H1, dtype=np.float32), D1, axis=0),
        "below": rows(np.tril(np.ones((NG, NG), np.float32), -1)),
        "order8": rows(np.arange(E0, 0, -1, dtype=np.float32)),
    }
    wg16 = np.zeros((G0, G0), np.float32)
    wg16[:E0] = np.asarray(L0_ffn_wg)
    arrays = {
        "x": np.asarray(x),
        "pack_a": pack(PACK_A, parts),
        "pack_b": pack(PACK_B, parts),
        "rows16": np.concatenate([np.asarray(L0_ffn_w_red).T, wg16, np.tile(np.asarray(L0_ffn_b2), (2, 1))], axis=1),
        "mask": np.asarray(mask_BxS2_bf0).reshape(1, B * KV),
        "sel0": np.broadcast_to(np.tile(np.eye(E0, dtype=np.float32), (2, 1))[:, :, None], (2 * E0, E0, P)),
        "sel1": np.tile(np.repeat(np.eye(E1, dtype=np.float32), I1, axis=1), (2, 1)).reshape(2 * E1, R1, P),
        "w1": np.asarray(L0_ffn_W1).transpose(1, 0, 2).reshape(C, R0 * P),
        "w2_0": np.asarray(L0_ffn_W2).reshape(R0, P, C).transpose(1, 0, 2),
        "gu1": up(*(np.concatenate([np.asarray(w).reshape(E1 * I1, C), np.asarray(sw)]).T
                    for w, sw in ((L1_ffn_w1, L1_ffn_ws1), (L1_ffn_w3, L1_ffn_ws3)))),
        "w2_1": np.asarray(L1_ffn_w2).transpose(0, 2, 1).reshape(R1, P, C).transpose(1, 0, 2),
        "ws2": np.asarray(L1_ffn_ws2).T,
    }
    arrays = {f"in_{k}": np.ascontiguousarray(v) for k, v in arrays.items()}
    nc = bacc.Bacc("TRN2", target_bir_lowering=False, num_devices=1)
    aps = {k[3:]: nc.dram_tensor(k, v.shape, mybir.dt.from_np(v.dtype), kind="ExternalInput").ap()
           for k, v in arrays.items()}
    out = nc.dram_tensor("out_x", (B, CH, C), F32, kind="ExternalOutput").ap()
    xattn_moe_kernel(nc, aps, out)
    r = run_bass_kernel_spmd(nc, [arrays], core_ids=[0])
    return r.results[0]["out_x"]
```
